# Optimizing a Trainium2 kernel written in Bass

```python
import numpy as np
import jax
import jax.numpy as jnp

def _softmax(x, axis=-1):
    return jax.nn.softmax(x, axis=axis)

def _gelu(x):
    return jax.nn.gelu(x, approximate=True)

def _silu(x):
    return jax.nn.silu(x)

def _sigmoid(x):
    return jax.nn.sigmoid(x)

def _layernorm(x, axis=-1, eps=1e-05):
    m = jnp.mean(x, axis=axis, keepdims=True)
    v = jnp.var(x, axis=axis, keepdims=True)
    return (x - m) / jnp.sqrt(v + eps)

def _scatter_add(tgt, idx, src, axis=0):
    return tgt.at[idx].add(src)

def _segment_sum(src, seg, n):
    return jax.ops.segment_sum(src, seg, n)
kernel_name = 'mk_decoder_postln_d1_seqx_r8_ac1edb'

def setup_inputs(seed: int=0):
    np.random.seed(seed)
    _w = jnp.asarray

    def _rec_inputs():
        import jax
        import jax.numpy as jnp
        _rk = jax.random.key(seed)
        x = 7.22e-05 + 1 * jax.random.normal(jax.random.fold_in(_rk, 1), (32, 128, 128), jnp.float32)
        _lenS = 128 - jax.random.randint(jax.random.fold_in(_rk, 7), (32,), 0, max(1, 128 // 4) + 1, jnp.int32)
        _lenS2 = 128 - jax.random.randint(jax.random.fold_in(_rk, 8), (32,), 0, max(1, 128 // 4) + 1, jnp.int32)
        _ctx_1024P = jax.random.normal(jax.random.fold_in(_rk, 11), (32, 16, 128), jnp.float32)
        _ctx_1024c = jax.random.dirichlet(jax.random.fold_in(_rk, 511), 0.3 * jnp.ones((16,), jnp.float32), (32, 128))
        _ctx_1024t = jnp.einsum('bsk,bkd->bsd', _ctx_1024c, _ctx_1024P)
        _ctx_1024t = _ctx_1024t * jax.lax.rsqrt(jnp.mean(jnp.square(_ctx_1024t)) + 1e-12) * 0.953939
        ctx_1024 = 4.13588e-05 + 0.999923 * (_ctx_1024t + 0.3 * jax.random.normal(jax.random.fold_in(_rk, 611), (32, 128, 128), jnp.float32))
        return (x, ctx_1024)
    x, ctx_1024 = _rec_inputs()

    def _L0_attn_setup():
        import jax, jax.numpy as jnp
        import numpy as np
        H, DK, DV, L = (16, 64, 64, 64)
        B, S, D = (4, 1024, 128)
        key = jax.random.key(seed)
        k = jax.random.split(key, 6)
        w = 0.02
        return {'x': jax.random.normal(k[0], (B, S, D), jnp.float32), 'Wq': jax.random.normal(k[1], (D, H * DK), jnp.float32) * w, 'Wk': jax.random.normal(k[2], (D, H * DK), jnp.float32) * w, 'Wv': jax.random.normal(k[3], (D, H * DV), jnp.float32) * w, 'Wo': jax.random.normal(k[4], (H * DV, D), jnp.float32) * w, 'betas': jax.random.normal(k[5], (1, H, 1, DV), jnp.float32)}
    _L0_attn_all = _L0_attn_setup()
    _L0_attn_in = {k: v for k, v in _L0_attn_all.items() if k in ('Wq', 'Wk', 'Wv', 'Wo', 'betas')}
    del _L0_attn_all

    def _L0_xattn_setup():
        import jax, jax.numpy as jnp
        import numpy as np
        EMBED_DIM = 128
        HEAD_DIM = 128
        GAMMA = 0.96875
        THETA = 10000.0
        SCALE_BASE = 512.0

        def _dup_interleave(x):
            return jnp.repeat(x, 2, axis=-1)

        def _rotate_half(x):
            x_even = x[..., ::2]
            x_odd = x[..., 1::2]
            return jnp.stack((-x_odd, x_even), axis=-1).reshape(x.shape)

        def _xpos(x, offset=0, inverse_scale=False):
            l = x.shape[-2]
            half = HEAD_DIM // 2
            scale_vec = (jnp.arange(0, HEAD_DIM, 2, dtype=jnp.float32) + 0.4 * HEAD_DIM) / (1.4 * HEAD_DIM)
            pos = jnp.arange(offset, offset + l, dtype=jnp.float32)
            scale = scale_vec[None, :] ** (pos / SCALE_BASE)[:, None]
            freqs = 1.0 / THETA ** (jnp.arange(half, dtype=jnp.float32) / half)
            sin_in = pos[:, None] * freqs[None, :]
            sin, cos = (jnp.sin(sin_in), jnp.cos(sin_in))
            if inverse_scale:
                scale = 1.0 / scale
            return x * _dup_interleave(cos * scale) + _rotate_half(x) * _dup_interleave(sin * scale)

        def _decay_mask(l, gamma):
            idx = jnp.arange(l, dtype=jnp.float32)
            diff = idx[:, None] - idx[None, :]
            return jnp.where(diff >= 0, gamma ** diff, 0.0)
        key = jax.random.key(seed)
        k1, k2, k3, k4, k5, k6 = jax.random.split(key, 6)
        B, L = (4, 256)
        s = 1.0 / np.sqrt(EMBED_DIM)
        return {'q': jax.random.normal(k1, (B, L, EMBED_DIM), dtype=jnp.float32), 'k': jax.random.normal(k2, (B, L, EMBED_DIM), dtype=jnp.float32), 'v': jax.random.normal(k3, (B, L, EMBED_DIM), dtype=jnp.float32), 'Wq': jax.random.normal(k4, (EMBED_DIM, HEAD_DIM), dtype=jnp.float32) * s, 'Wk': jax.random.normal(k5, (EMBED_DIM, HEAD_DIM), dtype=jnp.float32) * s, 'Wv': jax.random.normal(k6, (EMBED_DIM, HEAD_DIM), dtype=jnp.float32) * s}
    _L0_xattn_all = _L0_xattn_setup()
    _L0_xattn_in = {k: v for k, v in _L0_xattn_all.items() if k in ('Wq', 'Wk', 'Wv')}
    del _L0_xattn_all

    def _L0_ffn_setup():
        import jax, jax.numpy as jnp
        import numpy as np
        D_MODEL = 128
        D_HIDDEN = 512
        NUM_EXPERTS = 8
        B, T = (2, 256)
        key = jax.random.key(seed)
        ks = jax.random.split(key, 8)
        s = 0.02
        x = jax.random.normal(ks[0], (B, T, D_MODEL), dtype=jnp.float32)
        Wg = jax.random.normal(ks[1], (D_MODEL, NUM_EXPERTS), dtype=jnp.float32) * s
        bg = jnp.zeros((NUM_EXPERTS,), dtype=jnp.float32)
        W1 = jax.random.normal(ks[2], (NUM_EXPERTS, D_MODEL, D_HIDDEN), dtype=jnp.float32) * s
        b1 = jnp.zeros((NUM_EXPERTS, D_HIDDEN), dtype=jnp.float32)
        W2 = jax.random.normal(ks[3], (NUM_EXPERTS, D_HIDDEN, D_MODEL), dtype=jnp.float32) * s
        b2 = jnp.zeros((NUM_EXPERTS, D_MODEL), dtype=jnp.float32)
        return {'x': x, 'Wg': Wg, 'bg': bg, 'W1': W1, 'b1': b1, 'W2': W2, 'b2': b2}
    _L0_ffn_all = _L0_ffn_setup()
    _L0_ffn_in = {k: v for k, v in _L0_ffn_all.items() if k in ('Wg', 'bg', 'W1', 'b1', 'W2', 'b2')}
    del _L0_ffn_all
    return {'x': x, 'ctx_1024': ctx_1024, 'L0_attn_Wq': _L0_attn_in['Wq'], 'L0_attn_Wk': _L0_attn_in['Wk'], 'L0_attn_Wv': _L0_attn_in['Wv'], 'L0_attn_Wo': _L0_attn_in['Wo'], 'L0_attn_betas': _L0_attn_in['betas'], 'L0_xattn_Wq': _L0_xattn_in['Wq'], 'L0_xattn_Wk': _L0_xattn_in['Wk'], 'L0_xattn_Wv': _L0_xattn_in['Wv'], 'L0_ffn_Wg': _L0_ffn_in['Wg'], 'L0_ffn_bg': _L0_ffn_in['bg'], 'L0_ffn_W1': _L0_ffn_in['W1'], 'L0_ffn_b1': _L0_ffn_in['b1'], 'L0_ffn_W2': _L0_ffn_in['W2'], 'L0_ffn_b2': _L0_ffn_in['b2']}

def reference(x, ctx_1024, L0_attn_Wq, L0_attn_Wk, L0_attn_Wv, L0_attn_Wo, L0_attn_betas, L0_xattn_Wq, L0_xattn_Wk, L0_xattn_Wv, L0_ffn_Wg, L0_ffn_bg, L0_ffn_W1, L0_ffn_b1, L0_ffn_W2, L0_ffn_b2):
    import jax
    import jax.numpy as jnp

    def _L0_attn_ref(x, Wq, Wk, Wv, Wo, betas):
        import jax, jax.numpy as jnp
        import numpy as np
        H, DK, DV, L = (16, 64, 64, 64)
        B, S, D = (4, 1024, 128)
        Bx, Sx, Dx = x.shape
        n_seg = Sx // L
        xs = x.reshape(Bx, n_seg, L, Dx)

        def proj(W, dh):
            p = jnp.einsum('bnld,df->bnlf', xs, W)
            return p.reshape(Bx, n_seg, H, L, dh).transpose(1, 0, 2, 3, 4)
        q = proj(Wq, DK)
        k = proj(Wk, DK)
        v = proj(Wv, DV)
        gate = jax.nn.sigmoid(betas)
        scale = 1.0 / jnp.sqrt(jnp.float32(DK))

        def step(carry, qkv):
            mem, zc = carry
            qs, ks, vs = qkv
            sq = jax.nn.elu(qs) + 1.0
            mem = mem + jnp.einsum('bhsk,bhsv->bhkv', sq, vs)
            zc = zc + (jax.nn.elu(ks) + 1.0).sum(axis=-2, keepdims=True)
            scores = jnp.einsum('bhsk,bhtk->bhst', qs, ks) * scale
            att_dot = jnp.einsum('bhst,bhtv->bhsv', jax.nn.softmax(scores, axis=-1), vs)
            num = jnp.einsum('bhsk,bhkv->bhsv', sq, mem)
            den = sq.sum(axis=-1, keepdims=True) * zc
            att = gate * (num / den) + (1.0 - gate) * att_dot
            out_seg = att.reshape(Bx, L, H * DV) @ Wo
            return ((mem, zc), out_seg)
        mem0 = jnp.zeros((Bx, H, DK, DV), x.dtype)
        zc0 = jnp.zeros((Bx, H, 1, DK), x.dtype)
        _, outs = jax.lax.scan(step, (mem0, zc0), (q, k, v))
        return outs.transpose(1, 0, 2, 3).reshape(Bx, Sx, Dx)

    def _L0_xattn_ref(q, k, v, Wq, Wk, Wv):
        import jax, jax.numpy as jnp
        import numpy as np
        EMBED_DIM = 128
        HEAD_DIM = 128
        GAMMA = 0.96875
        THETA = 10000.0
        SCALE_BASE = 512.0

        def _dup_interleave(x):
            return jnp.repeat(x, 2, axis=-1)

        def _rotate_half(x):
            x_even = x[..., ::2]
            x_odd = x[..., 1::2]
            return jnp.stack((-x_odd, x_even), axis=-1).reshape(x.shape)

        def _xpos(x, offset=0, inverse_scale=False):
            l = x.shape[-2]
            half = HEAD_DIM // 2
            scale_vec = (jnp.arange(0, HEAD_DIM, 2, dtype=jnp.float32) + 0.4 * HEAD_DIM) / (1.4 * HEAD_DIM)
            pos = jnp.arange(offset, offset + l, dtype=jnp.float32)
            scale = scale_vec[None, :] ** (pos / SCALE_BASE)[:, None]
            freqs = 1.0 / THETA ** (jnp.arange(half, dtype=jnp.float32) / half)
            sin_in = pos[:, None] * freqs[None, :]
            sin, cos = (jnp.sin(sin_in), jnp.cos(sin_in))
            if inverse_scale:
                scale = 1.0 / scale
            return x * _dup_interleave(cos * scale) + _rotate_half(x) * _dup_interleave(sin * scale)

        def _decay_mask(l, gamma):
            idx = jnp.arange(l, dtype=jnp.float32)
            diff = idx[:, None] - idx[None, :]
            return jnp.where(diff >= 0, gamma ** diff, 0.0)
        qh = _xpos(q @ Wq, offset=0, inverse_scale=False)
        kh = _xpos(k @ Wk, offset=0, inverse_scale=True)
        vh = v @ Wv
        L = qh.shape[-2]
        mask = _decay_mask(L, GAMMA)
        scores = jnp.einsum('bld,bmd->blm', qh, kh) * mask[None, :, :]
        return scores @ vh

    def _L0_ffn_ref(x, Wg, bg, W1, b1, W2, b2):
        import jax, jax.numpy as jnp
        import numpy as np
        D_MODEL = 128
        D_HIDDEN = 512
        NUM_EXPERTS = 8
        B, T = (2, 256)
        gate_logits = jnp.einsum('btd,de->bte', x, Wg) + bg
        gate_scores = jax.nn.softmax(gate_logits, axis=-1)
        top1_idx = jnp.argmax(gate_scores, axis=-1)
        top1_mask = jax.nn.one_hot(top1_idx, NUM_EXPERTS, dtype=x.dtype)
        top1_weight = jnp.sum(gate_scores * top1_mask, axis=-1, keepdims=True)
        h = jax.nn.silu(jnp.einsum('btd,edh->bteh', x, W1) + b1)
        o = jnp.einsum('bteh,ehd->bted', h, W2) + b2
        y = jnp.sum(o * top1_mask[..., None], axis=2) * top1_weight
        return y
    x = _layernorm(x + _L0_attn_ref(x, L0_attn_Wq, L0_attn_Wk, L0_attn_Wv, L0_attn_Wo, L0_attn_betas), axis=-1)
    x = _layernorm(x + _L0_xattn_ref(x, ctx_1024, ctx_1024, L0_xattn_Wq, L0_xattn_Wk, L0_xattn_Wv), axis=-1)
    x = _layernorm(x + _L0_ffn_ref(x, L0_ffn_Wg, L0_ffn_bg, L0_ffn_W1, L0_ffn_b1, L0_ffn_W2, L0_ffn_b2), axis=-1)
    return x

_drawn_inputs = setup_inputs


def setup_inputs(seed=0):
    import zlib

    import numpy as np

    out = dict(_drawn_inputs(seed))
    spreads = {'L0_ffn_bg': (0.0, 0.665), 'L0_ffn_b1': (0.0, 0.8), 'L0_ffn_b2': (0.0, 0.458)}
    factors = {'L0_attn_Wq': 8.0,
     'L0_attn_Wk': 8.0,
     'L0_attn_Wv': 2.817,
     'L0_attn_Wo': 2.798,
     'L0_attn_betas': 8.0,
     'L0_ffn_Wg': 3.047,
     'L0_ffn_W1': 6.127,
     'L0_ffn_W2': 5.623}
    for name, (base, spread) in spreads.items():
        noise = np.random.default_rng([zlib.crc32(name.encode()), seed]).standard_normal(out[name].shape)
        drawn = base * np.exp(spread * noise) if base else spread * noise
        out[name] = jnp.asarray(drawn.astype(out[name].dtype))
    for name, factor in factors.items():
        out[name] = (out[name] * factor).astype(out[name].dtype)
    return out
```

```python
from contextlib import ExitStack

import numpy as np
import concourse.bass as bass
from concourse import mybir

F32 = mybir.dt.float32
U32 = mybir.dt.uint32
ALU = mybir.AluOpType
ACT = mybir.ActivationFunctionType
X = mybir.AxisListType.X

P = 128
B = 32
D = 128
H = 16
SEG = 2
L = 64
DK = 64
C = 16
J = L // H
HF = C * DK
BANK = 512
EPS = 1e-5
SM_SCALE = 1.0 / np.sqrt(DK)
E = 8
HID = 512
FT = HID // P
G = 4
NG = B // G


def shape_constants():
    ident = np.eye(P, dtype=np.float32)
    tok = np.arange(P)
    head, seg = (tok % L) // J, tok // L
    same = head[:, None] == head[None, :]
    both = same.astype(np.float32)
    first = (same & (seg[:, None] == 0)).astype(np.float32)
    half = D // 2
    scale_vec = (np.arange(0, D, 2, dtype=np.float32) + np.float32(0.4 * D)) / np.float32(1.4 * D)
    pos = np.arange(P, dtype=np.float32)
    scale = scale_vec[None, :] ** (pos / np.float32(512.0))[:, None]
    freqs = np.float32(1.0) / np.float32(10000.0) ** (np.arange(half, dtype=np.float32) / np.float32(half))
    ang = pos[:, None] * freqs[None, :]
    sin, cos = np.sin(ang), np.cos(ang)
    tabs = []
    for s in (scale, np.float32(1.0) / scale):
        for t in (cos, sin):
            tabs.append(np.repeat(t * s, 2, axis=-1).T)
    diff = pos[None, :] - pos[:, None]
    decay = np.where(diff >= 0, np.float32(0.96875) ** np.maximum(diff, 0), 0.0)
    iota = np.tile(np.arange(E, dtype=np.float32), (P, 1))
    eye_sel = np.zeros((P, E * P), np.float32)
    for e in range(E):
        eye_sel[e, e * P:(e + 1) * P] = 1.0
    cols = [ident, both, first] + tabs + [decay, iota, eye_sel]
    return np.ascontiguousarray(np.concatenate(cols, axis=1).astype(np.float32))


CONST_AT = {}
_at = 0
for _n, _w in (("ident", P), ("both", P), ("first", P), ("qcos", P), ("qsin", P), ("kcos", P), ("ksin", P),
               ("decay", P), ("iota", E), ("eye_sel", E * P)):
    CONST_AT[_n] = (_at, _at + _w)
    _at += _w
NCONST = _at


def run_steps(eng, step, n):
    step(0, 0, True, False)
    step(0, 1, True, True)
    with eng.Fori(1, n // 2) as i:
        step(i, 0, True, True)
        step(i, 1, True, True)
    step(n // 2, 0, False, True)


def is_step(t, *values):
    return isinstance(t, int) and t in values


def norm_act(act, n, ready, sq_ready):
    act.wait_ge(ready, 3)
    act.activation(n["dev"][:, :], n["var"][:, :], ACT.Sqrt).then_inc(sq_ready, 1)


def norm_dve(dve, stats, n, ready, sq_ready):
    mean, var, rstd, tmp = (n[k][:, :] for k in ("mean", "var", "rstd", "tmp"))

    def col(c):
        return stats[:, :, c:c + 1].rearrange("p b o -> p (b o)")

    dve.tensor_tensor(mean, col(1), col(4), ALU.add)
    dve.tensor_tensor(tmp, col(1), col(4), ALU.subtract)
    dve.tensor_tensor(var, col(2), col(5), ALU.add).then_inc(ready, 1)
    dve.wait_ge(ready, 1)
    dve.tensor_scalar(mean, mean, 0.5, None, ALU.mult)
    dve.tensor_scalar(var, var, 1.0 / D, EPS, ALU.mult, ALU.add)
    dve.scalar_tensor_tensor(rstd, tmp, 0.25, tmp, ALU.mult, ALU.mult).then_inc(ready, 1)
    dve.wait_ge(ready, 2)
    dve.tensor_tensor(var, var, rstd, ALU.add).then_inc(ready, 1)
    dve.wait_ge(sq_ready, 1)
    dve.reciprocal(rstd, n["dev"][:, :]).then_inc(ready, 1)
    dve.wait_ge(ready, 4)
    dve.tensor_tensor(tmp, rstd, rstd, ALU.mult).then_inc(ready, 1)
    dve.wait_ge(ready, 5)
    dve.tensor_tensor(tmp, tmp, var, ALU.mult).then_inc(ready, 1)
    dve.wait_ge(ready, 6)
    dve.tensor_scalar(tmp, tmp, -0.5, 1.5, ALU.mult, ALU.add).then_inc(ready, 1)
    dve.wait_ge(ready, 7)
    dve.tensor_tensor(rstd, rstd, tmp, ALU.mult).then_inc(ready, 1)
    dve.wait_ge(ready, 8)


def attention_phase(nc, consts, const, r_all, stats, x, Wq, Wk, Wv, Wo, betas, scratch_qv, scratch_v):
    with ExitStack() as ctx:
        def sb(name, shape):
            return ctx.enter_context(nc.sbuf_tensor(name, shape, F32))

        def sem(name):
            return ctx.enter_context(nc.semaphore(name))

        def cst(name):
            return const[:, CONST_AT[name][0]:CONST_AT[name][1]]

        w_k, w_q, w_v = sb("w_k", [P, HF]), sb("w_q", [P, HF]), sb("w_v", [P, HF])
        w_o = sb("w_o", [DK, C, D])
        xT = sb("xT", [P, B + 1, P])
        x_cur = [sb(f"x_cur{i}", [P, P]) for i in range(2)]
        gate = sb("gate", [P, DK])
        ungate = sb("ungate", [P, DK])
        qk_tok = sb("qk_tok", [P, C, 2 * DK])
        e_qk = sb("e_qk", [P, C, 2 * DK])
        v_tok = sb("v_tok", [P, C, DK])
        qv_out = sb("qv_out", [P, C, 3 * DK])
        v_un = sb("v_un", [P, C, DK])
        k_sum = sb("k_sum", [P, DK])
        z = sb("z", [P, 2, DK])
        zg = sb("zg", [P, 2, DK])
        qT = sb("qT", [DK, P, C])
        kT = sb("kT", [DK, P, C])
        s_max = sb("s_max", [P, H])
        s_exp = sb("s_exp", [P, H, L])
        row_sum = sb("row_sum", [P, H])
        row_rec = sb("row_rec", [P, H])
        sq_sum = sb("sq_sum", [P, H])
        sq_rec = sb("sq_rec", [P, H])
        ps = sb("ps", [P, H, 2 * DK])
        psT = sb("psT", [P, H, P])
        pos_qv = [sb(f"pos_qv{i}", [P, H, 3 * DK]) for i in range(2)]
        lhs = [sb(f"lhs{i}", [P, SEG, H, DK]) for i in range(2)]
        attT = sb("attT", [DK, C, P])
        banks = [ctx.enter_context(nc.psum_tensor(f"bank{i}", [P, BANK], F32)) for i in range(8)]
        proj_bank, turn_bank, score_bank, mix_bank = banks[0:2], banks[2:4], banks[4:6], banks[6:8]

        loaded = sem("loaded")
        beta_loaded = sem("beta_loaded")
        xt_ready, xt_evac = sem("xt_ready"), sem("xt_evac")
        tanh_ready, gate_ready = sem("tanh_ready"), sem("gate_ready")
        x_pad, x_staged = sem("x_pad"), sem("x_staged")
        k_proj, q_proj, v_proj = sem("k_proj"), sem("q_proj"), sem("v_proj")
        k_evac, q_evac, v_evac = sem("k_evac"), sem("q_evac"), sem("v_evac")
        exp_cut, sk_ready, sq_ready, k_summed = sem("exp_cut"), sem("sk_ready"), sem("sq_ready"), sem("k_summed")
        zc_ready, z_rec, z_ready = sem("zc_ready"), sem("z_rec"), sem("z_ready")
        vboth_ready, vfirst_ready, vun_ready = sem("vboth_ready"), sem("vfirst_ready"), sem("vun_ready")
        stored_qv, stored_v = sem("stored_qv"), sem("stored_v")
        qv_loaded = [sem(f"qv_loaded{i}") for i in range(2)]
        v_loaded = [sem(f"v_loaded{i}") for i in range(2)]
        turned, qT_evac, kT_evac = sem("turned"), sem("qT_evac"), sem("kT_evac")
        scored, maxed, shifted, exped = sem("scored"), sem("maxed"), sem("shifted"), sem("exped")
        row_summed, row_inv, p_ready = sem("row_summed"), sem("row_inv"), sem("p_ready")
        sq_summed, sq_inv, sqn_ready = sem("sq_summed"), sem("sq_inv"), sem("sqn_ready")
        ps_turned, psT_evac = sem("ps_turned"), sem("psT_evac")
        mem_ready, mem_evac = sem("mem_ready"), sem("mem_evac")
        att_ready, att_evac = sem("att_ready"), sem("att_evac")
        out_ready, res_ready = sem("out_ready"), sem("res_ready")

        NLOAD = 6
        block = ctx.enter_context(nc.Block())

        @block.sync
        def _(sp):
            sp.dma_start(r_all[:, :, :], x.rearrange("b p d -> p b d")).then_inc(loaded, 16)
            sp.dma_start(const[:, :], consts).then_inc(loaded, 16)
            sp.dma_start(w_k[:, :], Wk).then_inc(loaded, 16)
            sp.dma_start(w_q[:, :], Wq).then_inc(loaded, 16)
            sp.dma_start(w_v[:, :], Wv).then_inc(loaded, 16)
            sp.dma_start(w_o[:, :, :], Wo.rearrange("(c v) m -> v c m", v=DK)).then_inc(loaded, 16)
            stored = 0

            def step(half, p, one, two):
                if not one:
                    return
                t = 2 * half + p
                sp.wait_ge(sq_ready, t + 1)
                sp.wait_ge(vboth_ready, t + 1)
                sp.wait_ge(vfirst_ready, t + 1)
                for n, w in ((0, 3 * DK), (1, 2 * DK)):
                    sp.dma_start(scratch_qv[bass.ds(t, 1), n * L:(n + 1) * L, :, 0:w].rearrange("o p c e -> (o p) c e"),
                                 qv_out[n * L:(n + 1) * L, :, 0:w]).then_inc(stored_qv, 16)
                sp.wait_ge(vun_ready, t + 1)
                sp.dma_start(scratch_v[bass.ds(t, 1)].rearrange("o p c e -> (o p) c e"), v_un[:, :, :]).then_inc(stored_v, 16)
                sp.wait_ge(stored_qv, 32 * (t + 1))
                for n, w in ((0, 3 * DK), (1, 2 * DK)):
                    src = scratch_qv[bass.ds(t, 1), n * L:(n + 1) * L, :, 0:w]
                    sp.dma_start(pos_qv[p][n * L:(n + 1) * L, :, 0:w],
                                 src.rearrange("o (h j) c e -> (o j c) h e", j=J)).then_inc(qv_loaded[p], 16)
                sp.wait_ge(stored_v, 16 * (t + 1))
                for n in range(SEG):
                    src = scratch_v[bass.ds(t, 1), n * L:(n + 1) * L]
                    sp.dma_start(lhs[p][0:L, n, :, :], src.rearrange("o (h j) c e -> (o j c) h e", j=J)).then_inc(v_loaded[p], 16)

            run_steps(sp, step, B)

        @block.gpsimd
        def _(pool):
            for n in range(SEG):
                for j in range(J):
                    a = n * L + j
                    pool.dma_start(gate[a:a + L - J + 1:J, :], betas.rearrange("o h q v -> (o h q) v")).then_inc(beta_loaded, 16)

            def stage_x(t, p):
                if not (isinstance(t, int) and t < 2):
                    pool.wait_ge(v_proj, 2 * (t - 1))
                pool.tensor_copy(x_cur[p][:, :], xT[:, bass.ds(t, 1), :].rearrange("p o c -> p (o c)")).then_inc(x_staged, 1)

            pool.memset(xT[:, B:B + 1, :], 0.0).then_inc(x_pad, 1)
            pool.wait_ge(x_pad, 1)
            pool.wait_ge(xt_evac, B // 4)
            stage_x(0, 0)

            def step(half, p, one, two):
                t = 2 * half + p
                if one:
                    stage_x(t + 1, 1 - p)
                if two:
                    q = 1 - p
                    u = t - 1
                    pool.wait_ge(sq_inv, t)
                    if not (isinstance(u, int) and u == 0):
                        pool.wait_ge(ps_turned, 4 * u)
                    pool.tensor_tensor(ps[:, :, DK:], pos_qv[q][:, :, 0:DK],
                                       sq_rec[:, :].unsqueeze(2).to_broadcast([P, H, DK]), ALU.mult).then_inc(sqn_ready, 1)
                if one:
                    pool.wait_ge(v_evac, 2 * (t + 1))
                    pool.wait_ge(gate_ready, 2)
                    if not (isinstance(t, int) and t == 0):
                        pool.wait_ge(stored_v, 16 * t)
                        pool.wait_ge(stored_qv, 32 * t)
                    pool.tensor_tensor(v_un[:, :, :], v_tok[:, :, :],
                                       ungate[:, :].unsqueeze(1).to_broadcast([P, C, DK]), ALU.mult).then_inc(vun_ready, 1)
                    pool.wait_ge(z_ready, t + 1)
                    pool.tensor_tensor(qv_out[0:L, :, 2 * DK:], v_tok[0:L, :, :],
                                       zg[0:L, 1, :].unsqueeze(1).to_broadcast([L, C, DK]), ALU.mult).then_inc(vfirst_ready, 1)
                    for hh in range(2):
                        pool.wait_ge(row_inv, 2 * t + hh + 1)
                        if hh == 0 and not (isinstance(t, int) and t == 0):
                            pool.wait_ge(ps_turned, 4 * t)
                        s = slice(8 * hh, 8 * hh + 8)
                        pool.tensor_tensor(ps[:, s, 0:DK], s_exp[:, s, :],
                                           row_rec[:, s].unsqueeze(2).to_broadcast([P, 8, L]), ALU.mult).then_inc(p_ready, 1)

            run_steps(pool, step, B)

        @block.tensor
        def _(pe):
            pe.wait_ge(loaded, 16 * NLOAD)
            for g in range(B // 4):
                for i in range(4):
                    last = pe.transpose(banks[g][:, i * P:(i + 1) * P], r_all[:, 4 * g + i, :], cst("ident"))
                last.then_inc(xt_ready, 1)

            def step(half, p, one, two):
                t = 2 * half + p
                u = t - 1
                first = isinstance(t, int) and t == 0
                second = isinstance(t, int) and t == 1
                if one:
                    xt_b = x_cur[p][:, :]
                    pe.wait_ge(x_staged, t + 1)

                    def project(w, hh, done):
                        pe.matmul(proj_bank[hh][:, :], xt_b, w[:, hh * BANK:(hh + 1) * BANK],
                                  start=True, stop=True).then_inc(done, 1)
                    if not first:
                        pe.wait_ge(z_rec, t)
                    project(w_k, 0, k_proj)
                    if not first and not second:
                        pe.wait_ge(res_ready, t - 1)
                    project(w_k, 1, k_proj)
                    for hh in range(2):
                        pe.wait_ge(k_evac, 2 * t + hh + 1)
                        project(w_q, hh, q_proj)
                if two:
                    for f in range(4):
                        if f < 2:
                            pe.wait_ge(qT_evac, 4 * u + 3 + f)
                            pe.wait_ge(kT_evac, 4 * u + 3 + f)
                        else:
                            pe.wait_ge(psT_evac, 4 * u + f - 1)
                        if f == 0:
                            pe.wait_ge(sqn_ready, t)
                        if f % 2 == 0:
                            pe.wait_ge(p_ready, 2 * u + f // 2 + 1)
                        for i in range(4):
                            last = pe.transpose(turn_bank[f % 2][:, i * P:(i + 1) * P], ps[:, 4 * f + i, :], cst("ident"))
                        last.then_inc(ps_turned, 1)
                if one:
                    for hh in range(2):
                        pe.wait_ge(q_evac, 2 * t + hh + 1)
                        project(w_v, hh, v_proj)
                    pe.wait_ge(k_summed, t + 1)
                    pe.wait_ge(v_evac, 2 * t + 1)
                    pe.matmul(proj_bank[0][:, 0:DK], cst("both"), k_sum[:, :], start=True, stop=True)
                    pe.matmul(proj_bank[0][:, DK:2 * DK], cst("first"), k_sum[:, :], start=True, stop=True).then_inc(zc_ready, 1)
                if two:
                    q = 1 - p
                    hq = half if p == 1 else half - 1
                    pe.wait_ge(qv_loaded[q], 32 * (hq + 1))
                    for f in range(4):
                        if f < 2:
                            if not second:
                                pe.wait_ge(att_evac, 4 * (u - 1) + 3 + f)
                        else:
                            pe.wait_ge(mem_evac, 4 * u + f - 1)
                        for i in range(4):
                            for n, k, vs in ((1, P, slice(DK, 2 * DK)), (0, L, slice(2 * DK, 3 * DK))):
                                h, at = 4 * f + i, n * 4 * DK + i * DK
                                last = pe.matmul(mix_bank[f % 2][DK:, at:at + DK], pos_qv[q][0:k, h, 0:DK],
                                                 pos_qv[q][0:k, h, vs], start=True, stop=True)
                        last.then_inc(mem_ready, 1)
                if one:
                    for f in range(4):
                        if f < 2:
                            if two:
                                pe.wait_ge(psT_evac, 4 * u + 3 + f)
                        else:
                            pe.wait_ge(qT_evac, 4 * t + f - 1)
                            pe.wait_ge(kT_evac, 4 * t + f - 1)
                        if f == 0:
                            pe.wait_ge(k_evac, 2 * t + 2)
                            pe.wait_ge(q_evac, 2 * t + 2)
                        for i in range(4):
                            last = pe.transpose(turn_bank[f % 2][:, i * P:(i + 1) * P], qk_tok[:, 4 * f + i, :], cst("ident"))
                        last.then_inc(turned, 1)
                if two:
                    pe.wait_ge(v_loaded[q], 32 * (hq + 1))
                    pe.wait_ge(psT_evac, 4 * u + 4)
                    pe.wait_ge(mem_evac, 4 * u + 4)
                    for f in range(4):
                        n, hh = f // 2, f % 2
                        if f >= 2:
                            pe.wait_ge(att_evac, 4 * u + f - 1)
                        for i in range(8):
                            h = 8 * hh + i
                            last = pe.matmul(mix_bank[f % 2][0:DK, i * L:(i + 1) * L], lhs[q][:, n, h, :],
                                             psT[:, h, n * L:(n + 1) * L], start=True, stop=True)
                        last.then_inc(att_ready, 1)
                if one:
                    pe.wait_ge(qT_evac, 4 * t + 4)
                    pe.wait_ge(kT_evac, 4 * t + 4)
                    for hh in range(2):
                        if not first:
                            pe.wait_ge(shifted, 2 * t - 1 + hh)
                        for i in range(8):
                            if i == 0:
                                tok = J * 8 * hh
                                pe.matmul(score_bank[hh][:, 0:L], qT[:, tok:tok + 2 * J, :], kT[:, tok:tok + J, :],
                                          start=True, stop=True)
                            for n in range(1 if i == 0 else 0, SEG):
                                tok = n * L + J * (8 * hh + i)
                                last = pe.matmul(score_bank[hh][n * L:(n + 1) * L, i * L:(i + 1) * L],
                                                 qT[:, tok:tok + J, :], kT[:, tok:tok + J, :], start=True, stop=True)
                        last.then_inc(scored, 1)
                if two:
                    pe.wait_ge(att_evac, 4 * u + 4)
                    if one:
                        pe.wait_ge(v_evac, 2 * t + 2)
                    else:
                        pe.wait_ge(res_ready, t - 1)
                    for c in range(C):
                        last = pe.matmul(proj_bank[1][:, 0:D], attT[:, c, :], w_o[:, c, :], start=(c == 0), stop=(c == C - 1))
                    last.then_inc(out_ready, 1)

            run_steps(pe, step, B)

        @block.scalar
        def _(act):
            act.wait_ge(beta_loaded, 16 * SEG * J)
            act.activation(gate[:, :], gate[:, :], ACT.Tanh, scale=0.5).then_inc(tanh_ready, 1)
            for g in range(B // 4):
                act.wait_ge(xt_ready, g + 1)
                act.activation(xT[:, 4 * g:4 * g + 4, :], banks[g][:, :].rearrange("p (b c) -> p b c", b=4), ACT.Copy).then_inc(xt_evac, 1)

            def step(half, p, one, two):
                t = 2 * half + p
                u = t - 1
                first = isinstance(t, int) and t == 0
                second = isinstance(t, int) and t == 1
                if one:
                    for slot, proj, evac in ((1, k_proj, k_evac), (0, q_proj, q_evac)):
                        s = slice(slot * DK, (slot + 1) * DK)
                        for hh in range(2):
                            act.wait_ge(proj, 2 * t + hh + 1)
                            if hh == 0 and slot == 1 and not first:
                                act.wait_ge(turned, 4 * t)
                                act.wait_ge(sq_ready, t)
                                act.wait_ge(k_summed, t)
                            c = slice(8 * hh, 8 * hh + 8)
                            bank = proj_bank[hh][:, :].rearrange("p (c k) -> p c k", c=8)
                            act.activation(e_qk[:, c, s], bank, ACT.Exp)
                            act.activation(qk_tok[:, c, s], bank, ACT.Copy).then_inc(evac, 1)
                if two:
                    for f in range(4):
                        act.wait_ge(ps_turned, 4 * u + f + 1)
                        if f == 0 and not second:
                            act.wait_ge(att_ready, 4 * u)
                        act.activation(psT[:, 4 * f:4 * f + 4, :], turn_bank[f % 2][:, :].rearrange("p (h s) -> p h s", h=4),
                                       ACT.Copy).then_inc(psT_evac, 1)
                if one:
                    for hh in range(2):
                        act.wait_ge(v_proj, 2 * t + hh + 1)
                        if hh == 0 and not first:
                            act.wait_ge(vboth_ready, t)
                            act.wait_ge(vfirst_ready, t)
                            act.wait_ge(vun_ready, t)
                        act.activation(v_tok[:, 8 * hh:8 * hh + 8, :], proj_bank[hh][:, :].rearrange("p (c k) -> p c k", c=8),
                                       ACT.Copy).then_inc(v_evac, 1)
                if two:
                    q = 1 - p
                    for f in range(4):
                        act.wait_ge(mem_ready, 4 * u + f + 1)
                        act.activation(lhs[q][DK:, :, 4 * f:4 * f + 4, :],
                                       mix_bank[f % 2][DK:, :].rearrange("p (n h k) -> p n h k", n=SEG, h=4), ACT.Copy).then_inc(mem_evac, 1)
                if one:
                    for f in range(4):
                        act.wait_ge(turned, 4 * t + f + 1)
                        if f == 0 and not first:
                            act.wait_ge(scored, 2 * t)
                        act.activation(qT[:, :, 4 * f:4 * f + 4],
                                       turn_bank[f % 2][0:DK, :].rearrange("p (c s) -> p s c", c=4), ACT.Copy).then_inc(qT_evac, 1)
                if two:
                    for f in range(4):
                        n, hh = f // 2, f % 2
                        act.wait_ge(att_ready, 4 * u + f + 1)
                        if f == 0 and not second:
                            act.wait_ge(out_ready, u)
                        at = n * L + hh * 32
                        act.activation(attT[:, :, at:at + 32],
                                       mix_bank[f % 2][0:DK, :].rearrange("p (t c) -> p c t", c=C), ACT.Copy).then_inc(att_evac, 1)
                if one:
                    for hh in range(2):
                        act.wait_ge(shifted, 2 * t + hh + 1)
                        s = slice(8 * hh, 8 * hh + 8)
                        act.activation(s_exp[:, s, :], s_exp[:, s, :], ACT.Exp, scale=float(SM_SCALE)).then_inc(exped, 1)

            run_steps(act, step, B)

        @block.vector
        def _(dve):
            dve.wait_ge(tanh_ready, 1)
            dve.tensor_scalar(ungate[:, :], gate[:, :], -0.5, 0.5, ALU.mult, ALU.add).then_inc(gate_ready, 1)
            dve.wait_ge(gate_ready, 1)
            dve.tensor_scalar(gate[:, :], gate[:, :], 0.5, 0.5, ALU.mult, ALU.add).then_inc(gate_ready, 1)

            def step(half, p, one, two):
                t = 2 * half + p
                u = t - 1
                first = isinstance(t, int) and t == 0
                if one:
                    dve.wait_ge(k_evac, 2 * t + 2)
                    dve.tensor_scalar(e_qk[:, :, DK:], e_qk[:, :, DK:], 1.0, None, ALU.min).then_inc(exp_cut, 1)
                    dve.wait_ge(exp_cut, 2 * t + 1)
                    dve.scalar_tensor_tensor(e_qk[:, :, DK:], qk_tok[:, :, DK:], 1.0, e_qk[:, :, DK:],
                                             ALU.add, ALU.max).then_inc(sk_ready, 1)
                    dve.wait_ge(sk_ready, t + 1)
                    if not first:
                        dve.wait_ge(zc_ready, t)
                    dve.tensor_reduce(k_sum[:, :], e_qk[:, :, DK:].rearrange("p c k -> p k c"), X, ALU.add).then_inc(k_summed, 1)
                    dve.wait_ge(q_evac, 2 * t + 2)
                    dve.tensor_scalar(e_qk[:, :, 0:DK], e_qk[:, :, 0:DK], 1.0, None, ALU.min).then_inc(exp_cut, 1)
                    dve.wait_ge(exp_cut, 2 * t + 2)
                    if not first:
                        dve.wait_ge(stored_qv, 32 * t)
                    dve.scalar_tensor_tensor(qv_out[:, :, 0:DK], qk_tok[:, :, 0:DK], 1.0, e_qk[:, :, 0:DK],
                                             ALU.add, ALU.max).then_inc(sq_ready, 1)
                    dve.wait_ge(zc_ready, t + 1)
                    if not first:
                        dve.wait_ge(z_ready, t)
                    dve.reciprocal(z[:, :, :], proj_bank[0][:, 0:2 * DK].rearrange("p (a k) -> p a k", a=2)).then_inc(z_rec, 1)
                    dve.wait_ge(z_rec, t + 1)
                    if not first:
                        dve.wait_ge(vfirst_ready, t)
                        dve.wait_ge(vboth_ready, t)
                    dve.tensor_tensor(zg[:, :, :], z[:, :, :], gate[:, :].unsqueeze(1).to_broadcast([P, 2, DK]),
                                      ALU.mult).then_inc(z_ready, 1)
                    dve.wait_ge(z_ready, t + 1)
                    dve.wait_ge(v_evac, 2 * t + 2)
                    dve.tensor_tensor(qv_out[:, :, DK:2 * DK], v_tok[:, :, :],
                                      zg[:, 0, :].unsqueeze(1).to_broadcast([P, C, DK]), ALU.mult).then_inc(vboth_ready, 1)
                    for f in range(4):
                        dve.wait_ge(turned, 4 * t + f + 1)
                        if f == 0 and not first:
                            dve.wait_ge(scored, 2 * t)
                        dve.tensor_copy(kT[:, :, 4 * f:4 * f + 4],
                                        turn_bank[f % 2][DK:, :].rearrange("p (c s) -> p s c", c=4)).then_inc(kT_evac, 1)
                    for hh in range(2):
                        s = slice(8 * hh, 8 * hh + 8)
                        bank = score_bank[hh][:, :].rearrange("p (h t) -> p h t", h=8)
                        dve.wait_ge(scored, 2 * t + hh + 1)
                        dve.tensor_reduce(s_max[:, s], bank, X, ALU.max).then_inc(maxed, 1)
                        dve.wait_ge(maxed, 2 * t + hh + 1)
                        if not first:
                            dve.wait_ge(p_ready, 2 * t - 1 + hh)
                        dve.tensor_tensor(s_exp[:, s, :], bank, s_max[:, s].unsqueeze(2).to_broadcast([P, 8, L]),
                                          ALU.subtract).then_inc(shifted, 1)
                    for hh in range(2):
                        s = slice(8 * hh, 8 * hh + 8)
                        dve.wait_ge(exped, 2 * t + hh + 1)
                        dve.tensor_reduce(row_sum[:, s], s_exp[:, s, :], X, ALU.add).then_inc(row_summed, 1)
                        dve.wait_ge(row_summed, 2 * t + hh + 1)
                        dve.reciprocal(row_rec[:, s], row_sum[:, s]).then_inc(row_inv, 1)
                if two:
                    dve.wait_ge(out_ready, t)
                    rb = r_all[:, bass.ds(u, 1), :].rearrange("p o d -> p (o d)")
                    dve.tensor_tensor(rb, proj_bank[1][:, 0:D], rb, ALU.add).then_inc(res_ready, 1)
                    dve.wait_ge(res_ready, t)
                    dve.wait_ge(loaded, 16 * NLOAD)
                    dve.bn_stats(stats[:, bass.ds(u, 1), :].rearrange("p o d -> p (o d)"), rb)
                if one:
                    dve.wait_ge(qv_loaded[p], 32 * (half + 1))
                    if not first:
                        dve.wait_ge(sqn_ready, t)
                    dve.tensor_reduce(sq_sum[:, :], pos_qv[p][:, :, 0:DK], X, ALU.add).then_inc(sq_summed, 1)
                    dve.wait_ge(sq_summed, t + 1)
                    dve.reciprocal(sq_rec[:, :], sq_sum[:, :]).then_inc(sq_inv, 1)

            run_steps(dve, step, B)


def retention_phase(nc, const, r_all, stats, ctx_in, Wq, Wk, Wv):
    with ExitStack() as ctx:
        def sb(name, shape):
            return ctx.enter_context(nc.sbuf_tensor(name, shape, F32))

        def sem(name):
            return ctx.enter_context(nc.semaphore(name))

        def cst(name):
            return const[:, CONST_AT[name][0]:CONST_AT[name][1]]

        def four(ap):
            return ap.unsqueeze(1).to_broadcast([P, G, P])

        wq, wk, wv = sb("r_wq", [P, D]), sb("r_wk", [P, D]), sb("r_wv", [P, D])
        wq_rot, wk_rot = sb("wq_rot", [P, D]), sb("wk_rot", [P, D])
        norm = {n: sb("r_" + n, [P, B]) for n in ("mean", "var", "dev", "rstd", "tmp")}
        x1 = [sb(f"x1_{i}", [P, G, D]) for i in range(2)]
        cx = [sb(f"cx_{i}", [P, G, D]) for i in range(2)]
        x1T, cxT = sb("x1T", [P, G, P]), sb("cxT", [P, G, P])
        q_cos, q_sin, k_cos, k_sin = (sb(n, [P, G, P]) for n in ("q_cos", "q_sin", "k_cos", "k_sin"))
        qh = [sb(f"qh{i}", [P, G, P]) for i in range(2)]
        kh = [sb(f"kh{i}", [P, G, P]) for i in range(2)]
        vh = [sb(f"vh{i}", [P, G, D]) for i in range(2)]
        sc = sb("sc", [P, G, P])
        names = ("x1t", "cxt", "q", "qr", "k", "kr", "score", "out")
        bank = {n: ctx.enter_context(nc.psum_tensor(f"r_{n}", [P, BANK], F32)) for n in names}

        w_loaded, rot_ready = sem("w_loaded"), sem("rot_ready")
        dev_in, dev_out = sem("dev_in"), sem("dev_out")
        cx_loaded = [sem(f"cx_loaded{i}") for i in range(2)]
        x1_ready, x1_turned, x1T_evac = sem("x1_ready"), sem("x1_turned"), sem("x1T_evac")
        cx_turned, cxT_evac = sem("cx_turned"), sem("cxT_evac")
        projected, scaled, qh_ready, kh_ready = sem("projected"), sem("scaled"), sem("qh_ready"), sem("kh_ready")
        v_done, v_evac = sem("v_done"), sem("rv_evac")
        scored, decayed = sem("r_scored"), sem("decayed")
        out_done, r_ready, bn_done, stats_done = sem("out_done"), sem("r_ready"), sem("bn_done"), sem("stats_done")
        block = ctx.enter_context(nc.Block())

        @block.sync
        def _(sp):
            sp.dma_start(wq[:, :], Wq).then_inc(w_loaded, 16)
            sp.dma_start(wk[:, :], Wk).then_inc(w_loaded, 16)
            sp.dma_start(wv[:, :], Wv).then_inc(w_loaded, 16)

            def step(half, p, one, two):
                t = 2 * half + p
                if one:
                    if not is_step(t, 0, 1):
                        sp.wait_ge(cx_turned, t - 1)
                    sp.dma_start(cx[p][:, :, :], ctx_in[bass.ds(G * t, G)].rearrange("b p d -> p b d")).then_inc(cx_loaded[p], 16)

            run_steps(sp, step, NG)

        @block.gpsimd
        def _(pool):
            def step(half, p, one, two):
                t = 2 * half + p
                if one:
                    pool.wait_ge(scaled, 4 * t + 2)
                    if not is_step(t, 0, 1):
                        pool.wait_ge(scored, t - 1)
                    pool.tensor_tensor(qh[p][:, :, :], q_cos[:, :, :], q_sin[:, :, :], ALU.add).then_inc(qh_ready, 1)
                    pool.wait_ge(scaled, 4 * t + 4)
                    pool.tensor_tensor(kh[p][:, :, :], k_cos[:, :, :], k_sin[:, :, :], ALU.add).then_inc(kh_ready, 1)

            run_steps(pool, step, NG)

        @block.tensor
        def _(pe):
            def step(half, p, one, two):
                t = 2 * half + p
                u = t - 1
                q = 1 - p
                hq = half if p == 1 else half - 1
                if one:
                    pe.wait_ge(cx_loaded[p], 16 * (half + 1))
                    if not is_step(t, 0):
                        pe.wait_ge(cxT_evac, t)
                    for i in range(G):
                        last = pe.transpose(bank["cxt"][:, i * P:(i + 1) * P], cx[p][:, i, :], cst("ident"))
                    last.then_inc(cx_turned, 1)
                    pe.wait_ge(x1_ready, t + 1)
                    if not is_step(t, 0):
                        pe.wait_ge(v_evac, t)
                    for i in range(G):
                        last = pe.transpose(bank["x1t"][:, i * P:(i + 1) * P], x1[p][:, i, :], cst("ident"))
                    last.then_inc(x1_turned, 1)
                if two:
                    pe.wait_ge(qh_ready, u + 1)
                    pe.wait_ge(kh_ready, u + 1)
                    if not is_step(t, 1):
                        pe.wait_ge(decayed, u)
                    for i in range(G):
                        last = pe.matmul(bank["score"][:, i * P:(i + 1) * P], kh[q][:, i, :], qh[q][:, i, :], start=True, stop=True)
                    last.then_inc(scored, 1)
                if one:
                    if is_step(t, 0):
                        pe.wait_ge(w_loaded, 48)
                        pe.wait_ge(rot_ready, 4)
                    pe.wait_ge(x1T_evac, t + 1)
                    for n, (name, w, src) in enumerate((("q", wq, x1T), ("qr", wq_rot, x1T), ("k", wk, cxT), ("kr", wk_rot, cxT))):
                        if n == 2:
                            pe.wait_ge(cxT_evac, t + 1)
                        if not is_step(t, 0):
                            pe.wait_ge(scaled, 4 * (t - 1) + n + 1)
                        pe.matmul(bank[name][:, :], w[:, :], src[:, :, :].rearrange("p g t -> p (g t)"),
                                  start=True, stop=True).then_inc(projected, 1)
                    for i in range(G):
                        last = pe.matmul(bank["x1t"][:, i * P:(i + 1) * P], cxT[:, i, :], wv[:, :], start=True, stop=True)
                    last.then_inc(v_done, 1)
                if two:
                    pe.wait_ge(decayed, u + 1)
                    pe.wait_ge(v_evac, u + 1)
                    if not is_step(t, 1):
                        pe.wait_ge(r_ready, u)
                    for i in range(G):
                        last = pe.matmul(bank["out"][:, i * P:(i + 1) * P], sc[:, i, :], vh[q][:, i, :], start=True, stop=True)
                    last.then_inc(out_done, 1)

            run_steps(pe, step, NG)

        @block.scalar
        def _(act):
            norm_act(act, norm, dev_in, dev_out)

            def step(half, p, one, two):
                t = 2 * half + p
                if one:
                    act.wait_ge(cx_turned, t + 1)
                    if not is_step(t, 0):
                        act.wait_ge(v_done, t)
                    act.activation(cxT[:, :, :], bank["cxt"][:, :].rearrange("p (g t) -> p g t", g=G), ACT.Copy).then_inc(cxT_evac, 1)
                    act.wait_ge(x1_turned, t + 1)
                    act.activation(x1T[:, :, :], bank["x1t"][:, :].rearrange("p (g t) -> p g t", g=G), ACT.Copy).then_inc(x1T_evac, 1)
                    act.wait_ge(v_done, t + 1)
                    if not is_step(t, 0, 1):
                        act.wait_ge(out_done, t - 1)
                    act.activation(vh[p][:, :, :], bank["x1t"][:, :].rearrange("p (g t) -> p g t", g=G), ACT.Copy).then_inc(v_evac, 1)

            run_steps(act, step, NG)

        @block.vector
        def _(dve):
            norm_dve(dve, stats, norm, dev_in, dev_out)
            dve.wait_ge(w_loaded, 48)
            for w, rot in ((wq, wq_rot), (wk, wk_rot)):
                pairs = w[:, :].rearrange("p (i two) -> p i two", two=2)
                turned = rot[:, :].rearrange("p (i two) -> p i two", two=2)
                dve.tensor_scalar(turned[:, :, 0:1], pairs[:, :, 1:2], -1.0, None, ALU.mult).then_inc(rot_ready, 1)
                dve.tensor_copy(turned[:, :, 1:2], pairs[:, :, 0:1]).then_inc(rot_ready, 1)

            def step(half, p, one, two):
                t = 2 * half + p
                u = t - 1
                q = 1 - p
                if one:
                    if not is_step(t, 0, 1):
                        dve.wait_ge(r_ready, t - 1)
                        dve.wait_ge(x1_turned, t - 1)
                    for i in range(G):
                        b = G * t + i
                        last = dve.tensor_scalar(x1[p][:, i, :], r_all[:, bass.ds(b, 1), :].rearrange("p o d -> p (o d)"),
                                                 norm["mean"][:, bass.ds(b, 1)], norm["rstd"][:, bass.ds(b, 1)], ALU.subtract, ALU.mult)
                    last.then_inc(x1_ready, 1)
                if two:
                    dve.wait_ge(scored, u + 1)
                    if not is_step(t, 1):
                        dve.wait_ge(out_done, u)
                    dve.tensor_tensor(sc[:, :, :], bank["score"][:, :].rearrange("p (g t) -> p g t", g=G), four(cst("decay")),
                                      ALU.mult).then_inc(decayed, 1)
                if one:
                    for n, (name, table, dst) in enumerate((("q", "qcos", q_cos), ("qr", "qsin", q_sin),
                                                            ("k", "kcos", k_cos), ("kr", "ksin", k_sin))):
                        dve.wait_ge(projected, 4 * t + n + 1)
                        if not is_step(t, 0):
                            dve.wait_ge(qh_ready if n < 2 else kh_ready, t)
                        dve.tensor_tensor(dst[:, :, :], bank[name][:, :].rearrange("p (g t) -> p g t", g=G), four(cst(table)),
                                          ALU.mult).then_inc(scaled, 1)
                if two:
                    dve.wait_ge(out_done, u + 1)
                    dve.wait_ge(x1_ready, u + 1)
                    rb = r_all[:, bass.ds(G * u, G), :]
                    dve.tensor_tensor(rb, bank["out"][:, :].rearrange("p (g t) -> p g t", g=G), x1[q][:, :, :],
                                      ALU.add).then_inc(r_ready, 1)
                    dve.wait_ge(r_ready, u + 1)
                    dve.wait_ge(w_loaded, 48)
                    for i in range(G):
                        dve.bn_stats(stats[:, bass.ds(G * u + i, 1), :].rearrange("p o d -> p (o d)"),
                                     r_all[:, bass.ds(G * u + i, 1), :].rearrange("p o d -> p (o d)"))

            run_steps(dve, step, NG)


def gate_phase(nc, const, r_all, stats, x2T, pick_w, Wg, bg):
    with ExitStack() as ctx:
        def sb(name, shape):
            return ctx.enter_context(nc.sbuf_tensor(name, shape, F32))

        def sem(name):
            return ctx.enter_context(nc.semaphore(name))

        def cst(name):
            return const[:, CONST_AT[name][0]:CONST_AT[name][1]]

        wg, bg_rep = sb("wg", [P, E]), sb("bg_rep", [P, E])
        norm = {n: sb("g_" + n, [P, B]) for n in ("mean", "var", "dev", "rstd", "tmp")}
        x2 = [sb(f"x2_{i}", [P, G, D]) for i in range(2)]
        x2T_cur = [sb(f"x2T_{i}", [P, G, P]) for i in range(2)]
        logits, ex, hot = (sb(n, [P, B, E]) for n in ("logits", "ex", "hot"))
        top, total, inv, index = (sb(n, [P, B]) for n in ("top", "total", "inv", "index"))
        turn = [ctx.enter_context(nc.psum_tensor(f"g_turn{i}", [P, BANK], F32)) for i in range(2)]
        logit_bank = [ctx.enter_context(nc.psum_tensor(f"g_logit{i}", [P, BANK], F32)) for i in range(2)]

        w_loaded, dev_in, dev_out = sem("g_w_loaded"), sem("g_dev_in"), sem("g_dev_out")
        x2_ready, x2_turned, x2T_evac, x2_kept = sem("x2_ready"), sem("x2_turned"), sem("x2T_evac"), sem("x2_kept")
        gated, logit_ready = sem("gated"), sem("logit_ready")
        done, exp_done = sem("gate_done"), sem("gate_exp")
        block = ctx.enter_context(nc.Block())

        @block.sync
        def _(sp):
            sp.dma_start(wg[:, :], Wg).then_inc(w_loaded, 16)
            sp.dma_start(bg_rep[:, :], bg.rearrange("(o e) -> o e", o=1).to_broadcast([P, E])).then_inc(w_loaded, 16)

        @block.tensor
        def _(pe):
            pe.wait_ge(w_loaded, 32)

            def step(half, p, one, two):
                t = 2 * half + p
                u = t - 1
                q = 1 - p
                if one:
                    pe.wait_ge(x2_ready, t + 1)
                    if not is_step(t, 0, 1):
                        pe.wait_ge(x2T_evac, t - 1)
                    for i in range(G):
                        last = pe.transpose(turn[p][:, i * P:(i + 1) * P], x2[p][:, i, :], cst("ident"))
                    last.then_inc(x2_turned, 1)
                if two:
                    pe.wait_ge(x2T_evac, u + 1)
                    for i in range(G):
                        last = pe.matmul(logit_bank[q][:, i * E:(i + 1) * E], x2T_cur[q][:, i, :], wg[:, :], start=True, stop=True)
                    last.then_inc(gated, 1)

            run_steps(pe, step, NG)

        @block.scalar
        def _(act):
            norm_act(act, norm, dev_in, dev_out)

            def step(half, p, one, two):
                t = 2 * half + p
                if one:
                    act.wait_ge(x2_turned, t + 1)
                    if not is_step(t, 0, 1):
                        act.wait_ge(gated, t - 1)
                        act.wait_ge(x2_kept, 2 * (t - 1))
                    act.activation(x2T_cur[p][:, :, :], turn[p][:, :].rearrange("p (g t) -> p g t", g=G), ACT.Copy).then_inc(x2T_evac, 1)

            run_steps(act, step, NG)
            act.wait_ge(done, 2)
            act.activation(ex[:, :, :], logits[:, :, :], ACT.Exp).then_inc(exp_done, 1)

        @block.gpsimd
        def _(pool):
            def step(half, p, one, two):
                t = 2 * half + p
                if one:
                    pool.wait_ge(x2_ready, t + 1)
                    pool.tensor_copy(r_all[:, bass.ds(G * t, G), :], x2[p][:, :, :]).then_inc(x2_kept, 1)
                    pool.wait_ge(x2T_evac, t + 1)
                    pool.tensor_copy(x2T[:, bass.ds(G * t, G), :], x2T_cur[p][:, :, :]).then_inc(x2_kept, 1)

            run_steps(pool, step, NG)

        @block.vector
        def _(dve):
            norm_dve(dve, stats, norm, dev_in, dev_out)
            dve.wait_ge(w_loaded, 32)

            def step(half, p, one, two):
                t = 2 * half + p
                u = t - 1
                q = 1 - p
                if one:
                    if not is_step(t, 0, 1):
                        dve.wait_ge(x2_turned, t - 1)
                        dve.wait_ge(x2_kept, 2 * (t - 1))
                    for i in range(G):
                        b = G * t + i
                        last = dve.tensor_scalar(x2[p][:, i, :], r_all[:, bass.ds(b, 1), :].rearrange("p o d -> p (o d)"),
                                                 norm["mean"][:, bass.ds(b, 1)], norm["rstd"][:, bass.ds(b, 1)], ALU.subtract, ALU.mult)
                    last.then_inc(x2_ready, 1)
                if two:
                    dve.wait_ge(gated, u + 1)
                    dve.tensor_tensor(logits[:, bass.ds(G * u, G), :], logit_bank[q][:, 0:G * E].rearrange("p (g e) -> p g e", e=E),
                                      bg_rep[:, :].unsqueeze(1).to_broadcast([P, G, E]), ALU.add).then_inc(logit_ready, 1)

            run_steps(dve, step, NG)

            def bc(t):
                return t[:, :].unsqueeze(2).to_broadcast([P, B, E])
            iota = cst("iota").unsqueeze(1).to_broadcast([P, B, E])
            dve.wait_ge(logit_ready, NG)
            dve.tensor_reduce(top[:, :], logits[:, :, :], X, ALU.max).then_inc(done, 1)
            dve.wait_ge(done, 1)
            dve.tensor_tensor(logits[:, :, :], logits[:, :, :], bc(top), ALU.subtract).then_inc(done, 1)
            dve.wait_ge(exp_done, 1)
            dve.tensor_reduce(total[:, :], ex[:, :, :], X, ALU.add).then_inc(done, 1)
            dve.wait_ge(done, 3)
            dve.reciprocal(inv[:, :], total[:, :]).then_inc(done, 1)
            dve.wait_ge(done, 4)
            dve.tensor_tensor(ex[:, :, :], ex[:, :, :], bc(inv), ALU.mult).then_inc(done, 1)
            dve.wait_ge(done, 5)
            dve.tensor_reduce(top[:, :], ex[:, :, :], X, ALU.max).then_inc(done, 1)
            dve.wait_ge(done, 6)
            dve.tensor_tensor(hot[:, :, :], ex[:, :, :], bc(top), ALU.is_equal).then_inc(done, 1)
            dve.wait_ge(done, 7)
            dve.tensor_scalar(hot[:, :, :], hot[:, :, :], -float(E), float(E), ALU.mult, ALU.add).then_inc(done, 1)
            dve.wait_ge(done, 8)
            dve.tensor_tensor(hot[:, :, :], hot[:, :, :], iota, ALU.add).then_inc(done, 1)
            dve.wait_ge(done, 9)
            dve.tensor_reduce(index[:, :], hot[:, :, :], X, ALU.min).then_inc(done, 1)
            dve.wait_ge(done, 10)
            dve.tensor_tensor(hot[:, :, :], bc(index), iota, ALU.is_equal).then_inc(done, 1)
            dve.wait_ge(done, 11)
            dve.tensor_tensor(pick_w[:, :, :], hot[:, :, :], bc(top), ALU.mult).then_inc(done, 1)


def dense_phase(nc, x2T, r_all, stats, pick_w, W1, b1, W2, b2, out):
    with ExitStack() as ctx:
        def sb(name, shape):
            return ctx.enter_context(nc.sbuf_tensor(name, shape, F32))

        def sem(name):
            return ctx.enter_context(nc.semaphore(name))

        w1, w2 = sb("w1", [P, E, HID]), sb("w2", [P, E, FT, D])
        b1c, b2r = sb("b1c", [P, E, FT]), sb("b2r", [P, E, D])
        hT = [sb(f"hT{i}", [P, FT, G * P]) for i in range(2)]
        y = sb("y", [P, G, D])
        norm = {n: sb("o_" + n, [P, B]) for n in ("mean", "var", "dev", "rstd", "tmp")}
        o = [sb(f"o_{i}", [P, G, D]) for i in range(2)]
        h_bank = [ctx.enter_context(nc.psum_tensor(f"h_bank{n}", [P, BANK], F32)) for n in range(4)]
        y_bank = [ctx.enter_context(nc.psum_tensor(f"y_bank{n}", [P, BANK], F32)) for n in range(2)]
        loaded, hid, act_done, y_ready, y_added = sem("e_loaded"), sem("hid"), sem("act_done"), sem("y_ready"), sem("y_added")
        y_kept, bn_done, stats_done = sem("y_kept"), sem("e_bn"), sem("e_stats")
        dev_in, dev_out, o_ready = sem("e_dev_in"), sem("e_dev_out"), sem("o_ready")
        stored = [sem(f"stored{i}") for i in range(2)]
        block = ctx.enter_context(nc.Block())

        @block.sync
        def _(sp):
            sp.dma_start(w1[:, :, :], W1.rearrange("e d h -> d e h")).then_inc(loaded, 16)
            sp.dma_start(w2[:, :, :, :], W2.rearrange("e (f p) d -> p e f d", p=P)).then_inc(loaded, 16)
            for e in range(E):
                sp.dma_start(b1c[:, e, :], b1[e:e + 1, :].rearrange("o (f p) -> p (o f)", p=P), allow_slow_non_contiguous=True).then_inc(loaded, 16)
            sp.dma_start(b2r[:, :, :], b2.rearrange("(o e) d -> o e d", o=1).to_broadcast([P, E, D])).then_inc(loaded, 16)
            for g in range(NG):
                sp.wait_ge(o_ready, g + 1)
                sp.dma_start(out[G * g:G * g + G].rearrange("b p d -> p b d"), o[g % 2][:, :, :]).then_inc(stored[g % 2], 16)
            for i in range(2):
                sp.wait_ge(stored[i], 16 * NG // 2)

        @block.tensor
        def _(pe):
            pe.wait_ge(loaded, 16 * (3 + E))

            def turn(g):
                def second(e):
                    pe.wait_ge(act_done, E * FT * g + FT * (e + 1))
                    if e >= 2 or not is_step(g, 0):
                        pe.wait_ge(y_added, E * g + max(e - 1, 0))
                    for i in range(G):
                        for f in range(FT):
                            last = pe.matmul(y_bank[e % 2][:, i * P:(i + 1) * P], hT[e % 2][:, f, i * P:(i + 1) * P],
                                             w2[:, e, f, :], start=(f == 0), stop=(f == FT - 1))
                    last.then_inc(y_ready, 1)
                for e in range(E):
                    for f in range(FT):
                        if e or not is_step(g, 0):
                            pe.wait_ge(act_done, E * FT * g + max(FT * e + f - 3, 0))
                        pe.matmul(h_bank[f][:, :], w1[:, e, f * P:(f + 1) * P],
                                  x2T[:, bass.ds(G * g, G), :].rearrange("p g t -> p (g t)"), start=True, stop=True).then_inc(hid, 1)
                    if e:
                        second(e - 1)
                second(E - 1)

            turn(0)
            with pe.Fori(1, NG) as i:
                turn(i)

        @block.scalar
        def _(act):
            act.wait_ge(loaded, 16 * (3 + E))

            def turn(g):
                for e in range(E):
                    for f in range(FT):
                        act.wait_ge(hid, E * FT * g + FT * e + f + 1)
                        if e >= 2 or not is_step(g, 0):
                            act.wait_ge(y_ready, E * g + max(e - 1, 0))
                        act.activation(hT[e % 2][:, f, :], h_bank[f][:, :], ACT.Silu, bias=b1c[:, e, f:f + 1]).then_inc(act_done, 1)

            turn(0)
            with act.Fori(1, NG) as i:
                turn(i)
            norm_act(act, norm, dev_in, dev_out)

        @block.vector
        def _(dve):
            dve.wait_ge(loaded, 16 * (3 + E))
            with dve.Fori(0, NG) as g:
                for e in range(E):
                    dve.wait_ge(y_ready, E * g + e + 1)
                    for i in range(G):
                        w = pick_w[:, bass.ds(G * g + i, 1), e:e + 1].rearrange("p o c -> p (o c)")
                        xb = r_all[:, bass.ds(G * g + i, 1), :].rearrange("p o d -> p (o d)")
                        last = dve.scalar_tensor_tensor(xb, y_bank[e % 2][:, i * P:(i + 1) * P], w, xb, ALU.mult, ALU.add)
                    last.then_inc(y_added, 1)
                    dve.wait_ge(y_added, E * g + e + 1)
                    for i in range(G):
                        w = pick_w[:, bass.ds(G * g + i, 1), e:e + 1].rearrange("p o c -> p (o c)")
                        xb = r_all[:, bass.ds(G * g + i, 1), :].rearrange("p o d -> p (o d)")
                        last = dve.scalar_tensor_tensor(xb, b2r[:, e, :], w, xb, ALU.mult, ALU.add)
                    last.then_inc(y_kept, 1)
                    dve.wait_ge(y_kept, E * g + e + 1)
                dve.wait_ge(loaded, 16 * (3 + E))
                for i in range(G):
                    last = dve.bn_stats(stats[:, bass.ds(G * g + i, 1), :].rearrange("p o d -> p (o d)"),
                                        r_all[:, bass.ds(G * g + i, 1), :].rearrange("p o d -> p (o d)"))
                last.then_inc(stats_done, 1)
            dve.wait_ge(stats_done, NG)
            norm_dve(dve, stats, norm, dev_in, dev_out)
            for g in range(NG):
                if g >= 2:
                    dve.wait_ge(stored[g % 2], 16 * (g // 2))
                for i in range(G):
                    b = G * g + i
                    last = dve.tensor_scalar(o[g % 2][:, i, :], r_all[:, b, :], norm["mean"][:, b:b + 1], norm["rstd"][:, b:b + 1], ALU.subtract, ALU.mult)
                last.then_inc(o_ready, 1)


def build(nc, x, context, Wq, Wk, Wv, Wo, betas, xWq, xWk, xWv, Wg, bg, W1, b1, W2, b2, consts, out):
    with ExitStack() as ctx:
        const = ctx.enter_context(nc.sbuf_tensor("const", [P, NCONST], F32))
        r_all = ctx.enter_context(nc.sbuf_tensor("r_all", [P, B, D], F32))
        stats = ctx.enter_context(nc.sbuf_tensor("stats", [P, B, 6], F32))
        scratch_qv = nc.dram_tensor("scratch_qv", (B, P, C, 3 * DK), F32, kind="Internal").ap()
        scratch_v = nc.dram_tensor("scratch_v", (B, P, C, DK), F32, kind="Internal").ap()
        attention_phase(nc, consts, const, r_all, stats, x, Wq, Wk, Wv, Wo, betas, scratch_qv, scratch_v)
        retention_phase(nc, const, r_all, stats, context, xWq, xWk, xWv)
        x2T = ctx.enter_context(nc.sbuf_tensor("x2T", [P, B, P], F32))
        pick_w = ctx.enter_context(nc.sbuf_tensor("pick_w", [P, B, E], F32))
        gate_phase(nc, const, r_all, stats, x2T, pick_w, Wg, bg)
        dense_phase(nc, x2T, r_all, stats, pick_w, W1, b1, W2, b2, out)


_NAMES = ["x", "ctx_1024", "L0_attn_Wq", "L0_attn_Wk", "L0_attn_Wv", "L0_attn_Wo", "L0_attn_betas",
          "L0_xattn_Wq", "L0_xattn_Wk", "L0_xattn_Wv", "L0_ffn_Wg", "L0_ffn_bg", "L0_ffn_W1", "L0_ffn_b1",
          "L0_ffn_W2", "L0_ffn_b2"]


def kernel(**inputs):
    import numpy as _np
    import concourse.bacc as _bacc
    from concourse import mybir as _mybir
    from concourse.bass_utils import run_bass_kernel_spmd as _run

    nc = _bacc.Bacc("TRN2", target_bir_lowering=False, num_devices=1)
    arrays, args = {}, []
    for name in _NAMES:
        a = _np.ascontiguousarray(inputs[name])
        arrays[f"in_{name}_dram"] = a
        args.append(nc.dram_tensor(f"in_{name}_dram", a.shape, _mybir.dt.from_np(a.dtype), kind="ExternalInput").ap())
    a = shape_constants()
    arrays["in_consts_dram"] = a
    args.append(nc.dram_tensor("in_consts_dram", a.shape, _mybir.dt.from_np(a.dtype), kind="ExternalInput").ap())
    args.append(nc.dram_tensor("out_0_dram", (B, P, D), F32, kind="ExternalOutput").ap())
    build(nc, *args)
    r = _run(nc, [arrays], core_ids=[0])
    return r.results[0]["out_0_dram"]
```

```python
from contextlib import ExitStack

import numpy as np
import concourse.bass as bass
from concourse import mybir

F32 = mybir.dt.float32
U32 = mybir.dt.uint32
ALU = mybir.AluOpType
ACT = mybir.ActivationFunctionType
X = mybir.AxisListType.X

P = 128
B = 32
D = 128
H = 16
SEG = 2
L = 64
DK = 64
C = 16
J = L // H
HF = C * DK
BANK = 512
EPS = 1e-5
SM_SCALE = 1.0 / np.sqrt(DK)
E = 8
HID = 512
FT = HID // P
G = 4
NG = B // G
NT = B + E - 1


def shape_constants():
    ident = np.eye(P, dtype=np.float32)
    tok = np.arange(P)
    head, seg = (tok % L) // J, tok // L
    same = head[:, None] == head[None, :]
    both = same.astype(np.float32)
    first = (same & (seg[:, None] == 0)).astype(np.float32)
    half = D // 2
    scale_vec = (np.arange(0, D, 2, dtype=np.float32) + np.float32(0.4 * D)) / np.float32(1.4 * D)
    pos = np.arange(P, dtype=np.float32)
    scale = scale_vec[None, :] ** (pos / np.float32(512.0))[:, None]
    freqs = np.float32(1.0) / np.float32(10000.0) ** (np.arange(half, dtype=np.float32) / np.float32(half))
    ang = pos[:, None] * freqs[None, :]
    sin, cos = np.sin(ang), np.cos(ang)
    tabs = []
    for s in (scale, np.float32(1.0) / scale):
        for t in (cos, sin):
            tabs.append(np.repeat(t * s, 2, axis=-1).T)
    diff = pos[None, :] - pos[:, None]
    decay = np.where(diff >= 0, np.float32(0.96875) ** np.maximum(diff, 0), 0.0)

    def row(values):
        return np.tile(np.asarray(values, np.float32).reshape(1, -1), (P, 1))

    iota = row(np.arange(E))
    below = (tok[:, None] < tok[None, :]).astype(np.float32)
    ones = np.ones((P, P), np.float32)
    upto = row(np.arange(E)[None, :] <= np.arange(E)[:, None])
    tile_at = row(np.arange(NT))
    full = row(P * np.arange(B))
    cols = [ident, both, first] + tabs + [decay, iota, below, ones, upto, tile_at, full]
    return np.ascontiguousarray(np.concatenate(cols, axis=1).astype(np.float32))


CONST_AT = {}
_at = 0
for _n, _w in (("ident", P), ("both", P), ("first", P), ("qcos", P), ("qsin", P), ("kcos", P), ("ksin", P),
               ("decay", P), ("iota", E), ("below", P), ("ones", P), ("upto", E * E),
               ("tile_at", NT), ("full", B)):
    CONST_AT[_n] = (_at, _at + _w)
    _at += _w
NCONST = _at


def run_steps(eng, step, n, peeled=1):
    for i in range(peeled):
        step(i, 0, True, i > 0)
        step(i, 1, True, True)
    with eng.Fori(peeled, n // 2) as i:
        step(i, 0, True, True)
        step(i, 1, True, True)
    if n % 2:
        step(n // 2, 0, True, True)
    step(n // 2, n % 2, False, True)


def is_step(t, *values):
    return isinstance(t, int) and t in values


def norm_act(act, n, ready, sq_ready):
    act.wait_ge(ready, 3)
    act.activation(n["dev"][:, :], n["var"][:, :], ACT.Sqrt).then_inc(sq_ready, 1)


def norm_dve(dve, stats, n, ready, sq_ready):
    mean, var, rstd, tmp = (n[k][:, :] for k in ("mean", "var", "rstd", "tmp"))

    def col(c):
        return stats[:, :, c:c + 1].rearrange("p b o -> p (b o)")

    dve.tensor_tensor(mean, col(1), col(4), ALU.add)
    dve.tensor_tensor(tmp, col(1), col(4), ALU.subtract)
    dve.tensor_tensor(var, col(2), col(5), ALU.add).then_inc(ready, 1)
    dve.wait_ge(ready, 1)
    dve.tensor_scalar(mean, mean, 0.5, None, ALU.mult)
    dve.tensor_scalar(var, var, 1.0 / D, EPS, ALU.mult, ALU.add)
    dve.scalar_tensor_tensor(rstd, tmp, 0.25, tmp, ALU.mult, ALU.mult).then_inc(ready, 1)
    dve.wait_ge(ready, 2)
    dve.tensor_tensor(var, var, rstd, ALU.add).then_inc(ready, 1)
    dve.wait_ge(sq_ready, 1)
    dve.reciprocal(rstd, n["dev"][:, :]).then_inc(ready, 1)
    dve.wait_ge(ready, 4)
    dve.tensor_tensor(tmp, rstd, rstd, ALU.mult).then_inc(ready, 1)
    dve.wait_ge(ready, 5)
    dve.tensor_tensor(tmp, tmp, var, ALU.mult).then_inc(ready, 1)
    dve.wait_ge(ready, 6)
    dve.tensor_scalar(tmp, tmp, -0.5, 1.5, ALU.mult, ALU.add).then_inc(ready, 1)
    dve.wait_ge(ready, 7)
    dve.tensor_tensor(rstd, rstd, tmp, ALU.mult).then_inc(ready, 1)
    dve.wait_ge(ready, 8)


def attention_phase(nc, consts, const, r_all, stats, x, Wq, Wk, Wv, Wo, betas, scratch_qv, scratch_v):
    with ExitStack() as ctx:
        def sb(name, shape):
            return ctx.enter_context(nc.sbuf_tensor(name, shape, F32))

        def sem(name):
            return ctx.enter_context(nc.semaphore(name))

        def cst(name):
            return const[:, CONST_AT[name][0]:CONST_AT[name][1]]

        w_k, w_q, w_v = sb("w_k", [P, HF]), sb("w_q", [P, HF]), sb("w_v", [P, HF])
        w_o = sb("w_o", [P, C // 2, D])
        xT = sb("xT", [P, B + 1, P])
        x_cur = [sb(f"x_cur{i}", [P, P]) for i in range(2)]
        gate = sb("gate", [P, DK])
        ungate = sb("ungate", [P, DK])
        qk_tok = sb("qk_tok", [P, C, 2 * DK])
        e_qk = sb("e_qk", [P, C, 2 * DK])
        v_tok = sb("v_tok", [P, C, DK])
        qv_out = sb("qv_out", [P, C, 3 * DK])
        v_un = sb("v_un", [P, C, DK])
        k_sum = sb("k_sum", [P, DK])
        z = sb("z", [P, 2, DK])
        zg = sb("zg", [P, 2, DK])
        qT = sb("qT", [DK, P, C])
        kT = sb("kT", [DK, P, C])
        s_max = sb("s_max", [P, H])
        s_exp = sb("s_exp", [P, H, L])
        row_sum = sb("row_sum", [P, H])
        row_rec = sb("row_rec", [P, H])
        sq_sum = sb("sq_sum", [P, H])
        sq_rec = sb("sq_rec", [P, H])
        ps = sb("ps", [P, H, 2 * DK])
        psT = sb("psT", [P, H, P])
        pos_qv = [sb(f"pos_qv{i}", [P, H, 3 * DK]) for i in range(2)]
        lhs = [sb(f"lhs{i}", [P, SEG, H, DK]) for i in range(2)]
        attT = sb("attT", [P, C // 2, P])
        banks = [ctx.enter_context(nc.psum_tensor(f"bank{i}", [P, BANK], F32)) for i in range(8)]
        proj_bank, turn_bank, score_bank, mix_bank = banks[0:2], banks[2:4], banks[4:6], banks[6:8]

        loaded = sem("loaded")
        beta_loaded = sem("beta_loaded")
        xt_ready, xt_evac = sem("xt_ready"), sem("xt_evac")
        tanh_ready, gate_ready = sem("tanh_ready"), sem("gate_ready")
        x_pad, v_pad, x_staged = sem("x_pad"), sem("v_pad"), sem("x_staged")
        k_proj, q_proj, v_proj = sem("k_proj"), sem("q_proj"), sem("v_proj")
        k_evac, q_evac, v_evac = sem("k_evac"), sem("q_evac"), sem("v_evac")
        exp_cut, sk_ready, sq_ready, k_summed = sem("exp_cut"), sem("sk_ready"), sem("sq_ready"), sem("k_summed")
        zc_ready, z_rec, z_ready = sem("zc_ready"), sem("z_rec"), sem("z_ready")
        vboth_ready, vfirst_ready, vun_ready = sem("vboth_ready"), sem("vfirst_ready"), sem("vun_ready")
        stored_qv, stored_v = sem("stored_qv"), sem("stored_v")
        qv_loaded = [sem(f"qv_loaded{i}") for i in range(2)]
        v_loaded = [sem(f"v_loaded{i}") for i in range(2)]
        turned, qT_evac, kT_evac = sem("turned"), sem("qT_evac"), sem("kT_evac")
        scored, maxed, shifted, exped = sem("scored"), sem("maxed"), sem("shifted"), sem("exped")
        row_summed, row_inv, p_ready = sem("row_summed"), sem("row_inv"), sem("p_ready")
        sq_summed, sq_inv, sqn_ready = sem("sq_summed"), sem("sq_inv"), sem("sqn_ready")
        ps_turned, psT_evac = sem("ps_turned"), sem("psT_evac")
        mem_ready, mem_evac = sem("mem_ready"), sem("mem_evac")
        att_ready, att_evac = sem("att_ready"), sem("att_evac")
        out_ready, res_ready = sem("out_ready"), sem("res_ready")

        NLOAD = 6
        block = ctx.enter_context(nc.Block())

        @block.sync
        def _(sp):
            sp.dma_start(r_all[:, :, :], x.rearrange("b p d -> p b d")).then_inc(loaded, 16)
            sp.dma_start(const[:, :], consts).then_inc(loaded, 16)
            sp.dma_start(w_k[:, :], Wk).then_inc(loaded, 16)
            sp.dma_start(w_q[:, :], Wq).then_inc(loaded, 16)
            sp.dma_start(w_v[:, :], Wv).then_inc(loaded, 16)
            sp.dma_start(w_o[:, :, :], Wo.rearrange("(c p) m -> p c m", p=P)).then_inc(loaded, 16)
            stored = 0

            def step(half, p, one, two):
                if not one:
                    return
                t = 2 * half + p
                sp.wait_ge(sq_ready, t + 1)
                sp.wait_ge(vboth_ready, t + 1)
                sp.wait_ge(vfirst_ready, t + 1)
                for n, w in ((0, 3 * DK), (1, 2 * DK)):
                    sp.dma_start(scratch_qv[bass.ds(t, 1), n * L:(n + 1) * L, :, 0:w].rearrange("o p c e -> (o p) c e"),
                                 qv_out[n * L:(n + 1) * L, :, 0:w]).then_inc(stored_qv, 16)
                sp.wait_ge(vun_ready, t + 1)
                sp.dma_start(scratch_v[bass.ds(t, 1)].rearrange("o p c e -> (o p) c e"), v_un[:, :, :]).then_inc(stored_v, 16)
                sp.wait_ge(stored_qv, 32 * (t + 1))
                for n, w in ((0, 3 * DK), (1, 2 * DK)):
                    src = scratch_qv[bass.ds(t, 1), n * L:(n + 1) * L, :, 0:w]
                    sp.dma_start(pos_qv[p][n * L:(n + 1) * L, :, 0:w],
                                 src.rearrange("o (h j) c e -> (o j c) h e", j=J)).then_inc(qv_loaded[p], 16)
                sp.wait_ge(stored_v, 16 * (t + 1))
                for n in range(SEG):
                    src = scratch_v[bass.ds(t, 1), n * L:(n + 1) * L]
                    sp.dma_start(lhs[p][0:L, 1 - n, :, :], src.rearrange("o (h j) c e -> (o j c) h e", j=J)).then_inc(v_loaded[p], 16)

            run_steps(sp, step, B)

        @block.gpsimd
        def _(pool):
            for n in range(SEG):
                for j in range(J):
                    a = n * L + j
                    pool.dma_start(gate[a:a + L - J + 1:J, :], betas.rearrange("o h q v -> (o h q) v")).then_inc(beta_loaded, 16)

            def stage_x(t, p):
                if not (isinstance(t, int) and t < 2):
                    pool.wait_ge(v_proj, 2 * (t - 1))
                pool.tensor_copy(x_cur[p][:, :], xT[:, bass.ds(t, 1), :].rearrange("p o c -> p (o c)")).then_inc(x_staged, 1)

            pool.memset(xT[:, B:B + 1, :], 0.0).then_inc(x_pad, 1)
            pool.wait_ge(x_pad, 1)
            pool.wait_ge(xt_evac, B // 4)
            stage_x(0, 0)

            def step(half, p, one, two):
                t = 2 * half + p
                if one:
                    stage_x(t + 1, 1 - p)
                if two:
                    q = 1 - p
                    u = t - 1
                    pool.wait_ge(sq_inv, t)
                    if not (isinstance(u, int) and u == 0):
                        pool.wait_ge(ps_turned, 4 * u)
                    pool.tensor_tensor(ps[:, :, DK:], pos_qv[q][:, :, 0:DK],
                                       sq_rec[:, :].unsqueeze(2).to_broadcast([P, H, DK]), ALU.mult).then_inc(sqn_ready, 1)
                if one:
                    pool.wait_ge(v_evac, 2 * (t + 1))
                    pool.wait_ge(gate_ready, 2)
                    if not (isinstance(t, int) and t == 0):
                        pool.wait_ge(stored_v, 16 * t)
                        pool.wait_ge(stored_qv, 32 * t)
                    pool.tensor_tensor(v_un[:, :, :], v_tok[:, :, :],
                                       ungate[:, :].unsqueeze(1).to_broadcast([P, C, DK]), ALU.mult).then_inc(vun_ready, 1)
                    pool.wait_ge(z_ready, t + 1)
                    pool.tensor_tensor(qv_out[0:L, :, 2 * DK:], v_tok[0:L, :, :],
                                       zg[0:L, 1, :].unsqueeze(1).to_broadcast([L, C, DK]), ALU.mult).then_inc(vfirst_ready, 1)
                    for hh in range(2):
                        pool.wait_ge(row_inv, 2 * t + hh + 1)
                        if hh == 0 and not (isinstance(t, int) and t == 0):
                            pool.wait_ge(ps_turned, 4 * t)
                        s = slice(8 * hh, 8 * hh + 8)
                        pool.tensor_tensor(ps[:, s, 0:DK], s_exp[:, s, :],
                                           row_rec[:, s].unsqueeze(2).to_broadcast([P, 8, L]), ALU.mult).then_inc(p_ready, 1)

            run_steps(pool, step, B)

        @block.tensor
        def _(pe):
            pe.wait_ge(v_pad, 2)
            pe.wait_ge(loaded, 16 * NLOAD)
            for g in range(B // 4):
                for i in range(4):
                    last = pe.transpose(banks[g][:, i * P:(i + 1) * P], r_all[:, 4 * g + i, :], cst("ident"))
                last.then_inc(xt_ready, 1)

            def step(half, p, one, two):
                t = 2 * half + p
                u = t - 1
                first = isinstance(t, int) and t == 0
                second = isinstance(t, int) and t == 1
                if one:
                    xt_b = x_cur[p][:, :]
                    pe.wait_ge(x_staged, t + 1)

                    def project(w, hh, done):
                        pe.matmul(proj_bank[hh][:, :], xt_b, w[:, hh * BANK:(hh + 1) * BANK],
                                  start=True, stop=True).then_inc(done, 1)
                    if not first:
                        pe.wait_ge(v_evac, 2 * t - 1)
                    project(w_k, 0, k_proj)
                    if not first and not second:
                        pe.wait_ge(res_ready, t - 1)
                    project(w_k, 1, k_proj)
                    for hh in range(2):
                        pe.wait_ge(k_evac, 2 * t + hh + 1)
                        project(w_q, hh, q_proj)

                def turn_ps(f):
                    if f < 2:
                        pe.wait_ge(qT_evac, 4 * u + 3 + f)
                        pe.wait_ge(kT_evac, 4 * u + 3 + f)
                    else:
                        pe.wait_ge(psT_evac, 4 * u + f - 1)
                    if f == 0:
                        pe.wait_ge(sqn_ready, t)
                    if f % 2 == 0:
                        pe.wait_ge(p_ready, 2 * u + f // 2 + 1)
                    for i in range(4):
                        last = pe.transpose(turn_bank[f % 2][:, i * P:(i + 1) * P], ps[:, 4 * f + i, :], cst("ident"))
                    last.then_inc(ps_turned, 1)

                def turn_qk(f):
                    if f < 2:
                        if two:
                            pe.wait_ge(psT_evac, 4 * u + 3 + f)
                    else:
                        pe.wait_ge(qT_evac, 4 * t + f - 1)
                        pe.wait_ge(kT_evac, 4 * t + f - 1)
                    if f == 0:
                        pe.wait_ge(k_evac, 2 * t + 2)
                        pe.wait_ge(q_evac, 2 * t + 2)
                    for i in range(4):
                        last = pe.transpose(turn_bank[f % 2][:, i * P:(i + 1) * P], qk_tok[:, 4 * f + i, :], cst("ident"))
                    last.then_inc(turned, 1)

                def attend(f):
                    n, hh = f // 2, f % 2
                    if f == 0:
                        pe.wait_ge(v_loaded[q], 32 * (hq + 1))
                        pe.wait_ge(psT_evac, 4 * u + 4)
                        pe.wait_ge(mem_evac, 4 * u + 4)
                    if f >= 2:
                        pe.wait_ge(att_evac, 4 * u + f - 1)
                    for i in range(8):
                        h = 8 * hh + i
                        last = pe.matmul(mix_bank[f % 2][0:DK, i * L:(i + 1) * L], lhs[q][:, 1 - n, h, :],
                                         psT[:, h, n * L:(n + 1) * L], start=True, stop=True)
                    last.then_inc(att_ready, 1)

                q = 1 - p
                hq = half if p == 1 else half - 1
                if two:
                    turn_ps(0)
                    turn_ps(1)
                if one:
                    for hh in range(2):
                        pe.wait_ge(q_evac, 2 * t + hh + 1)
                        project(w_v, hh, v_proj)
                    pe.wait_ge(k_summed, t + 1)
                    if not first:
                        pe.wait_ge(shifted, 2 * t - 1)
                    pe.matmul(score_bank[0][:, 0:DK], cst("both"), k_sum[:, :], start=True, stop=True)
                    pe.matmul(score_bank[0][:, DK:2 * DK], cst("first"), k_sum[:, :], start=True, stop=True).then_inc(zc_ready, 1)
                if two:
                    turn_ps(2)
                    turn_ps(3)
                    pe.wait_ge(qv_loaded[q], 32 * (hq + 1))
                    for f in range(4):
                        if f < 2:
                            if not second:
                                pe.wait_ge(att_evac, 4 * (u - 1) + 3 + f)
                        else:
                            pe.wait_ge(mem_evac, 4 * u + f - 1)
                        for i in range(4):
                            last = pe.matmul(mix_bank[f % 2][DK:, i * P:(i + 1) * P], pos_qv[q][:, 4 * f + i, 0:DK],
                                             pos_qv[q][:, 4 * f + i, DK:], start=True, stop=True)
                        last.then_inc(mem_ready, 1)
                for f in (0, 2):
                    if one:
                        turn_qk(f)
                        turn_qk(f + 1)
                    if two:
                        attend(f)
                        attend(f + 1)
                if one:
                    pe.wait_ge(qT_evac, 4 * t + 4)
                    pe.wait_ge(kT_evac, 4 * t + 4)
                    for hh in range(2):
                        if hh == 0:
                            pe.wait_ge(z_rec, t + 1)
                        elif not first:
                            pe.wait_ge(shifted, 2 * t)
                        for i in range(8):
                            if i == 0:
                                tok = J * 8 * hh
                                pe.matmul(score_bank[hh][:, 0:L], qT[:, tok:tok + 2 * J, :], kT[:, tok:tok + J, :],
                                          start=True, stop=True)
                            for n in range(1 if i == 0 else 0, SEG):
                                tok = n * L + J * (8 * hh + i)
                                last = pe.matmul(score_bank[hh][n * L:(n + 1) * L, i * L:(i + 1) * L],
                                                 qT[:, tok:tok + J, :], kT[:, tok:tok + J, :], start=True, stop=True)
                        last.then_inc(scored, 1)
                if two:
                    pe.wait_ge(att_evac, 4 * u + 4)
                    if one:
                        pe.wait_ge(v_evac, 2 * t + 2)
                    else:
                        pe.wait_ge(res_ready, t - 1)
                    for c in range(C // 2):
                        last = pe.matmul(proj_bank[1][:, 0:D], attT[:, c, :], w_o[:, c, :], start=(c == 0), stop=(c == C // 2 - 1))
                    last.then_inc(out_ready, 1)

            run_steps(pe, step, B)

        @block.scalar
        def _(act):
            act.wait_ge(beta_loaded, 16 * SEG * J)
            act.activation(gate[:, :], gate[:, :], ACT.Tanh, scale=0.5).then_inc(tanh_ready, 1)
            for g in range(B // 4):
                act.wait_ge(xt_ready, g + 1)
                act.activation(xT[:, 4 * g:4 * g + 4, :], banks[g][:, :].rearrange("p (b c) -> p b c", b=4), ACT.Copy).then_inc(xt_evac, 1)

            def step(half, p, one, two):
                t = 2 * half + p
                u = t - 1
                first = isinstance(t, int) and t == 0
                second = isinstance(t, int) and t == 1
                if one:
                    for slot, proj, evac in ((1, k_proj, k_evac), (0, q_proj, q_evac)):
                        s = slice(slot * DK, (slot + 1) * DK)
                        for hh in range(2):
                            act.wait_ge(proj, 2 * t + hh + 1)
                            if hh == 0 and slot == 1 and not first:
                                act.wait_ge(turned, 4 * t)
                                act.wait_ge(sq_ready, t)
                                act.wait_ge(k_summed, t)
                            c = slice(8 * hh, 8 * hh + 8)
                            bank = proj_bank[hh][:, :].rearrange("p (c k) -> p c k", c=8)
                            act.activation(e_qk[:, c, s], bank, ACT.Exp)
                            act.activation(qk_tok[:, c, s], bank, ACT.Copy).then_inc(evac, 1)

                def evac_ps(f):
                    act.wait_ge(ps_turned, 4 * u + f + 1)
                    if f == 0 and not second:
                        act.wait_ge(att_ready, 4 * u)
                    act.activation(psT[:, 4 * f:4 * f + 4, :], turn_bank[f % 2][:, :].rearrange("p (h s) -> p h s", h=4),
                                   ACT.Copy).then_inc(psT_evac, 1)

                def evac_q(f):
                    act.wait_ge(turned, 4 * t + f + 1)
                    if f == 0 and not first:
                        act.wait_ge(scored, 2 * t)
                    act.activation(qT[:, :, 4 * f:4 * f + 4],
                                   turn_bank[f % 2][0:DK, :].rearrange("p (c s) -> p s c", c=4), ACT.Copy).then_inc(qT_evac, 1)

                def evac_att(f):
                    n, hh = f // 2, f % 2
                    act.wait_ge(att_ready, 4 * u + f + 1)
                    if f == 0 and not second:
                        act.wait_ge(out_ready, u)
                    at = n * L + hh * 32
                    src = mix_bank[f % 2][0:DK, :].rearrange("p (t c two) -> p two c t", c=C // 2, two=2)
                    for odd in range(2):
                        last = act.activation(attT[odd * DK:(odd + 1) * DK, :, at:at + 32], src[:, odd, :, :], ACT.Copy)
                    last.then_inc(att_evac, 1)

                if two:
                    evac_ps(0)
                    evac_ps(1)
                if one:
                    for hh in range(2):
                        act.wait_ge(v_proj, 2 * t + hh + 1)
                        if hh == 0 and not first:
                            act.wait_ge(vboth_ready, t)
                            act.wait_ge(vfirst_ready, t)
                            act.wait_ge(vun_ready, t)
                        act.activation(v_tok[:, 8 * hh:8 * hh + 8, :], proj_bank[hh][:, :].rearrange("p (c k) -> p c k", c=8),
                                       ACT.Copy).then_inc(v_evac, 1)
                if two:
                    evac_ps(2)
                    evac_ps(3)
                    q = 1 - p
                    for f in range(4):
                        act.wait_ge(mem_ready, 4 * u + f + 1)
                        act.activation(lhs[q][DK:, :, 4 * f:4 * f + 4, :].rearrange("p n h k -> p h n k"),
                                       mix_bank[f % 2][DK:, :].rearrange("p (h n k) -> p h n k", n=SEG, h=4), ACT.Copy).then_inc(mem_evac, 1)
                for f in (0, 2):
                    if one:
                        evac_q(f)
                        evac_q(f + 1)
                    if two:
                        evac_att(f)
                        evac_att(f + 1)
                if one:
                    for hh in range(2):
                        act.wait_ge(shifted, 2 * t + hh + 1)
                        s = slice(8 * hh, 8 * hh + 8)
                        act.activation(s_exp[:, s, :], s_exp[:, s, :], ACT.Exp, scale=float(SM_SCALE)).then_inc(exped, 1)

            run_steps(act, step, B)

        @block.vector
        def _(dve):
            for i in range(2):
                dve.memset(pos_qv[i][L:, :, 2 * DK:], 0.0).then_inc(v_pad, 1)
            dve.wait_ge(tanh_ready, 1)
            dve.tensor_scalar(ungate[:, :], gate[:, :], -0.5, 0.5, ALU.mult, ALU.add).then_inc(gate_ready, 1)
            dve.wait_ge(gate_ready, 1)
            dve.tensor_scalar(gate[:, :], gate[:, :], 0.5, 0.5, ALU.mult, ALU.add).then_inc(gate_ready, 1)

            def step(half, p, one, two):
                t = 2 * half + p
                u = t - 1
                first = isinstance(t, int) and t == 0
                if one:
                    dve.wait_ge(k_evac, 2 * t + 2)
                    dve.tensor_scalar(e_qk[:, :, DK:], e_qk[:, :, DK:], 1.0, None, ALU.min).then_inc(exp_cut, 1)
                    dve.wait_ge(exp_cut, 2 * t + 1)
                    dve.scalar_tensor_tensor(e_qk[:, :, DK:], qk_tok[:, :, DK:], 1.0, e_qk[:, :, DK:],
                                             ALU.add, ALU.max).then_inc(sk_ready, 1)
                    dve.wait_ge(sk_ready, t + 1)
                    if not first:
                        dve.wait_ge(zc_ready, t)
                    dve.tensor_reduce(k_sum[:, :], e_qk[:, :, DK:].rearrange("p c k -> p k c"), X, ALU.add).then_inc(k_summed, 1)
                    dve.wait_ge(q_evac, 2 * t + 2)
                    dve.tensor_scalar(e_qk[:, :, 0:DK], e_qk[:, :, 0:DK], 1.0, None, ALU.min).then_inc(exp_cut, 1)
                    dve.wait_ge(exp_cut, 2 * t + 2)
                    if not first:
                        dve.wait_ge(stored_qv, 32 * t)
                    dve.scalar_tensor_tensor(qv_out[:, :, 0:DK], qk_tok[:, :, 0:DK], 1.0, e_qk[:, :, 0:DK],
                                             ALU.add, ALU.max).then_inc(sq_ready, 1)
                    dve.wait_ge(zc_ready, t + 1)
                    if not first:
                        dve.wait_ge(z_ready, t)
                    dve.reciprocal(z[:, :, :], score_bank[0][:, 0:2 * DK].rearrange("p (a k) -> p a k", a=2)).then_inc(z_rec, 1)
                    dve.wait_ge(z_rec, t + 1)
                    if not first:
                        dve.wait_ge(vfirst_ready, t)
                        dve.wait_ge(vboth_ready, t)
                    dve.tensor_tensor(zg[:, :, :], z[:, :, :], gate[:, :].unsqueeze(1).to_broadcast([P, 2, DK]),
                                      ALU.mult).then_inc(z_ready, 1)
                    dve.wait_ge(z_ready, t + 1)
                    dve.wait_ge(v_evac, 2 * t + 2)
                    dve.tensor_tensor(qv_out[:, :, DK:2 * DK], v_tok[:, :, :],
                                      zg[:, 0, :].unsqueeze(1).to_broadcast([P, C, DK]), ALU.mult).then_inc(vboth_ready, 1)
                    for f in range(4):
                        dve.wait_ge(turned, 4 * t + f + 1)
                        if f == 0 and not first:
                            dve.wait_ge(scored, 2 * t)
                        dve.tensor_copy(kT[:, :, 4 * f:4 * f + 4],
                                        turn_bank[f % 2][DK:, :].rearrange("p (c s) -> p s c", c=4)).then_inc(kT_evac, 1)
                    for hh in range(2):
                        s = slice(8 * hh, 8 * hh + 8)
                        bank = score_bank[hh][:, :].rearrange("p (h t) -> p h t", h=8)
                        dve.wait_ge(scored, 2 * t + hh + 1)
                        dve.tensor_reduce(s_max[:, s], bank, X, ALU.max).then_inc(maxed, 1)
                        dve.wait_ge(maxed, 2 * t + hh + 1)
                        if not first:
                            dve.wait_ge(p_ready, 2 * t - 1 + hh)
                        dve.tensor_tensor(s_exp[:, s, :], bank, s_max[:, s].unsqueeze(2).to_broadcast([P, 8, L]),
                                          ALU.subtract).then_inc(shifted, 1)
                    for hh in range(2):
                        s = slice(8 * hh, 8 * hh + 8)
                        dve.wait_ge(exped, 2 * t + hh + 1)
                        dve.tensor_reduce(row_sum[:, s], s_exp[:, s, :], X, ALU.add).then_inc(row_summed, 1)
                        dve.wait_ge(row_summed, 2 * t + hh + 1)
                        dve.reciprocal(row_rec[:, s], row_sum[:, s]).then_inc(row_inv, 1)
                if two:
                    dve.wait_ge(out_ready, t)
                    rb = r_all[:, bass.ds(u, 1), :].rearrange("p o d -> p (o d)")
                    dve.tensor_tensor(rb, proj_bank[1][:, 0:D], rb, ALU.add).then_inc(res_ready, 1)
                    dve.wait_ge(res_ready, t)
                    dve.wait_ge(loaded, 16 * NLOAD)
                    dve.bn_stats(stats[:, bass.ds(u, 1), :].rearrange("p o d -> p (o d)"), rb)
                if one:
                    dve.wait_ge(qv_loaded[p], 32 * (half + 1))
                    if not first:
                        dve.wait_ge(sqn_ready, t)
                    dve.tensor_reduce(sq_sum[:, :], pos_qv[p][:, :, 0:DK], X, ALU.add).then_inc(sq_summed, 1)
                    dve.wait_ge(sq_summed, t + 1)
                    dve.reciprocal(sq_rec[:, :], sq_sum[:, :]).then_inc(sq_inv, 1)

            run_steps(dve, step, B)


def retention_phase(nc, const, r_all, stats, ctx_in, Wq, Wk, Wv, preload):
    with ExitStack() as ctx:
        def sb(name, shape):
            return ctx.enter_context(nc.sbuf_tensor(name, shape, F32))

        def sem(name):
            return ctx.enter_context(nc.semaphore(name))

        def cst(name):
            return const[:, CONST_AT[name][0]:CONST_AT[name][1]]

        def four(ap):
            return ap.unsqueeze(1).to_broadcast([P, G, P])

        wq, wk, wv = sb("r_wq", [P, D]), sb("r_wk", [P, D]), sb("r_wv", [P, D])
        wq_rot, wk_rot = sb("wq_rot", [P, D]), sb("wk_rot", [P, D])
        norm = {n: sb("r_" + n, [P, B]) for n in ("mean", "var", "dev", "rstd", "tmp")}
        x1 = [sb(f"x1_{i}", [P, G, D]) for i in range(2)]
        cx = [sb(f"cx_{i}", [P, G, D]) for i in range(2)]
        x1T, cxT = sb("x1T", [P, G, P]), sb("cxT", [P, G, P])
        q_cos, q_sin, k_cos, k_sin = (sb(n, [P, G, P]) for n in ("q_cos", "q_sin", "k_cos", "k_sin"))
        qh = [sb(f"qh{i}", [P, G, P]) for i in range(2)]
        kh = [sb(f"kh{i}", [P, G, P]) for i in range(2)]
        vh = [sb(f"vh{i}", [P, G, D]) for i in range(2)]
        sc = sb("sc", [P, G, P])
        zero = sb("zero", [P, D])
        names = ("x1t", "cxt", "q", "qr", "k", "kr", "score", "out")
        bank = {n: ctx.enter_context(nc.psum_tensor(f"r_{n}", [P, BANK], F32)) for n in names}

        w_loaded, rot_ready = sem("w_loaded"), sem("rot_ready")
        zeroed, preloaded = sem("zeroed"), sem("preloaded")
        dev_in, dev_out = sem("dev_in"), sem("dev_out")
        cx_loaded = [sem(f"cx_loaded{i}") for i in range(2)]
        x1_ready, x1_turned, x1T_evac = sem("x1_ready"), sem("x1_turned"), sem("x1T_evac")
        cx_turned, cxT_evac = sem("cx_turned"), sem("cxT_evac")
        projected, scaled, qh_ready, kh_ready = sem("projected"), sem("scaled"), sem("qh_ready"), sem("kh_ready")
        v_done, v_evac = sem("v_done"), sem("rv_evac")
        scored, decayed = sem("r_scored"), sem("decayed")
        out_done, r_ready, bn_done, stats_done = sem("out_done"), sem("r_ready"), sem("bn_done"), sem("stats_done")
        block = ctx.enter_context(nc.Block())

        @block.sync
        def _(sp):
            sp.dma_start(wq[:, :], Wq).then_inc(w_loaded, 16)
            sp.dma_start(wk[:, :], Wk).then_inc(w_loaded, 16)
            sp.dma_start(wv[:, :], Wv).then_inc(w_loaded, 16)

            def step(half, p, one, two):
                t = 2 * half + p
                if one:
                    if not is_step(t, 0, 1):
                        sp.wait_ge(cx_turned, t - 1)
                    sp.dma_start(cx[p][:, :, :], ctx_in[bass.ds(G * t, G)].rearrange("b p d -> p b d")).then_inc(cx_loaded[p], 16)

            run_steps(sp, step, NG)
            sp.wait_ge(zeroed, 1)
            for target, source in preload:
                if source is None:
                    source = zero[:, :].unsqueeze(1).to_broadcast([P, NT, D])
                sp.dma_start(target, source).then_inc(preloaded, 16)
            sp.wait_ge(preloaded, 16 * len(preload))

        @block.gpsimd
        def _(pool):
            pool.memset(zero[:, :], 0.0).then_inc(zeroed, 1)

            def step(half, p, one, two):
                t = 2 * half + p
                if one:
                    pool.wait_ge(scaled, 4 * t + 2)
                    if not is_step(t, 0, 1):
                        pool.wait_ge(scored, t - 1)
                    pool.tensor_tensor(qh[p][:, :, :], q_cos[:, :, :], q_sin[:, :, :], ALU.add).then_inc(qh_ready, 1)
                    pool.wait_ge(scaled, 4 * t + 4)
                    pool.tensor_tensor(kh[p][:, :, :], k_cos[:, :, :], k_sin[:, :, :], ALU.add).then_inc(kh_ready, 1)

            run_steps(pool, step, NG)

        @block.tensor
        def _(pe):
            def step(half, p, one, two):
                t = 2 * half + p
                u = t - 1
                q = 1 - p
                hq = half if p == 1 else half - 1
                if one:
                    pe.wait_ge(cx_loaded[p], 16 * (half + 1))
                    if not is_step(t, 0):
                        pe.wait_ge(cxT_evac, t)
                    for i in range(G):
                        last = pe.transpose(bank["cxt"][:, i * P:(i + 1) * P], cx[p][:, i, :], cst("ident"))
                    last.then_inc(cx_turned, 1)
                    pe.wait_ge(x1_ready, t + 1)
                    if not is_step(t, 0):
                        pe.wait_ge(v_evac, t)
                    for i in range(G):
                        last = pe.transpose(bank["x1t"][:, i * P:(i + 1) * P], x1[p][:, i, :], cst("ident"))
                    last.then_inc(x1_turned, 1)
                if two:
                    pe.wait_ge(qh_ready, u + 1)
                    pe.wait_ge(kh_ready, u + 1)
                    if not is_step(t, 1):
                        pe.wait_ge(decayed, u)
                    for i in range(G):
                        last = pe.matmul(bank["score"][:, i * P:(i + 1) * P], kh[q][:, i, :], qh[q][:, i, :], start=True, stop=True)
                    last.then_inc(scored, 1)
                if one:
                    if is_step(t, 0):
                        pe.wait_ge(w_loaded, 48)
                        pe.wait_ge(rot_ready, 4)
                    pe.wait_ge(x1T_evac, t + 1)
                    for n, (name, w, src) in enumerate((("q", wq, x1T), ("qr", wq_rot, x1T), ("k", wk, cxT), ("kr", wk_rot, cxT))):
                        if n == 2:
                            pe.wait_ge(cxT_evac, t + 1)
                        if not is_step(t, 0):
                            pe.wait_ge(scaled, 4 * (t - 1) + n + 1)
                        pe.matmul(bank[name][:, :], w[:, :], src[:, :, :].rearrange("p g t -> p (g t)"),
                                  start=True, stop=True).then_inc(projected, 1)
                    for i in range(G):
                        last = pe.matmul(bank["x1t"][:, i * P:(i + 1) * P], cxT[:, i, :], wv[:, :], start=True, stop=True)
                    last.then_inc(v_done, 1)
                if two:
                    pe.wait_ge(decayed, u + 1)
                    pe.wait_ge(v_evac, u + 1)
                    if not is_step(t, 1):
                        pe.wait_ge(r_ready, u)
                    for i in range(G):
                        last = pe.matmul(bank["out"][:, i * P:(i + 1) * P], sc[:, i, :], vh[q][:, i, :], start=True, stop=True)
                    last.then_inc(out_done, 1)

            run_steps(pe, step, NG)

        @block.scalar
        def _(act):
            norm_act(act, norm, dev_in, dev_out)

            def step(half, p, one, two):
                t = 2 * half + p
                if one:
                    act.wait_ge(cx_turned, t + 1)
                    if not is_step(t, 0):
                        act.wait_ge(v_done, t)
                    act.activation(cxT[:, :, :], bank["cxt"][:, :].rearrange("p (g t) -> p g t", g=G), ACT.Copy).then_inc(cxT_evac, 1)
                    act.wait_ge(x1_turned, t + 1)
                    act.activation(x1T[:, :, :], bank["x1t"][:, :].rearrange("p (g t) -> p g t", g=G), ACT.Copy).then_inc(x1T_evac, 1)
                    act.wait_ge(v_done, t + 1)
                    if not is_step(t, 0, 1):
                        act.wait_ge(out_done, t - 1)
                    act.activation(vh[p][:, :, :], bank["x1t"][:, :].rearrange("p (g t) -> p g t", g=G), ACT.Copy).then_inc(v_evac, 1)

            run_steps(act, step, NG)

        @block.vector
        def _(dve):
            norm_dve(dve, stats, norm, dev_in, dev_out)
            dve.wait_ge(w_loaded, 48)
            for w, rot in ((wq, wq_rot), (wk, wk_rot)):
                pairs = w[:, :].rearrange("p (i two) -> p i two", two=2)
                turned = rot[:, :].rearrange("p (i two) -> p i two", two=2)
                dve.tensor_scalar(turned[:, :, 0:1], pairs[:, :, 1:2], -1.0, None, ALU.mult).then_inc(rot_ready, 1)
                dve.tensor_copy(turned[:, :, 1:2], pairs[:, :, 0:1]).then_inc(rot_ready, 1)

            def step(half, p, one, two):
                t = 2 * half + p
                u = t - 1
                q = 1 - p
                if one:
                    if not is_step(t, 0, 1):
                        dve.wait_ge(r_ready, t - 1)
                        dve.wait_ge(x1_turned, t - 1)
                    for i in range(G):
                        b = G * t + i
                        last = dve.tensor_scalar(x1[p][:, i, :], r_all[:, bass.ds(b, 1), :].rearrange("p o d -> p (o d)"),
                                                 norm["mean"][:, bass.ds(b, 1)], norm["rstd"][:, bass.ds(b, 1)], ALU.subtract, ALU.mult)
                    last.then_inc(x1_ready, 1)
                if two:
                    dve.wait_ge(scored, u + 1)
                    if not is_step(t, 1):
                        dve.wait_ge(out_done, u)
                    dve.tensor_tensor(sc[:, :, :], bank["score"][:, :].rearrange("p (g t) -> p g t", g=G), four(cst("decay")),
                                      ALU.mult).then_inc(decayed, 1)
                if one:
                    for n, (name, table, dst) in enumerate((("q", "qcos", q_cos), ("qr", "qsin", q_sin),
                                                            ("k", "kcos", k_cos), ("kr", "ksin", k_sin))):
                        dve.wait_ge(projected, 4 * t + n + 1)
                        if not is_step(t, 0):
                            dve.wait_ge(qh_ready if n < 2 else kh_ready, t)
                        dve.tensor_tensor(dst[:, :, :], bank[name][:, :].rearrange("p (g t) -> p g t", g=G), four(cst(table)),
                                          ALU.mult).then_inc(scaled, 1)
                if two:
                    dve.wait_ge(out_done, u + 1)
                    dve.wait_ge(x1_ready, u + 1)
                    rb = r_all[:, bass.ds(G * u, G), :]
                    dve.tensor_tensor(rb, bank["out"][:, :].rearrange("p (g t) -> p g t", g=G), x1[q][:, :, :],
                                      ALU.add).then_inc(r_ready, 1)
                    dve.wait_ge(r_ready, u + 1)
                    dve.wait_ge(w_loaded, 48)
                    for i in range(G):
                        dve.bn_stats(stats[:, bass.ds(G * u + i, 1), :].rearrange("p o d -> p (o d)"),
                                     r_all[:, bass.ds(G * u + i, 1), :].rearrange("p o d -> p (o d)"))

            run_steps(dve, step, NG)


def gate_phase(nc, const, r_all, stats, top, place, tile_expert, w1b, Wg, bg, b1, sorted_x):
    with ExitStack() as ctx:
        def sb(name, shape):
            return ctx.enter_context(nc.sbuf_tensor(name, shape, F32))

        def sem(name):
            return ctx.enter_context(nc.semaphore(name))

        def cst(name):
            return const[:, CONST_AT[name][0]:CONST_AT[name][1]]

        wg, bg_rep = sb("wg", [P, E]), sb("bg_rep", [P, E])
        norm = {n: sb("g_" + n, [P, B]) for n in ("mean", "var", "dev", "rstd", "tmp")}
        x2 = [sb(f"x2_{i}", [P, G, D]) for i in range(2)]
        x2T = [sb(f"x2T_{i}", [P, G, P]) for i in range(2)]
        logits, ex, hot = (sb(n, [P, B, E]) for n in ("logits", "ex", "hot"))
        total, inv, index = (sb(n, [P, B]) for n in ("total", "inv", "index"))
        b1_rows = sb("b1_rows", [E * FT, P])
        count, upto_batch = sb("count", [P, B, E]), [sb(f"upto_batch{i}", [P, B, E]) for i in range(2)]
        is_full, tiles, by_expert = sb("is_full", [P, E, B]), sb("tiles", [P, E]), sb("by_expert", [P, E, E])
        tile_end, tile_start = sb("tile_end", [P, E]), sb("tile_start", [P, E])
        after, expert_f = sb("after", [P, NT, E - 1]), sb("expert_f", [P, NT])
        row_of, place_f = sb("row_of", [P, B, E]), sb("place_f", [P, B])
        b1_bank = ctx.enter_context(nc.psum_tensor("b1_bank", [P, BANK], F32))
        rank_bank = ctx.enter_context(nc.psum_tensor("rank_bank", [P, 2, B, E], F32))
        turn = [ctx.enter_context(nc.psum_tensor(f"g_turn{i}", [P, BANK], F32)) for i in range(2)]
        logit_bank = [ctx.enter_context(nc.psum_tensor(f"g_logit{i}", [P, BANK], F32)) for i in range(2)]

        w_loaded, dev_in, dev_out = sem("g_w_loaded"), sem("g_dev_in"), sem("g_dev_out")
        x2_ready, x2_turned, x2T_evac, x2_kept = sem("x2_ready"), sem("x2_turned"), sem("x2T_evac"), sem("x2_kept")
        gated, logit_ready = sem("gated"), sem("logit_ready")
        done, exp_done = sem("gate_done"), sem("gate_exp")
        b1_turned, b1_kept = sem("b1_turned"), sem("b1_kept")
        hot_ready, ranked, placed, scattered = sem("hot_ready"), sem("ranked"), sem("placed"), sem("scattered")
        block = ctx.enter_context(nc.Block())

        @block.sync
        def _(sp):
            sp.dma_start(wg[:, :], Wg).then_inc(w_loaded, 16)
            sp.dma_start(bg_rep[:, :], bg.rearrange("(o e) -> o e", o=1).to_broadcast([P, E])).then_inc(w_loaded, 16)
            sp.dma_start(b1_rows[:, :], b1.rearrange("e (f p) -> (e f) p", p=P)).then_inc(w_loaded, 16)

        @block.tensor
        def _(pe):
            pe.wait_ge(w_loaded, 48)
            pe.transpose(b1_bank[:, 0:E * FT], b1_rows[:, :], cst("ident")[0:E * FT, 0:E * FT]).then_inc(b1_turned, 1)

            def step(half, p, one, two):
                t = 2 * half + p
                u = t - 1
                q = 1 - p
                if one:
                    pe.wait_ge(x2_ready, t + 1)
                    if not is_step(t, 0, 1):
                        pe.wait_ge(x2T_evac, t - 1)
                    for i in range(G):
                        last = pe.transpose(turn[p][:, i * P:(i + 1) * P], x2[p][:, i, :], cst("ident"))
                    last.then_inc(x2_turned, 1)
                if two:
                    pe.wait_ge(x2T_evac, u + 1)
                    for i in range(G):
                        last = pe.matmul(logit_bank[q][:, i * E:(i + 1) * E], x2T[q][:, i, :], wg[:, :], start=True, stop=True)
                    last.then_inc(gated, 1)

            run_steps(pe, step, NG)
            pe.wait_ge(hot_ready, 1)
            flat = hot[:, :, :].rearrange("p b e -> p (b e)")
            pe.matmul(rank_bank[:, 0, :, :].rearrange("p b e -> p (b e)"), cst("below"), flat, start=True, stop=True)
            pe.matmul(rank_bank[:, 1, :, :].rearrange("p b e -> p (b e)"), cst("ones"), flat, start=True, stop=True).then_inc(ranked, 1)

        @block.scalar
        def _(act):
            norm_act(act, norm, dev_in, dev_out)

            def step(half, p, one, two):
                t = 2 * half + p
                if one:
                    act.wait_ge(x2_turned, t + 1)
                    if not is_step(t, 0, 1):
                        act.wait_ge(gated, t - 1)
                    act.activation(x2T[p][:, :, :], turn[p][:, :].rearrange("p (g t) -> p g t", g=G), ACT.Copy).then_inc(x2T_evac, 1)

            run_steps(act, step, NG)
            act.wait_ge(done, 2)
            act.activation(ex[:, :, :], logits[:, :, :], ACT.Exp).then_inc(exp_done, 1)

        @block.gpsimd
        def _(pool):
            def step(half, p, one, two):
                t = 2 * half + p
                if one:
                    pool.wait_ge(x2_ready, t + 1)
                    pool.tensor_copy(r_all[:, bass.ds(G * t, G), :], x2[p][:, :, :]).then_inc(x2_kept, 1)

            run_steps(pool, step, NG)
            pool.wait_ge(x2_kept, NG)
            pool.wait_ge(placed, 1)
            for b in range(B):
                pool.indirect_dma_start(sorted_x, bass.IndirectOffsetOnAxis(ap=place[:, b:b + 1], axis=0),
                                        r_all[:, b, :], None).then_inc(scattered, 16)
            pool.wait_ge(scattered, 16 * B)

        @block.vector
        def _(dve):
            norm_dve(dve, stats, norm, dev_in, dev_out)
            dve.wait_ge(w_loaded, 48)
            dve.wait_ge(b1_turned, 1)
            dve.tensor_copy(w1b[:, :, HID:], b1_bank[:, 0:E * FT].rearrange("p (e f) -> p e f", f=FT)).then_inc(b1_kept, 1)

            def step(half, p, one, two):
                t = 2 * half + p
                u = t - 1
                q = 1 - p
                if one:
                    if not is_step(t, 0, 1):
                        dve.wait_ge(x2_turned, t - 1)
                        dve.wait_ge(x2_kept, t - 1)
                    for i in range(G):
                        b = G * t + i
                        last = dve.tensor_scalar(x2[p][:, i, :], r_all[:, bass.ds(b, 1), :].rearrange("p o d -> p (o d)"),
                                                 norm["mean"][:, bass.ds(b, 1)], norm["rstd"][:, bass.ds(b, 1)], ALU.subtract, ALU.mult)
                    last.then_inc(x2_ready, 1)
                if two:
                    dve.wait_ge(gated, u + 1)
                    dve.tensor_tensor(logits[:, bass.ds(G * u, G), :], logit_bank[q][:, 0:G * E].rearrange("p (g e) -> p g e", e=E),
                                      bg_rep[:, :].unsqueeze(1).to_broadcast([P, G, E]), ALU.add).then_inc(logit_ready, 1)

            run_steps(dve, step, NG)

            def bc(t):
                return t[:, :].unsqueeze(2).to_broadcast([P, B, E])
            iota = cst("iota").unsqueeze(1).to_broadcast([P, B, E])
            dve.wait_ge(logit_ready, NG)
            dve.tensor_reduce(top[:, :], logits[:, :, :], X, ALU.max).then_inc(done, 1)
            dve.wait_ge(done, 1)
            dve.tensor_tensor(logits[:, :, :], logits[:, :, :], bc(top), ALU.subtract).then_inc(done, 1)
            dve.wait_ge(exp_done, 1)
            dve.tensor_reduce(total[:, :], ex[:, :, :], X, ALU.add).then_inc(done, 1)
            dve.wait_ge(done, 3)
            dve.reciprocal(inv[:, :], total[:, :]).then_inc(done, 1)
            dve.wait_ge(done, 4)
            dve.tensor_tensor(ex[:, :, :], ex[:, :, :], bc(inv), ALU.mult).then_inc(done, 1)
            dve.wait_ge(done, 5)
            dve.tensor_reduce(top[:, :], ex[:, :, :], X, ALU.max).then_inc(done, 1)
            dve.wait_ge(done, 6)
            dve.tensor_tensor(hot[:, :, :], ex[:, :, :], bc(top), ALU.is_equal).then_inc(done, 1)
            dve.wait_ge(done, 7)
            dve.tensor_scalar(hot[:, :, :], hot[:, :, :], -float(E), float(E), ALU.mult, ALU.add).then_inc(done, 1)
            dve.wait_ge(done, 8)
            dve.tensor_tensor(hot[:, :, :], hot[:, :, :], iota, ALU.add).then_inc(done, 1)
            dve.wait_ge(done, 9)
            dve.tensor_reduce(index[:, :], hot[:, :, :], X, ALU.min).then_inc(done, 1)
            dve.wait_ge(done, 10)
            dve.tensor_tensor(hot[:, :, :], bc(index), iota, ALU.is_equal).then_inc(hot_ready, 1)

            dve.wait_ge(ranked, 1)
            dve.tensor_copy(count[:, :, :], rank_bank[:, 1, :, :])
            dve.tensor_copy(upto_batch[0][:, :, :], rank_bank[:, 1, :, :]).then_inc(done, 1)
            n, shift, cur = 11, 1, 0
            while shift < B:
                a, z = upto_batch[cur], upto_batch[1 - cur]
                dve.wait_ge(done, n)
                dve.tensor_copy(z[:, 0:shift, :], a[:, 0:shift, :])
                dve.tensor_tensor(z[:, shift:, :], a[:, shift:, :], a[:, 0:B - shift, :], ALU.add).then_inc(done, 1)
                n, shift, cur = n + 1, 2 * shift, 1 - cur
            upto, spare = upto_batch[cur], upto_batch[1 - cur]
            dve.wait_ge(done, n)
            dve.tensor_tensor(is_full[:, :, :], upto[:, B - 1, :].unsqueeze(2).to_broadcast([P, E, B]),
                              cst("full").unsqueeze(1).to_broadcast([P, E, B]), ALU.is_gt).then_inc(done, 1)
            dve.tensor_tensor(spare[:, :, :], upto[:, :, :], count[:, :, :], ALU.subtract).then_inc(done, 1)
            dve.wait_ge(done, n + 1)
            dve.tensor_reduce(tiles[:, :], is_full[:, :, :], X, ALU.add).then_inc(done, 1)
            dve.wait_ge(done, n + 2)
            dve.tensor_tensor(row_of[:, :, :], spare[:, :, :], rank_bank[:, 0, :, :], ALU.add).then_inc(done, 1)
            dve.wait_ge(done, n + 3)
            dve.tensor_tensor(by_expert[:, :, :], tiles[:, :].unsqueeze(1).to_broadcast([P, E, E]),
                              cst("upto").rearrange("p (e f) -> p e f", f=E), ALU.mult).then_inc(done, 1)
            dve.wait_ge(done, n + 5)
            dve.tensor_reduce(tile_end[:, :], by_expert[:, :, :], X, ALU.add).then_inc(done, 1)
            dve.wait_ge(done, n + 6)
            dve.tensor_tensor(tile_start[:, :], tile_end[:, :], tiles[:, :], ALU.subtract).then_inc(done, 1)
            dve.tensor_tensor(after[:, :, :], cst("tile_at").unsqueeze(2).to_broadcast([P, NT, E - 1]),
                              tile_end[:, 0:E - 1].unsqueeze(1).to_broadcast([P, NT, E - 1]), ALU.is_ge).then_inc(done, 1)
            dve.wait_ge(done, n + 7)
            dve.scalar_tensor_tensor(row_of[:, :, :], tile_start[:, :].unsqueeze(1).to_broadcast([P, B, E]), float(P),
                                     row_of[:, :, :], ALU.mult, ALU.add).then_inc(done, 1)
            dve.wait_ge(done, n + 8)
            dve.tensor_reduce(expert_f[:, :], after[:, :, :], X, ALU.add).then_inc(done, 1)
            dve.wait_ge(done, n + 9)
            dve.tensor_tensor(row_of[:, :, :], row_of[:, :, :], hot[:, :, :], ALU.mult).then_inc(done, 1)
            dve.wait_ge(done, n + 11)
            dve.tensor_reduce(place_f[:, :], row_of[:, :, :], X, ALU.add).then_inc(done, 1)
            dve.tensor_copy(tile_expert[:, :], expert_f[:, :])
            dve.wait_ge(done, n + 12)
            dve.tensor_copy(place[:, :], place_f[:, :]).then_inc(placed, 1)


def expert_phase(nc, const, w1b, w2, b2r, tile_expert, sorted_x, sorted_y):
    with ExitStack() as ctx:
        def sb(name, shape):
            return ctx.enter_context(nc.sbuf_tensor(name, shape, F32))

        def sem(name):
            return ctx.enter_context(nc.semaphore(name))

        def two(name, shape):
            return [sb(f"{name}{i}", shape) for i in range(2)]

        def banks(name):
            return [ctx.enter_context(nc.psum_tensor(f"{name}{i}", [P, BANK], F32)) for i in range(2)]

        ident = const[:, CONST_AT["ident"][0]:CONST_AT["ident"][1]]
        xs = sb("xs", [P, NT + 1, D])
        x_cur, xT, w1_cur = two("e_x", [P, D]), two("e_xT", [P, P]), two("w1_cur", [P, HID + FT])
        hT, y = two("hT", [P, FT, P]), two("y", [P, D])
        turn_bank, y_bank = banks("e_turn"), banks("y_bank")
        h_bank = [banks("h_bank_a"), banks("h_bank_b")]
        cuts = (0, 3, 12, 24, NT)
        x_loaded = [sem(f"xs_loaded{i}") for i in range(len(cuts) - 1)]
        pad_done, x_staged, turned, xT_evac = sem("pad_done"), sem("e_x_staged"), sem("e_turned"), sem("e_xT_evac")
        w1_staged, hid, hid_done = sem("w1_staged"), sem("hid"), sem("hid_done")
        y_done, y_added = sem("y_done"), sem("y_added")
        stored = [sem(f"y_stored{i}") for i in range(2)]
        block = ctx.enter_context(nc.Block())

        def expert_of(eng, t):
            return eng.value_load(tile_expert[0:1, bass.ds(t, 1)], min_val=0, max_val=E - 1)

        @block.sync
        def _(sp):
            rows = sorted_x.rearrange("(t p) d -> p t d", p=P)
            for i, ready in enumerate(x_loaded):
                a, z = cuts[i], cuts[i + 1]
                sp.dma_start(xs[:, a:z, :], rows[:, a:z, :]).then_inc(ready, 16)
            out_rows = sorted_y.rearrange("(t p) d -> p t d", p=P)

            def step(half, p, one, two):
                if two:
                    u, q = 2 * half + p - 1, 1 - p
                    sp.wait_ge(y_added, u + 1)
                    sp.dma_start(out_rows[:, bass.ds(u, 1), :].rearrange("p o d -> p (o d)"), y[q][:, :]).then_inc(stored[q], 16)

            run_steps(sp, step, NT)
            sp.wait_ge(stored[0], 16 * ((NT + 1) // 2))
            sp.wait_ge(stored[1], 16 * (NT // 2))

        @block.gpsimd
        def _(pool):
            def stage(t, p):
                if not is_step(t, 0, 1):
                    pool.wait_ge(turned, t - 1)
                pool.tensor_copy(x_cur[p][:, :], xs[:, bass.ds(t, 1), :].rearrange("p o d -> p (o d)")).then_inc(x_staged, 1)

            pool.memset(xs[:, NT:NT + 1, :], 0.0).then_inc(pad_done, 1)
            pool.wait_ge(pad_done, 1)
            for ready in x_loaded:
                pool.wait_ge(ready, 16)
            stage(0, 0)

            def step(half, p, one, two):
                if one:
                    stage(2 * half + p + 1, 1 - p)

            run_steps(pool, step, NT)

        @block.tensor
        def _(pe):
            def turn(t, p):
                pe.wait_ge(x_staged, t + 1)
                if not is_step(t, 0, 1):
                    pe.wait_ge(xT_evac, t - 1)
                pe.transpose(turn_bank[p][:, 0:P], x_cur[p][:, :], ident).then_inc(turned, 1)

            turn(0, 0)

            def step(half, p, one, two):
                t = 2 * half + p
                u, q = t - 1, 1 - p
                if one:
                    pe.wait_ge(w1_staged, t + 1)
                    pe.wait_ge(xT_evac, t + 1)
                    if not is_step(t, 0, 1):
                        pe.wait_ge(hid_done, FT * (t - 1))
                    for part in range(2):
                        for f in range(FT // 2 * part, FT // 2 * (part + 1)):
                            last = pe.matmul(h_bank[p][part][:, f * P:(f + 1) * P], w1_cur[p][:, f * P:(f + 1) * P], xT[p][:, :],
                                             start=True, stop=True)
                        last.then_inc(hid, 1)
                    turn(t + 1, 1 - p)
                if two:
                    e = expert_of(pe, u)
                    pe.wait_ge(hid_done, FT * (u + 1))
                    if not one:
                        pe.wait_ge(y_added, u - 1)
                    for f in range(FT):
                        last = pe.matmul(y_bank[q][:, 0:D], hT[q][:, f, :],
                                         w2[:, bass.ds(e, 1), f, :].rearrange("p o d -> p (o d)"),
                                         start=(f == 0), stop=(f == FT - 1))
                    last.then_inc(y_done, 1)

            run_steps(pe, step, NT)

        @block.scalar
        def _(act):
            def step(half, p, one, two):
                t = 2 * half + p
                if one:
                    for f in range(FT):
                        part = f // (FT // 2)
                        if f % (FT // 2) == 0:
                            act.wait_ge(hid, 2 * t + part + 1)
                        if f == 0 and not is_step(t, 0, 1):
                            act.wait_ge(y_done, t - 1)
                        act.activation(hT[p][:, f, :], h_bank[p][part][:, f * P:(f + 1) * P], ACT.Silu,
                                       bias=w1_cur[p][:, HID + f:HID + f + 1]).then_inc(hid_done, 1)

            run_steps(act, step, NT)

        @block.vector
        def _(dve):
            def stage(t, p):
                e = expert_of(dve, t)
                if not is_step(t, 0, 1):
                    dve.wait_ge(hid_done, FT * (t - 1))
                dve.tensor_copy(w1_cur[p][:, :], w1b[:, bass.ds(e, 1), :].rearrange("p o d -> p (o d)")).then_inc(w1_staged, 1)

            def evac(t, p):
                dve.wait_ge(turned, t + 1)
                dve.tensor_copy(xT[p][:, :], turn_bank[p][:, 0:P]).then_inc(xT_evac, 1)

            stage(0, 0)
            evac(0, 0)

            def step(half, p, one, two):
                t = 2 * half + p
                u, q = t - 1, 1 - p
                if one:
                    if not is_step(t, NT - 1):
                        stage(t + 1, 1 - p)
                    evac(t + 1, 1 - p)
                if two:
                    e = expert_of(dve, u)
                    dve.wait_ge(y_done, u + 1)
                    if not is_step(t, 1, 2):
                        dve.wait_ge(stored[q], 16 * (half if p == 1 else half - 1))
                    dve.tensor_tensor(y[q][:, :], y_bank[q][:, 0:D], b2r[:, bass.ds(e, 1), :].rearrange("p o d -> p (o d)"),
                                      ALU.add).then_inc(y_added, 1)

            run_steps(dve, step, NT, peeled=2)


def finish_phase(nc, r_all, stats, top, place, sorted_y, out):
    with ExitStack() as ctx:
        def sb(name, shape):
            return ctx.enter_context(nc.sbuf_tensor(name, shape, F32))

        def sem(name):
            return ctx.enter_context(nc.semaphore(name))

        y_tok = sb("y_tok", [P, B, D])
        norm = {n: sb("o_" + n, [P, B]) for n in ("mean", "var", "dev", "rstd", "tmp")}
        o = [sb(f"o_{i}", [P, G, D]) for i in range(2)]
        gathered = [sem(f"gathered{g}") for g in range(NG)]
        added, stats_done, dev_in, dev_out, o_ready = sem("f_added"), sem("f_stats"), sem("f_dev_in"), sem("f_dev_out"), sem("o_ready")
        stored = [sem(f"o_stored{i}") for i in range(2)]
        block = ctx.enter_context(nc.Block())

        @block.gpsimd
        def _(pool):
            for b in range(B):
                pool.indirect_dma_start(y_tok[:, b, :], None, sorted_y,
                                        bass.IndirectOffsetOnAxis(ap=place[:, b:b + 1], axis=0)).then_inc(gathered[b // G], 16)

        @block.sync
        def _(sp):
            for g in range(NG):
                sp.wait_ge(o_ready, g + 1)
                sp.dma_start(out[G * g:G * g + G].rearrange("b p d -> p b d"), o[g % 2][:, :, :]).then_inc(stored[g % 2], 16)
            for i in range(2):
                sp.wait_ge(stored[i], 16 * NG // 2)

        @block.scalar
        def _(act):
            norm_act(act, norm, dev_in, dev_out)

        @block.vector
        def _(dve):
            for g in range(NG):
                dve.wait_ge(gathered[g], 16 * G)
                for b in range(G * g, G * g + G):
                    last = dve.scalar_tensor_tensor(r_all[:, b, :], y_tok[:, b, :], top[:, b:b + 1], r_all[:, b, :], ALU.mult, ALU.add)
                last.then_inc(added, 1)
                dve.wait_ge(added, g + 1)
                for b in range(G * g, G * g + G):
                    last = dve.bn_stats(stats[:, b, :], r_all[:, b, :])
                last.then_inc(stats_done, 1)
            dve.wait_ge(stats_done, NG)
            norm_dve(dve, stats, norm, dev_in, dev_out)
            for g in range(NG):
                if g >= 2:
                    dve.wait_ge(stored[g % 2], 16 * (g // 2))
                for i in range(G):
                    b = G * g + i
                    last = dve.tensor_scalar(o[g % 2][:, i, :], r_all[:, b, :], norm["mean"][:, b:b + 1], norm["rstd"][:, b:b + 1],
                                             ALU.subtract, ALU.mult)
                last.then_inc(o_ready, 1)


def build(nc, x, context, Wq, Wk, Wv, Wo, betas, xWq, xWk, xWv, Wg, bg, W1, b1, W2, b2, consts, out):
    with ExitStack() as ctx:
        const = ctx.enter_context(nc.sbuf_tensor("const", [P, NCONST], F32))
        r_all = ctx.enter_context(nc.sbuf_tensor("r_all", [P, B, D], F32))
        stats = ctx.enter_context(nc.sbuf_tensor("stats", [P, B, 6], F32))
        scratch_qv = nc.dram_tensor("scratch_qv", (B, P, C, 3 * DK), F32, kind="Internal").ap()
        scratch_v = nc.dram_tensor("scratch_v", (B, P, C, DK), F32, kind="Internal").ap()
        sorted_x = nc.dram_tensor("sorted_x", (NT * P, D), F32, kind="Internal").ap()
        sorted_y = nc.dram_tensor("sorted_y", (NT * P, D), F32, kind="Internal").ap()
        attention_phase(nc, consts, const, r_all, stats, x, Wq, Wk, Wv, Wo, betas, scratch_qv, scratch_v)
        w1b = ctx.enter_context(nc.sbuf_tensor("w1b", [P, E, HID + FT], F32))
        w2 = ctx.enter_context(nc.sbuf_tensor("w2", [P, E, FT, D], F32))
        b2r = ctx.enter_context(nc.sbuf_tensor("b2r", [P, E, D], F32))
        top = ctx.enter_context(nc.sbuf_tensor("top", [P, B], F32))
        place = ctx.enter_context(nc.sbuf_tensor("place", [P, B], U32))
        tile_expert = ctx.enter_context(nc.sbuf_tensor("tile_expert", [P, NT], U32))
        preload = ((sorted_x.rearrange("(t p) d -> p t d", p=P), None),
                   (w1b[:, :, 0:HID], W1.rearrange("e d h -> d e h")),
                   (w2[:, :, :, :], W2.rearrange("e (f p) d -> p e f d", p=P)),
                   (b2r[:, :, :], b2.rearrange("(o e) d -> o e d", o=1).to_broadcast([P, E, D])))
        retention_phase(nc, const, r_all, stats, context, xWq, xWk, xWv, preload)
        gate_phase(nc, const, r_all, stats, top, place, tile_expert, w1b, Wg, bg, b1, sorted_x)
        expert_phase(nc, const, w1b, w2, b2r, tile_expert, sorted_x, sorted_y)
        finish_phase(nc, r_all, stats, top, place, sorted_y, out)


_NAMES = ["x", "ctx_1024", "L0_attn_Wq", "L0_attn_Wk", "L0_attn_Wv", "L0_attn_Wo", "L0_attn_betas",
          "L0_xattn_Wq", "L0_xattn_Wk", "L0_xattn_Wv", "L0_ffn_Wg", "L0_ffn_bg", "L0_ffn_W1", "L0_ffn_b1",
          "L0_ffn_W2", "L0_ffn_b2"]


def kernel(**inputs):
    import numpy as _np
    import concourse.bacc as _bacc
    from concourse import mybir as _mybir
    from concourse.bass_utils import run_bass_kernel_spmd as _run

    nc = _bacc.Bacc("TRN2", target_bir_lowering=False, num_devices=1)
    arrays, args = {}, []
    for name in _NAMES:
        a = _np.ascontiguousarray(inputs[name])
        arrays[f"in_{name}_dram"] = a
        args.append(nc.dram_tensor(f"in_{name}_dram", a.shape, _mybir.dt.from_np(a.dtype), kind="ExternalInput").ap())
    a = shape_constants()
    arrays["in_consts_dram"] = a
    args.append(nc.dram_tensor("in_consts_dram", a.shape, _mybir.dt.from_np(a.dtype), kind="ExternalInput").ap())
    args.append(nc.dram_tensor("out_0_dram", (B, P, D), F32, kind="ExternalOutput").ap())
    build(nc, *args)
    r = _run(nc, [arrays], core_ids=[0])
    return r.results[0]["out_0_dram"]
```

```python
from contextlib import ExitStack

import numpy as np
import concourse.bass as bass
from concourse import mybir

F32 = mybir.dt.float32
F32R = mybir.dt.float32r
U32 = mybir.dt.uint32
ALU = mybir.AluOpType
ACT = mybir.ActivationFunctionType
X = mybir.AxisListType.X

P = 128
B = 32
D = 128
H = 16
SEG = 2
L = 64
DK = 64
C = 16
J = L // H
HF = C * DK
BANK = 512
EPS = 1e-5
SM_SCALE = 1.0 / np.sqrt(DK)
E = 8
HID = 512
FT = HID // P
G = 4
NG = B // G
NT = B + E - 1


def shape_constants():
    ident = np.eye(P, dtype=np.float32)
    tok = np.arange(P)
    head, seg = (tok % L) // J, tok // L
    same = head[:, None] == head[None, :]
    both = same.astype(np.float32)
    first = (same & (seg[:, None] == 0)).astype(np.float32)
    half = D // 2
    scale_vec = (np.arange(0, D, 2, dtype=np.float32) + np.float32(0.4 * D)) / np.float32(1.4 * D)
    pos = np.arange(P, dtype=np.float32)
    scale = scale_vec[None, :] ** (pos / np.float32(512.0))[:, None]
    freqs = np.float32(1.0) / np.float32(10000.0) ** (np.arange(half, dtype=np.float32) / np.float32(half))
    ang = pos[:, None] * freqs[None, :]
    sin, cos = np.sin(ang), np.cos(ang)
    tabs = []
    for s in (scale, np.float32(1.0) / scale):
        for t in (cos, sin):
            tabs.append(np.repeat(t * s, 2, axis=-1).T)
    diff = pos[None, :] - pos[:, None]
    decay = np.where(diff >= 0, np.float32(0.96875) ** np.maximum(diff, 0), 0.0)

    def row(values):
        return np.tile(np.asarray(values, np.float32).reshape(1, -1), (P, 1))

    iota = row(np.arange(E))
    below = (tok[:, None] < tok[None, :]).astype(np.float32)
    ones = np.ones((P, P), np.float32)
    upto = row(np.arange(E)[None, :] <= np.arange(E)[:, None])
    tile_at = row(np.arange(NT))
    full = row(P * np.arange(B))
    token_row = tok[:, None] + P * np.arange(B)[None, :]
    spare_row = P * B + tok[:, None] + P * np.arange(NT)[None, :]
    cols = [ident, both, first] + tabs + [decay, iota, below, ones, upto, tile_at, full, token_row, spare_row]
    return np.ascontiguousarray(np.concatenate(cols, axis=1).astype(np.float32))


CONST_AT = {}
_at = 0
for _n, _w in (("ident", P), ("both", P), ("first", P), ("qcos", P), ("qsin", P), ("kcos", P), ("ksin", P),
               ("decay", P), ("iota", E), ("below", P), ("ones", P), ("upto", E * E),
               ("tile_at", NT), ("full", B), ("token_row", B), ("spare_row", NT)):
    CONST_AT[_n] = (_at, _at + _w)
    _at += _w
NCONST = _at


def run_steps(eng, step, n, peeled=1):
    for i in range(peeled):
        step(i, 0, True, i > 0)
        step(i, 1, True, True)
    with eng.Fori(peeled, n // 2) as i:
        step(i, 0, True, True)
        step(i, 1, True, True)
    if n % 2:
        step(n // 2, 0, True, True)
    step(n // 2, n % 2, False, True)


def is_step(t, *values):
    return isinstance(t, int) and t in values


def norm_act(act, n, ready, sq_ready):
    act.wait_ge(ready, 3)
    act.activation(n["dev"][:, :], n["var"][:, :], ACT.Sqrt).then_inc(sq_ready, 1)


def norm_dve(dve, stats, n, ready, sq_ready):
    mean, var, rstd, tmp = (n[k][:, :] for k in ("mean", "var", "rstd", "tmp"))

    def col(c):
        return stats[:, :, c:c + 1].rearrange("p b o -> p (b o)")

    dve.tensor_tensor(mean, col(1), col(4), ALU.add)
    dve.tensor_tensor(tmp, col(1), col(4), ALU.subtract)
    dve.tensor_tensor(var, col(2), col(5), ALU.add).then_inc(ready, 1)
    dve.wait_ge(ready, 1)
    dve.tensor_scalar(mean, mean, 0.5, None, ALU.mult)
    dve.tensor_scalar(var, var, 1.0 / D, EPS, ALU.mult, ALU.add)
    dve.scalar_tensor_tensor(rstd, tmp, 0.25, tmp, ALU.mult, ALU.mult).then_inc(ready, 1)
    dve.wait_ge(ready, 2)
    dve.tensor_tensor(var, var, rstd, ALU.add).then_inc(ready, 1)
    dve.wait_ge(sq_ready, 1)
    dve.reciprocal(rstd, n["dev"][:, :]).then_inc(ready, 1)
    dve.wait_ge(ready, 4)
    dve.tensor_tensor(tmp, rstd, rstd, ALU.mult).then_inc(ready, 1)
    dve.wait_ge(ready, 5)
    dve.tensor_tensor(tmp, tmp, var, ALU.mult).then_inc(ready, 1)
    dve.wait_ge(ready, 6)
    dve.tensor_scalar(tmp, tmp, -0.5, 1.5, ALU.mult, ALU.add).then_inc(ready, 1)
    dve.wait_ge(ready, 7)
    dve.tensor_tensor(rstd, rstd, tmp, ALU.mult).then_inc(ready, 1)
    dve.wait_ge(ready, 8)


def attention_phase(nc, consts, const, r_all, stats, x, Wq, Wk, Wv, Wo, betas, scratch_qv, scratch_z):
    with ExitStack() as ctx:
        def sb(name, shape):
            return ctx.enter_context(nc.sbuf_tensor(name, shape, F32))

        def sem(name):
            return ctx.enter_context(nc.semaphore(name))

        def cst(name):
            return const[:, CONST_AT[name][0]:CONST_AT[name][1]]

        w_k, w_q, w_v = (ctx.enter_context(nc.sbuf_tensor(n, [P, 2, HF], F32R)) for n in ("w_k", "w_q", "w_v"))
        w_o = sb("w_o", [P, C // 2, D])
        xT = ctx.enter_context(nc.sbuf_tensor("xT", [P, B + 1, 2, P], F32R))
        x_cur = [ctx.enter_context(nc.sbuf_tensor(f"x_cur{i}", [P, 2, P], F32R)) for i in range(2)]
        gate = sb("gate", [L, DK])
        ungate = sb("ungate", [P, H, DK])
        qk_tok = sb("qk_tok", [P, C, 2 * DK])
        e_qk = sb("e_qk", [P, C, 2 * DK])
        qv_out = sb("qv_out", [P, C, 2 * DK])
        k_sum = sb("k_sum", [P, DK])
        z = sb("z", [L, 2, DK])
        zg = sb("zg", [L, 2, DK])
        zg_all = sb("zg_all", [P, H, 2, DK])
        qT = sb("qT", [DK, P, C])
        kT = sb("kT", [DK, P, C])
        s_max = sb("s_max", [P, H])
        s_exp = sb("s_exp", [P, H, L])
        row_sum = sb("row_sum", [P, H])
        row_rec = sb("row_rec", [P, H])
        sq_sum = sb("sq_sum", [P, H])
        sq_rec = sb("sq_rec", [P, H])
        ps = sb("ps", [P, H, 2 * DK])
        psT = sb("psT", [P, H, P])
        pos_qv = [sb(f"pos_qv{i}", [P, H, 2 * DK]) for i in range(2)]
        lhs = sb("lhs", [P, SEG, H, DK])
        attT = sb("attT", [P, C // 2, P])
        raw = [psT[:, 0:HF // P, :], psT[:, HF // P:2 * HF // P, :], attT[:, :, :]]
        banks = [ctx.enter_context(nc.psum_tensor(f"bank{i}", [P, BANK], F32)) for i in range(8)]
        proj_bank, turn_bank, score_bank, mix_bank = banks[0:2], banks[2:4], banks[4:6], banks[6:8]
        qk_bank = turn_bank + score_bank

        XL = 4
        x_loaded = [sem(f"x_loaded{i}") for i in range(XL)]
        ident_loaded, const_loaded = sem("ident_loaded"), sem("const_loaded")
        wk_loaded, wq_loaded, wv_loaded, wo_loaded = (sem(n) for n in ("wk_loaded", "wq_loaded", "wv_loaded", "wo_loaded"))
        beta_loaded = sem("beta_loaded")
        xt_ready, xt_evac, xt_low, w_split = sem("xt_ready"), sem("xt_evac"), sem("xt_low"), sem("w_split")
        tanh_ready, gate_ready = sem("tanh_ready"), sem("gate_ready")
        x_pad, x_staged = sem("x_pad"), sem("x_staged")
        k_proj, q_proj, v_proj = sem("k_proj"), sem("q_proj"), sem("v_proj")
        k_evac, q_evac, v_evac = sem("k_evac"), sem("q_evac"), sem("v_evac")
        exp_cut, sk_ready, sq_ready, k_summed = sem("exp_cut"), sem("sk_ready"), sem("sq_ready"), sem("k_summed")
        zc_ready, z_rec, z_ready = sem("zc_ready"), sem("z_rec"), sem("z_ready")
        stored_qv, stored_z, z_loaded = sem("stored_qv"), sem("stored_z"), sem("z_loaded")
        qv_loaded = [sem(f"qv_loaded{i}") for i in range(2)]
        v_ready = sem("v_ready")
        turned, qT_evac = sem("turned"), sem("qT_evac")
        kT_early, kT_late = sem("kT_early"), sem("kT_late")
        scored, maxed, shifted, exped = sem("scored"), sem("maxed"), sem("shifted"), sem("exped")
        row_summed, row_inv, p_ready = sem("row_summed"), sem("row_inv"), sem("p_ready")
        sq_summed, sq_inv, sqn_ready = sem("sq_summed"), sem("sq_inv"), sem("sqn_ready")
        ps_turned, psT_evac = sem("ps_turned"), sem("psT_evac")
        mem_ready, mem_evac = sem("mem_ready"), sem("mem_evac")
        att_ready, att_evac = sem("att_ready"), sem("att_evac")
        out_ready, res_ready = sem("out_ready"), sem("res_ready")

        block = ctx.enter_context(nc.Block())

        @block.sync
        def _(sp):
            ident = slice(*CONST_AT["ident"])
            rest = slice(CONST_AT["ident"][1], NCONST)
            sp.dma_start(const[:, ident], consts[:, ident]).then_inc(ident_loaded, 16)
            for i in range(XL):
                b = slice(i * B // XL, (i + 1) * B // XL)
                sp.dma_start(r_all[:, b, :], x[b].rearrange("b p d -> p b d")).then_inc(x_loaded[i], 16)
            for dst, w, ready in zip(raw, (Wk, Wq, Wv), (wk_loaded, wq_loaded, wv_loaded)):
                sp.dma_start(dst, w.rearrange("d (a b) -> d a b", b=P)).then_inc(ready, 16)
            sp.dma_start(const[:, rest], consts[:, rest]).then_inc(const_loaded, 16)
            sp.dma_start(w_o[:, :, :], Wo.rearrange("(c p) m -> p c m", p=P)).then_inc(wo_loaded, 16)

            def step(half, p, one, two):
                if not one:
                    return
                t = 2 * half + p
                sp.wait_ge(v_evac, t + 1)
                sp.wait_ge(sq_ready, t + 1)
                sp.dma_start(scratch_qv[bass.ds(t, 1)].rearrange("o p c e -> (o p) c e"), qv_out[:, :, :]).then_inc(stored_qv, 16)
                sp.wait_ge(stored_qv, 16 * (t + 1))
                for n in range(SEG):
                    src = scratch_qv[bass.ds(t, 1), n * L:(n + 1) * L]
                    sp.dma_start(pos_qv[p][n * L:(n + 1) * L, :, :],
                                 src.rearrange("o (h j) c e -> (o j c) h e", j=J)).then_inc(qv_loaded[p], 16)
                sp.wait_ge(z_ready, t + 1)
                sp.dma_start(scratch_z[bass.ds(t, 1)].rearrange("o h n v -> (o h) n v"), zg[0:L:J, :, :]).then_inc(stored_z, 16)
                if two:
                    sp.wait_ge(mem_evac, 4 * t)
                sp.wait_ge(stored_z, 16 * (t + 1))
                sp.dma_start(zg_all[L:, :, :, :], scratch_z[bass.ds(t, 1)].to_broadcast([L, H, 2, DK])).then_inc(z_loaded, 16)

            run_steps(sp, step, B)

        @block.gpsimd
        def _(pool):
            for j in range(J):
                pool.dma_start(gate[j:L:J, :], betas.rearrange("o h q v -> (o h) (q v)")).then_inc(beta_loaded, 16)
            pool.dma_start(ungate[:, :, :], betas.rearrange("o h q v -> (o q) h v").to_broadcast([P, H, DK])).then_inc(beta_loaded, 16)

            def stage_x(t, p):
                if not is_step(t, 0, 1):
                    pool.wait_ge(v_proj, 2 * (t - 1))
                pool.tensor_copy(x_cur[p][:, :, :], xT[:, bass.ds(t, 1), :, :].rearrange("p o a c -> p (o a) c")).then_inc(x_staged, 1)

            pool.memset(xT[:, B:B + 1, :, :].bitcast(F32), 0.0).then_inc(x_pad, 1)
            pool.wait_ge(x_pad, 1)
            pool.wait_ge(xt_low, B // 4)
            stage_x(0, 0)

            def step(half, p, one, two):
                t = 2 * half + p
                if one:
                    stage_x(t + 1, 1 - p)
                if two:
                    q = 1 - p
                    u = t - 1
                    pool.wait_ge(sq_inv, t)
                    if not is_step(u, 0):
                        pool.wait_ge(ps_turned, 4 * u)
                    pool.tensor_tensor(ps[:, :, DK:], pos_qv[q][:, :, 0:DK],
                                       sq_rec[:, :].unsqueeze(2).to_broadcast([P, H, DK]), ALU.mult).then_inc(sqn_ready, 1)
                    if is_step(u, 0):
                        pool.wait_ge(gate_ready, 2)
                    if not is_step(u, 0):
                        pool.wait_ge(att_ready, 4 * u)
                    pool.wait_ge(sqn_ready, t)
                    for n in range(SEG):
                        s = slice(n * L, (n + 1) * L)
                        pool.tensor_tensor(lhs[0:L, 1 - n, :, :], pos_qv[q][s, :, DK:], ungate[s, :, :], ALU.mult).then_inc(v_ready, 1)
                        pool.wait_ge(v_ready, 2 * u + n + 1)
                if one:
                    for hh in range(2):
                        pool.wait_ge(row_inv, 2 * t + hh + 1)
                        if hh == 0 and not is_step(t, 0):
                            pool.wait_ge(ps_turned, 4 * t)
                        s = slice(8 * hh, 8 * hh + 8)
                        pool.tensor_tensor(ps[:, s, 0:DK], s_exp[:, s, :],
                                           row_rec[:, s].unsqueeze(2).to_broadcast([P, 8, L]), ALU.mult).then_inc(p_ready, 1)

            run_steps(pool, step, B)

        @block.tensor
        def _(pe):
            pe.wait_ge(ident_loaded, 16)
            for g in range(B // 4):
                if 4 * g % (B // XL) == 0:
                    pe.wait_ge(x_loaded[4 * g // (B // XL)], 16)
                for i in range(4):
                    last = pe.transpose(banks[g][:, i * P:(i + 1) * P], r_all[:, 4 * g + i, :], cst("ident"))
                last.then_inc(xt_ready, 1)

            def attend(w, f):
                n, hh = f // 2, f % 2
                if f == 0:
                    pe.wait_ge(v_ready, 2 * w + 2)
                    pe.wait_ge(psT_evac, 4 * w + 4)
                    pe.wait_ge(mem_evac, 4 * w + 4)
                if f >= 2:
                    pe.wait_ge(att_evac, 4 * w + f - 1)
                for i in range(8):
                    h = 8 * hh + i
                    last = pe.matmul(mix_bank[f % 2][0:DK, i * L:(i + 1) * L], lhs[:, 1 - n, h, :],
                                     psT[:, h, n * L:(n + 1) * L], start=True, stop=True)
                last.then_inc(att_ready, 1)

            def output(w):
                pe.wait_ge(att_evac, 4 * w + 4)
                for c in range(C // 2):
                    last = pe.matmul(proj_bank[1][:, 0:D], attT[:, c, :], w_o[:, c, :], start=(c == 0), stop=(c == C // 2 - 1))
                last.then_inc(out_ready, 1)

            def step(half, p, one, two):
                t = 2 * half + p
                u = t - 1
                q = 1 - p
                hq = half if p == 1 else half - 1
                three = not is_step(t, 0, 1)

                def project(bank, w, hh, done):
                    for i, (a, b) in enumerate(((0, 0), (0, 1), (1, 0))):
                        last = pe.matmul(bank[hh][:, :], x_cur[p][:, a, :], w[:, b, hh * BANK:(hh + 1) * BANK],
                                         start=(i == 0), stop=(i == 2))
                    last.then_inc(done, 1)

                def turn_qk(f):
                    if f >= 2 and not is_step(t, 0):
                        pe.wait_ge(shifted, 2 * t - 3 + f)
                    if f == 0:
                        pe.wait_ge(q_evac, 2 * t + 2)
                    for i in range(4):
                        last = pe.transpose(qk_bank[f][:, i * P:(i + 1) * P], qk_tok[:, 4 * f + i, :], cst("ident"))
                    last.then_inc(turned, 1)

                def turn_ps(f):
                    if f >= 2:
                        pe.wait_ge(psT_evac, 4 * u + f - 1)
                    elif one:
                        pe.wait_ge(qT_evac, 4 * t + f + 1)
                        pe.wait_ge(kT_early, 2 * t + f + 1)
                    else:
                        pe.wait_ge(psT_evac, 4 * u + f - 1)
                    if f == 0:
                        pe.wait_ge(sqn_ready, t)
                    if f % 2 == 0:
                        pe.wait_ge(p_ready, 2 * u + f // 2 + 1)
                    for i in range(4):
                        last = pe.transpose(turn_bank[f % 2][:, i * P:(i + 1) * P], ps[:, 4 * f + i, :], cst("ident"))
                    last.then_inc(ps_turned, 1)

                def remember(f):
                    if f == 0:
                        pe.wait_ge(qv_loaded[q], 32 * (hq + 1))
                        if not is_step(u, 0):
                            pe.wait_ge(att_evac, 4 * u - 1)
                    elif f == 1:
                        if not is_step(u, 0):
                            pe.wait_ge(att_evac, 4 * u)
                    else:
                        pe.wait_ge(mem_evac, 4 * u + f - 1)
                    for i in range(4):
                        for n, k in ((0, P), (1, L)):
                            at = (2 * i + n) * DK
                            last = pe.matmul(mix_bank[f % 2][DK:, at:at + DK], pos_qv[q][0:k, 4 * f + i, 0:DK],
                                             pos_qv[q][0:k, 4 * f + i, DK:], start=True, stop=True)
                    last.then_inc(mem_ready, 1)

                def score(hh):
                    if hh == 0:
                        pe.wait_ge(qT_evac, 4 * t + 4)
                        pe.wait_ge(kT_early, 2 * t + 2)
                        pe.wait_ge(kT_late, 2 * t + 2)
                    for i in range(8):
                        if i == 0:
                            tok = J * 8 * hh
                            pe.matmul(score_bank[hh][:, 0:L], qT[:, tok:tok + 2 * J, :], kT[:, tok:tok + J, :],
                                      start=True, stop=True)
                        for n in range(1 if i == 0 else 0, SEG):
                            tok = n * L + J * (8 * hh + i)
                            last = pe.matmul(score_bank[hh][n * L:(n + 1) * L, i * L:(i + 1) * L],
                                             qT[:, tok:tok + J, :], kT[:, tok:tok + J, :], start=True, stop=True)
                    last.then_inc(scored, 1)

                if one:
                    pe.wait_ge(x_staged, t + 1)
                    if not is_step(t, 0):
                        pe.wait_ge(z_rec, t)
                    if is_step(t, 0):
                        pe.wait_ge(w_split, 2)
                    project(proj_bank, w_k, 0, k_proj)
                    if not is_step(t, 0):
                        pe.wait_ge(v_evac, t)
                    project(proj_bank, w_k, 1, k_proj)
                if three:
                    attend(t - 2, 0)
                for hh in range(2):
                    if is_step(t, 0):
                        pe.wait_ge(w_split, 4)
                    if one:
                        if is_step(t, 1):
                            pe.wait_ge(qT_evac, hh + 1)
                            pe.wait_ge(kT_early, hh + 1)
                        elif not is_step(t, 0):
                            pe.wait_ge(psT_evac, 4 * t - 5 + hh)
                        project(turn_bank, w_q, hh, q_proj)
                    if three and hh == 1:
                        attend(t - 2, 1)
                for hh in range(2):
                    if is_step(t, 0):
                        pe.wait_ge(w_split, 6)
                    if one:
                        pe.wait_ge(k_evac, 2 * t + hh + 1)
                        project(proj_bank, w_v, hh, v_proj)
                    if three:
                        attend(t - 2, 2 + hh)
                if one:
                    for f in range(4):
                        turn_qk(f)
                if three:
                    if one:
                        pe.wait_ge(v_evac, t + 1)
                    else:
                        pe.wait_ge(res_ready, t - 2)
                    output(t - 2)
                if one:
                    if is_step(t, 0):
                        pe.wait_ge(const_loaded, 16)
                        pe.wait_ge(wo_loaded, 16)
                    pe.wait_ge(k_summed, t + 1)
                    pe.wait_ge(v_evac, t + 1)
                    pe.matmul(proj_bank[0][:, 0:DK], cst("both"), k_sum[:, :], start=True, stop=True)
                    pe.matmul(proj_bank[0][:, DK:2 * DK], cst("first"), k_sum[:, :], start=True, stop=True).then_inc(zc_ready, 1)
                if two:
                    turn_ps(0)
                    turn_ps(1)
                    remember(0)
                    remember(1)
                if one:
                    score(0)
                if two:
                    turn_ps(2)
                    turn_ps(3)
                    remember(2)
                    remember(3)
                if one:
                    score(1)

            run_steps(pe, step, B)
            for f in range(4):
                attend(B - 1, f)
            pe.wait_ge(res_ready, B - 1)
            output(B - 1)

        @block.scalar
        def _(act):
            for g in range(B // 4):
                act.wait_ge(xt_ready, g + 1)
                act.activation(xT[:, 4 * g:4 * g + 4, 0, :], banks[g][:, :].rearrange("p (b c) -> p b c", b=4), ACT.Copy).then_inc(xt_evac, 1)

            def exp_scores(b, hh):
                act.wait_ge(shifted, 2 * b + hh + 1)
                s = slice(8 * hh, 8 * hh + 8)
                act.activation(s_exp[:, s, :], s_exp[:, s, :], ACT.Exp, scale=float(SM_SCALE)).then_inc(exped, 1)

            def evac_att(w, f):
                n, hh = f // 2, f % 2
                act.wait_ge(att_ready, 4 * w + f + 1)
                at = n * L + hh * 32
                src = mix_bank[f % 2][0:DK, :].rearrange("p (t c two) -> p two c t", c=C // 2, two=2)
                for odd in range(2):
                    last = act.activation(attT[odd * DK:(odd + 1) * DK, :, at:at + 32], src[:, odd, :, :], ACT.Copy)
                last.then_inc(att_evac, 1)

            def step(half, p, one, two):
                t = 2 * half + p
                u = t - 1
                three = not is_step(t, 0, 1)

                def evac_qk(slot, hh):
                    proj, evac = ((q_proj, q_evac), (k_proj, k_evac))[slot]
                    bank = (turn_bank, proj_bank)[slot][hh][:, :].rearrange("p (c k) -> p c k", c=8)
                    s = slice(slot * DK, (slot + 1) * DK)
                    c = slice(8 * hh, 8 * hh + 8)
                    act.wait_ge(proj, 2 * t + hh + 1)
                    if hh == 0 and slot == 1 and not is_step(t, 0):
                        act.wait_ge(turned, 4 * t)
                        act.wait_ge(sq_ready, t)
                        act.wait_ge(k_summed, t)
                    act.activation(e_qk[:, c, s], bank, ACT.Exp)
                    act.activation(qk_tok[:, c, s], bank, ACT.Copy).then_inc(evac, 1)

                if one:
                    evac_qk(1, 0)
                if two:
                    exp_scores(t - 1, 1)
                if one:
                    evac_qk(1, 1)
                if three:
                    if not one:
                        act.wait_ge(out_ready, t - 2)
                    evac_att(t - 2, 0)
                for hh in range(2):
                    if one:
                        evac_qk(0, hh)
                    if three and hh == 1:
                        evac_att(t - 2, 1)
                for hh in range(2):
                    if one:
                        act.wait_ge(v_proj, 2 * t + hh + 1)
                        if hh == 0 and not is_step(t, 0):
                            act.wait_ge(stored_qv, 16 * t)
                        last = act.activation(qv_out[:, 8 * hh:8 * hh + 8, DK:], proj_bank[hh][:, :].rearrange("p (c k) -> p c k", c=8),
                                              ACT.Copy)
                        if hh == 1:
                            last.then_inc(v_evac, 1)
                    if three:
                        evac_att(t - 2, 2 + hh)
                if is_step(t, 0):
                    act.wait_ge(beta_loaded, 16 * (J + 1))
                    act.activation(gate[:, :], gate[:, :], ACT.Tanh, scale=0.5).then_inc(tanh_ready, 1)
                    act.activation(ungate[:, :, :], ungate[:, :, :], ACT.Tanh, scale=0.5).then_inc(tanh_ready, 1)
                if one:
                    for f in range(4):
                        act.wait_ge(turned, 4 * t + f + 1)
                        if f == 0 and not is_step(t, 0):
                            act.wait_ge(scored, 2 * t)
                        act.activation(qT[:, :, 4 * f:4 * f + 4],
                                       qk_bank[f][0:DK, :].rearrange("p (c s) -> p s c", c=4), ACT.Copy).then_inc(qT_evac, 1)
                        if f >= 2:
                            act.activation(kT[:, :, 4 * f:4 * f + 4],
                                           qk_bank[f][DK:, :].rearrange("p (c s) -> p s c", c=4), ACT.Copy).then_inc(kT_late, 1)
                if two:
                    for f in range(4):
                        act.wait_ge(ps_turned, 4 * u + f + 1)
                        if f == 0 and not is_step(u, 0):
                            act.wait_ge(att_ready, 4 * u)
                        act.activation(psT[:, 4 * f:4 * f + 4, :], turn_bank[f % 2][:, :].rearrange("p (h s) -> p h s", h=4),
                                       ACT.Copy).then_inc(psT_evac, 1)
                if one:
                    exp_scores(t, 0)

            run_steps(act, step, B)
            act.wait_ge(out_ready, B - 1)
            for f in range(4):
                evac_att(B - 1, f)

        @block.vector
        def _(dve):
            def split_w(i):
                w = (w_k, w_q, w_v)[i]
                flat = raw[i].rearrange("p a b -> p (a b)")
                dve.wait_ge((wk_loaded, wq_loaded, wv_loaded)[i], 16)
                dve.tensor_copy(w[:, 0, :], flat).then_inc(w_split, 1)
                dve.wait_ge(w_split, 2 * i + 1)
                dve.tensor_tensor(w[:, 1, :], flat, w[:, 0, :].bitcast(F32), ALU.subtract).then_inc(w_split, 1)

            for g in range(B // 4):
                dve.wait_ge(xt_evac, g + 1)
                dve.tensor_tensor(xT[:, 4 * g:4 * g + 4, 1, :], banks[g][:, :].rearrange("p (b c) -> p b c", b=4),
                                  xT[:, 4 * g:4 * g + 4, 0, :].bitcast(F32), ALU.subtract).then_inc(xt_low, 1)
            for i in range(3):
                split_w(i)

            def residual(b):
                dve.wait_ge(out_ready, b + 1)
                rb = r_all[:, bass.ds(b, 1), :].rearrange("p o d -> p (o d)")
                dve.tensor_tensor(rb, proj_bank[1][:, 0:D], rb, ALU.add).then_inc(res_ready, 1)
                dve.wait_ge(res_ready, b + 1)
                dve.wait_ge(gate_ready, 2)
                dve.bn_stats(stats[:, bass.ds(b, 1), :].rearrange("p o d -> p (o d)"), rb)

            def step(half, p, one, two):
                t = 2 * half + p
                u = t - 1
                q = 1 - p
                hq = half if p == 1 else half - 1

                def evac_k(f):
                    dve.wait_ge(turned, 4 * t + f + 1)
                    if f == 0 and not is_step(t, 0):
                        dve.wait_ge(scored, 2 * t)
                    dve.tensor_copy(kT[:, :, 4 * f:4 * f + 4],
                                    qk_bank[f][DK:, :].rearrange("p (c s) -> p s c", c=4)).then_inc(kT_early, 1)

                def evac_memory(f):
                    dve.wait_ge(mem_ready, 4 * u + f + 1)
                    if f == 0:
                        dve.wait_ge(z_loaded, 16 * t)
                        if not is_step(u, 0):
                            dve.wait_ge(att_ready, 4 * u)
                    s = slice(4 * f, 4 * f + 4)
                    dve.tensor_tensor(lhs[DK:, :, s, :].rearrange("p n h k -> p h n k"),
                                      mix_bank[f % 2][DK:, :].rearrange("p (h n k) -> p h n k", n=SEG, h=4),
                                      zg_all[L:, s, :, :], ALU.mult).then_inc(mem_evac, 1)

                if two:
                    dve.wait_ge(qv_loaded[q], 32 * (hq + 1))
                    if not is_step(u, 0):
                        dve.wait_ge(sqn_ready, u)
                    dve.tensor_reduce(sq_sum[:, :], pos_qv[q][:, :, 0:DK], X, ALU.add).then_inc(sq_summed, 1)
                    dve.wait_ge(sq_summed, t)
                    dve.reciprocal(sq_rec[:, :], sq_sum[:, :]).then_inc(sq_inv, 1)
                if one:
                    dve.wait_ge(k_evac, 2 * t + 2)
                    dve.tensor_scalar(e_qk[:, :, DK:], e_qk[:, :, DK:], 1.0, None, ALU.min).then_inc(exp_cut, 1)
                    dve.wait_ge(exp_cut, 2 * t + 1)
                    dve.scalar_tensor_tensor(e_qk[:, :, DK:], qk_tok[:, :, DK:], 1.0, e_qk[:, :, DK:],
                                             ALU.add, ALU.max).then_inc(sk_ready, 1)
                    dve.wait_ge(sk_ready, t + 1)
                    if not is_step(t, 0):
                        dve.wait_ge(zc_ready, t)
                    dve.tensor_reduce(k_sum[:, :], e_qk[:, :, DK:].rearrange("p c k -> p k c"), X, ALU.add).then_inc(k_summed, 1)
                if one:
                    dve.wait_ge(q_evac, 2 * t + 2)
                    dve.tensor_scalar(e_qk[:, :, 0:DK], e_qk[:, :, 0:DK], 1.0, None, ALU.min).then_inc(exp_cut, 1)
                    dve.wait_ge(exp_cut, 2 * t + 2)
                    if not is_step(t, 0):
                        dve.wait_ge(stored_qv, 16 * t)
                    if not is_step(t, 0, 1):
                        dve.wait_ge(v_ready, 2 * t - 2)
                    dve.scalar_tensor_tensor(qv_out[:, :, 0:DK], qk_tok[:, :, 0:DK], 1.0, e_qk[:, :, 0:DK],
                                             ALU.add, ALU.max).then_inc(sq_ready, 1)
                    evac_k(0)
                    evac_k(1)
                if not is_step(t, 0, 1):
                    residual(t - 2)
                if one:
                    if is_step(t, 0):
                        dve.wait_ge(tanh_ready, 2)
                        dve.tensor_scalar(ungate[:, :, :], ungate[:, :, :], -0.5, 0.5, ALU.mult, ALU.add).then_inc(gate_ready, 1)
                        dve.tensor_scalar(gate[:, :], gate[:, :], 0.5, 0.5, ALU.mult, ALU.add).then_inc(gate_ready, 1)
                        dve.wait_ge(gate_ready, 2)
                    dve.wait_ge(zc_ready, t + 1)
                    if not is_step(t, 0):
                        dve.wait_ge(z_ready, t)
                    dve.reciprocal(z[:, :, :], proj_bank[0][0:L, 0:2 * DK].rearrange("p (a k) -> p a k", a=2)).then_inc(z_rec, 1)
                    dve.wait_ge(z_rec, t + 1)
                    if not is_step(t, 0):
                        dve.wait_ge(stored_z, 16 * t)
                    dve.tensor_tensor(zg[:, :, :], z[:, :, :], gate[:, :].unsqueeze(1).to_broadcast([L, 2, DK]),
                                      ALU.mult).then_inc(z_ready, 1)
                if two:
                    evac_memory(0)
                    evac_memory(1)
                    evac_memory(2)
                    evac_memory(3)
                if one:
                    for hh in range(2):
                        s = slice(8 * hh, 8 * hh + 8)
                        bank = score_bank[hh][:, :].rearrange("p (h t) -> p h t", h=8)
                        dve.wait_ge(scored, 2 * t + hh + 1)
                        dve.tensor_reduce(s_max[:, s], bank, X, ALU.max).then_inc(maxed, 1)
                        dve.wait_ge(maxed, 2 * t + hh + 1)
                        if not is_step(t, 0):
                            dve.wait_ge(p_ready, 2 * t - 1 + hh)
                        dve.tensor_tensor(s_exp[:, s, :], bank, s_max[:, s].unsqueeze(2).to_broadcast([P, 8, L]),
                                          ALU.subtract).then_inc(shifted, 1)
                    for hh in range(2):
                        s = slice(8 * hh, 8 * hh + 8)
                        dve.wait_ge(exped, 2 * t + hh + 1)
                        dve.tensor_reduce(row_sum[:, s], s_exp[:, s, :], X, ALU.add).then_inc(row_summed, 1)
                        dve.wait_ge(row_summed, 2 * t + hh + 1)
                        dve.reciprocal(row_rec[:, s], row_sum[:, s]).then_inc(row_inv, 1)
            run_steps(dve, step, B)
            residual(B - 1)


def retention_phase(nc, const, r_all, stats, ctx_in, Wq, Wk, Wv, preload, sorted_x):
    with ExitStack() as ctx:
        def sb(name, shape):
            return ctx.enter_context(nc.sbuf_tensor(name, shape, F32))

        def sem(name):
            return ctx.enter_context(nc.semaphore(name))

        def cst(name):
            return const[:, CONST_AT[name][0]:CONST_AT[name][1]]

        def four(ap):
            return ap.unsqueeze(1).to_broadcast([P, G, P])

        wq, wk, wv = sb("r_wq", [P, D]), sb("r_wk", [P, D]), sb("r_wv", [P, D])
        wq_rot, wk_rot = sb("wq_rot", [P, D]), sb("wk_rot", [P, D])
        norm = {n: sb("r_" + n, [P, B]) for n in ("mean", "var", "dev", "rstd", "tmp")}
        x1 = [sb(f"x1_{i}", [P, G, D]) for i in range(2)]
        cx = [sb(f"cx_{i}", [P, G, D]) for i in range(2)]
        x1T, cxT = sb("x1T", [P, G, P]), sb("cxT", [P, G, P])
        q_cos, q_sin, k_cos, k_sin = (sb(n, [P, G, P]) for n in ("q_cos", "q_sin", "k_cos", "k_sin"))
        qh = [sb(f"qh{i}", [P, G, P]) for i in range(2)]
        kh = [sb(f"kh{i}", [P, G, P]) for i in range(2)]
        vh = [sb(f"vh{i}", [P, G, D]) for i in range(2)]
        sc = sb("sc", [P, G, P])
        padding = sb("padding", [P, NT, D + 1])
        names = ("x1t", "cxt", "q", "qr", "k", "kr", "score", "out")
        bank = {n: ctx.enter_context(nc.psum_tensor(f"r_{n}", [P, BANK], F32)) for n in names}

        w_loaded, rot_ready = sem("w_loaded"), sem("rot_ready")
        padded, preloaded = sem("padded"), sem("preloaded")
        dev_in, dev_out = sem("dev_in"), sem("dev_out")
        cx_loaded = [sem(f"cx_loaded{i}") for i in range(2)]
        x1_kept = sem("x1_kept")
        x1_ready, x1_turned, x1T_evac = sem("x1_ready"), sem("x1_turned"), sem("x1T_evac")
        cx_turned, cxT_evac = sem("cx_turned"), sem("cxT_evac")
        projected, scaled, qh_ready, kh_ready = sem("projected"), sem("scaled"), sem("qh_ready"), sem("kh_ready")
        v_done, v_evac = sem("v_done"), sem("rv_evac")
        scored, decayed = sem("r_scored"), sem("decayed")
        out_done, r_ready = sem("out_done"), sem("r_ready")
        block = ctx.enter_context(nc.Block())

        @block.sync
        def _(sp):
            sp.dma_start(wq[:, :], Wq).then_inc(w_loaded, 16)
            sp.dma_start(wk[:, :], Wk).then_inc(w_loaded, 16)
            sp.dma_start(wv[:, :], Wv).then_inc(w_loaded, 16)

            def step(half, p, one, two):
                t = 2 * half + p
                if one:
                    if not is_step(t, 0, 1):
                        sp.wait_ge(cx_turned, t - 1)
                    sp.dma_start(cx[p][:, :, :], ctx_in[bass.ds(G * t, G)].rearrange("b p d -> p b d")).then_inc(cx_loaded[p], 16)

            run_steps(sp, step, NG)
            for target, source in preload:
                sp.dma_start(target, source).then_inc(preloaded, 16)
            sp.wait_ge(padded, 2)
            sp.dma_start(sorted_x.rearrange("(t p) d -> p t d", p=P), padding[:, :, :]).then_inc(preloaded, 16)
            sp.wait_ge(preloaded, 16 * (len(preload) + 1))

        @block.gpsimd
        def _(pool):
            pool.memset(padding[:, :, :], 0.0).then_inc(padded, 1)
            pool.wait_ge(padded, 1)
            pool.tensor_copy(padding[:, :, D:].rearrange("p t o -> p (t o)"), cst("spare_row")).then_inc(padded, 1)

            def step(half, p, one, two):
                t = 2 * half + p
                if one:
                    pool.wait_ge(x1_ready, t + 1)
                    pool.tensor_copy(r_all[:, bass.ds(G * t, G), :], x1[p][:, :, :]).then_inc(x1_kept, 1)
                    pool.wait_ge(scaled, 4 * t + 2)
                    if not is_step(t, 0, 1):
                        pool.wait_ge(scored, t - 1)
                    pool.tensor_tensor(qh[p][:, :, :], q_cos[:, :, :], q_sin[:, :, :], ALU.add).then_inc(qh_ready, 1)
                    pool.wait_ge(scaled, 4 * t + 4)
                    pool.tensor_tensor(kh[p][:, :, :], k_cos[:, :, :], k_sin[:, :, :], ALU.add).then_inc(kh_ready, 1)

            run_steps(pool, step, NG)

        @block.tensor
        def _(pe):
            def step(half, p, one, two):
                t = 2 * half + p
                u = t - 1
                q = 1 - p
                hq = half if p == 1 else half - 1
                if one:
                    pe.wait_ge(cx_loaded[p], 16 * (half + 1))
                    if not is_step(t, 0):
                        pe.wait_ge(cxT_evac, t)
                    for i in range(G):
                        last = pe.transpose(bank["cxt"][:, i * P:(i + 1) * P], cx[p][:, i, :], cst("ident"))
                    last.then_inc(cx_turned, 1)
                    pe.wait_ge(x1_ready, t + 1)
                    if not is_step(t, 0):
                        pe.wait_ge(v_evac, t)
                    for i in range(G):
                        last = pe.transpose(bank["x1t"][:, i * P:(i + 1) * P], x1[p][:, i, :], cst("ident"))
                    last.then_inc(x1_turned, 1)
                if two:
                    pe.wait_ge(qh_ready, u + 1)
                    pe.wait_ge(kh_ready, u + 1)
                    if not is_step(t, 1):
                        pe.wait_ge(decayed, u)
                    for i in range(G):
                        last = pe.matmul(bank["score"][:, i * P:(i + 1) * P], kh[q][:, i, :], qh[q][:, i, :], start=True, stop=True)
                    last.then_inc(scored, 1)
                if one:
                    if is_step(t, 0):
                        pe.wait_ge(w_loaded, 48)
                        pe.wait_ge(rot_ready, 4)
                    pe.wait_ge(x1T_evac, t + 1)
                    for n, (name, w, src) in enumerate((("q", wq, x1T), ("qr", wq_rot, x1T), ("k", wk, cxT), ("kr", wk_rot, cxT))):
                        if n == 2:
                            pe.wait_ge(cxT_evac, t + 1)
                        if not is_step(t, 0):
                            pe.wait_ge(scaled, 4 * (t - 1) + n + 1)
                        pe.matmul(bank[name][:, :], w[:, :], src[:, :, :].rearrange("p g t -> p (g t)"),
                                  start=True, stop=True).then_inc(projected, 1)
                    for i in range(G):
                        last = pe.matmul(bank["x1t"][:, i * P:(i + 1) * P], cxT[:, i, :], wv[:, :], start=True, stop=True)
                    last.then_inc(v_done, 1)
                if two:
                    pe.wait_ge(decayed, u + 1)
                    pe.wait_ge(v_evac, u + 1)
                    if not is_step(t, 1):
                        pe.wait_ge(r_ready, u)
                    for i in range(G):
                        last = pe.matmul(bank["out"][:, i * P:(i + 1) * P], sc[:, i, :], vh[q][:, i, :], start=True, stop=True)
                    last.then_inc(out_done, 1)

            run_steps(pe, step, NG)

        @block.scalar
        def _(act):
            norm_act(act, norm, dev_in, dev_out)

            def step(half, p, one, two):
                t = 2 * half + p
                if one:
                    act.wait_ge(cx_turned, t + 1)
                    if not is_step(t, 0):
                        act.wait_ge(v_done, t)
                    act.activation(cxT[:, :, :], bank["cxt"][:, :].rearrange("p (g t) -> p g t", g=G), ACT.Copy).then_inc(cxT_evac, 1)
                    act.wait_ge(x1_turned, t + 1)
                    act.activation(x1T[:, :, :], bank["x1t"][:, :].rearrange("p (g t) -> p g t", g=G), ACT.Copy).then_inc(x1T_evac, 1)
                    act.wait_ge(v_done, t + 1)
                    if not is_step(t, 0, 1):
                        act.wait_ge(out_done, t - 1)
                    act.activation(vh[p][:, :, :], bank["x1t"][:, :].rearrange("p (g t) -> p g t", g=G), ACT.Copy).then_inc(v_evac, 1)

            run_steps(act, step, NG)

        @block.vector
        def _(dve):
            norm_dve(dve, stats, norm, dev_in, dev_out)
            dve.wait_ge(w_loaded, 48)
            for w, rot in ((wq, wq_rot), (wk, wk_rot)):
                pairs = w[:, :].rearrange("p (i two) -> p i two", two=2)
                turned = rot[:, :].rearrange("p (i two) -> p i two", two=2)
                dve.tensor_scalar(turned[:, :, 0:1], pairs[:, :, 1:2], -1.0, None, ALU.mult).then_inc(rot_ready, 1)
                dve.tensor_copy(turned[:, :, 1:2], pairs[:, :, 0:1]).then_inc(rot_ready, 1)

            def residual(w):
                dve.wait_ge(out_done, w + 1)
                dve.wait_ge(x1_kept, w + 1)
                rb = r_all[:, bass.ds(G * w, G), :]
                dve.tensor_tensor(rb, bank["out"][:, :].rearrange("p (g t) -> p g t", g=G), rb, ALU.add).then_inc(r_ready, 1)
                dve.wait_ge(r_ready, w + 1)
                dve.wait_ge(w_loaded, 48)
                for i in range(G):
                    dve.bn_stats(stats[:, bass.ds(G * w + i, 1), :].rearrange("p o d -> p (o d)"),
                                 r_all[:, bass.ds(G * w + i, 1), :].rearrange("p o d -> p (o d)"))

            def step(half, p, one, two):
                t = 2 * half + p
                u = t - 1
                if one:
                    if not is_step(t, 0, 1):
                        dve.wait_ge(x1_kept, t - 1)
                        dve.wait_ge(x1_turned, t - 1)
                    for i in range(G):
                        b = G * t + i
                        last = dve.tensor_scalar(x1[p][:, i, :], r_all[:, bass.ds(b, 1), :].rearrange("p o d -> p (o d)"),
                                                 norm["mean"][:, bass.ds(b, 1)], norm["rstd"][:, bass.ds(b, 1)], ALU.subtract, ALU.mult)
                    last.then_inc(x1_ready, 1)
                if not is_step(t, 0, 1):
                    residual(t - 2)
                if two:
                    dve.wait_ge(scored, u + 1)
                    if not is_step(t, 1):
                        dve.wait_ge(out_done, u)
                    dve.tensor_tensor(sc[:, :, :], bank["score"][:, :].rearrange("p (g t) -> p g t", g=G), four(cst("decay")),
                                      ALU.mult).then_inc(decayed, 1)
                if one:
                    for n, (name, table, dst) in enumerate((("q", "qcos", q_cos), ("qr", "qsin", q_sin),
                                                            ("k", "kcos", k_cos), ("kr", "ksin", k_sin))):
                        dve.wait_ge(projected, 4 * t + n + 1)
                        if not is_step(t, 0):
                            dve.wait_ge(qh_ready if n < 2 else kh_ready, t)
                        dve.tensor_tensor(dst[:, :, :], bank[name][:, :].rearrange("p (g t) -> p g t", g=G), four(cst(table)),
                                          ALU.mult).then_inc(scaled, 1)

            run_steps(dve, step, NG)
            residual(NG - 1)


def gate_phase(nc, const, r_all, x2_row, stats, top, tile_expert, biases, Wg, bg, b1, sorted_x):
    with ExitStack() as ctx:
        def sb(name, shape):
            return ctx.enter_context(nc.sbuf_tensor(name, shape, F32))

        def sem(name):
            return ctx.enter_context(nc.semaphore(name))

        def cst(name):
            return const[:, CONST_AT[name][0]:CONST_AT[name][1]]

        wg, bg_rep = sb("wg", [P, E]), sb("bg_rep", [P, E])
        norm = {n: sb("g_" + n, [P, B]) for n in ("mean", "var", "dev", "rstd", "tmp")}
        x2 = [sb(f"x2_{i}", [P, G, D]) for i in range(2)]
        x2T = [sb(f"x2T_{i}", [P, G, P]) for i in range(2)]
        logits, ex, hot = (sb(n, [P, B, E]) for n in ("logits", "ex", "hot"))
        total, inv, index = (sb(n, [P, B]) for n in ("total", "inv", "index"))
        b1_rows = sb("b1_rows", [E * FT, P])
        count, upto_batch = sb("count", [P, B, E]), [sb(f"upto_batch{i}", [P, B, E]) for i in range(2)]
        is_full, tiles, by_expert = sb("is_full", [P, E, B]), sb("tiles", [P, E]), sb("by_expert", [P, E, E])
        tile_end, tile_start = sb("tile_end", [P, E]), sb("tile_start", [P, E])
        after, expert_f = sb("after", [P, NT, E - 1]), sb("expert_f", [P, NT])
        row_of, place_f = sb("row_of", [P, B, E]), sb("place_f", [P, B])
        place = ctx.enter_context(nc.sbuf_tensor("place", [P, B], U32))
        b1_bank = ctx.enter_context(nc.psum_tensor("b1_bank", [P, BANK], F32))
        rank_bank = ctx.enter_context(nc.psum_tensor("rank_bank", [P, 2, B, E], F32))
        turn = [ctx.enter_context(nc.psum_tensor(f"g_turn{i}", [P, BANK], F32)) for i in range(2)]
        logit_bank = [ctx.enter_context(nc.psum_tensor(f"g_logit{i}", [P, BANK], F32)) for i in range(2)]

        w_loaded, dev_in, dev_out = sem("g_w_loaded"), sem("g_dev_in"), sem("g_dev_out")
        x2_ready, x2_turned, x2T_evac, x2_kept = sem("x2_ready"), sem("x2_turned"), sem("x2T_evac"), sem("x2_kept")
        gated, logit_ready = sem("gated"), sem("logit_ready")
        done, exp_done = sem("gate_done"), sem("gate_exp")
        b1_turned, b1_kept = sem("b1_turned"), sem("b1_kept")
        hot_ready, ranked, placed, scattered = sem("hot_ready"), sem("ranked"), sem("placed"), sem("scattered")
        block = ctx.enter_context(nc.Block())

        @block.sync
        def _(sp):
            sp.dma_start(wg[:, :], Wg).then_inc(w_loaded, 16)
            sp.dma_start(bg_rep[:, :], bg.rearrange("(o e) -> o e", o=1).to_broadcast([P, E])).then_inc(w_loaded, 16)
            sp.dma_start(b1_rows[:, :], b1.rearrange("e (f p) -> (e f) p", p=P)).then_inc(w_loaded, 16)

        @block.tensor
        def _(pe):
            pe.wait_ge(w_loaded, 48)
            pe.transpose(b1_bank[:, 0:E * FT], b1_rows[:, :], cst("ident")[0:E * FT, 0:E * FT]).then_inc(b1_turned, 1)

            def step(half, p, one, two):
                t = 2 * half + p
                u = t - 1
                q = 1 - p
                if one:
                    pe.wait_ge(x2_ready, t + 1)
                    if not is_step(t, 0, 1):
                        pe.wait_ge(x2T_evac, t - 1)
                    for i in range(G):
                        last = pe.transpose(turn[p][:, i * P:(i + 1) * P], x2[p][:, i, :], cst("ident"))
                    last.then_inc(x2_turned, 1)
                if two:
                    pe.wait_ge(x2T_evac, u + 1)
                    if not one:
                        pe.wait_ge(logit_ready, u - 1)
                    for i in range(G):
                        last = pe.matmul(logit_bank[q][:, i * E:(i + 1) * E], x2T[q][:, i, :], wg[:, :], start=True, stop=True)
                    last.then_inc(gated, 1)

            run_steps(pe, step, NG)
            pe.wait_ge(hot_ready, 1)
            flat = hot[:, :, :].rearrange("p b e -> p (b e)")
            pe.matmul(rank_bank[:, 0, :, :].rearrange("p b e -> p (b e)"), cst("below"), flat, start=True, stop=True)
            pe.matmul(rank_bank[:, 1, :, :].rearrange("p b e -> p (b e)"), cst("ones"), flat, start=True, stop=True).then_inc(ranked, 1)

        @block.scalar
        def _(act):
            norm_act(act, norm, dev_in, dev_out)

            def step(half, p, one, two):
                t = 2 * half + p
                if one:
                    act.wait_ge(x2_turned, t + 1)
                    if not is_step(t, 0, 1):
                        act.wait_ge(gated, t - 1)
                    act.activation(x2T[p][:, :, :], turn[p][:, :].rearrange("p (g t) -> p g t", g=G), ACT.Copy).then_inc(x2T_evac, 1)

            run_steps(act, step, NG)
            act.wait_ge(done, 2)
            act.activation(ex[:, :, :], logits[:, :, :], ACT.Exp).then_inc(exp_done, 1)

        @block.gpsimd
        def _(pool):
            def step(half, p, one, two):
                t = 2 * half + p
                if one:
                    pool.wait_ge(x2_ready, t + 1)
                    pool.tensor_copy(x2_row[:, bass.ds(G * t, G), 0:D], x2[p][:, :, :]).then_inc(x2_kept, 1)

            run_steps(pool, step, NG)
            pool.tensor_copy(x2_row[:, :, D:].rearrange("p b o -> p (b o)"), cst("token_row")).then_inc(x2_kept, 1)
            pool.wait_ge(x2_kept, NG + 1)
            pool.wait_ge(placed, 1)
            for b in range(B):
                pool.indirect_dma_start(sorted_x, bass.IndirectOffsetOnAxis(ap=place[:, b:b + 1], axis=0),
                                        x2_row[:, b, :], None).then_inc(scattered, 16)
            pool.wait_ge(scattered, 16 * B)

        @block.vector
        def _(dve):
            norm_dve(dve, stats, norm, dev_in, dev_out)
            dve.wait_ge(w_loaded, 48)
            dve.wait_ge(b1_turned, 1)
            dve.tensor_copy(biases[:, :, 0:FT], b1_bank[:, 0:E * FT].rearrange("p (e f) -> p e f", f=FT)).then_inc(b1_kept, 1)

            def add_bias(w, p):
                dve.wait_ge(gated, w + 1)
                dve.tensor_tensor(logits[:, bass.ds(G * w, G), :], logit_bank[p][:, 0:G * E].rearrange("p (g e) -> p g e", e=E),
                                  bg_rep[:, :].unsqueeze(1).to_broadcast([P, G, E]), ALU.add).then_inc(logit_ready, 1)

            def step(half, p, one, two):
                t = 2 * half + p
                if one:
                    if not is_step(t, 0, 1):
                        dve.wait_ge(x2_turned, t - 1)
                        dve.wait_ge(x2_kept, t - 1)
                    for i in range(G):
                        b = G * t + i
                        last = dve.tensor_scalar(x2[p][:, i, :], r_all[:, bass.ds(b, 1), :].rearrange("p o d -> p (o d)"),
                                                 norm["mean"][:, bass.ds(b, 1)], norm["rstd"][:, bass.ds(b, 1)], ALU.subtract, ALU.mult)
                    last.then_inc(x2_ready, 1)
                if not is_step(t, 0, 1):
                    add_bias(t - 2, p)

            run_steps(dve, step, NG)
            add_bias(NG - 1, (NG - 1) % 2)

            def bc(t):
                return t[:, :].unsqueeze(2).to_broadcast([P, B, E])
            iota = cst("iota").unsqueeze(1).to_broadcast([P, B, E])
            dve.wait_ge(logit_ready, NG)
            dve.tensor_reduce(top[:, :], logits[:, :, :], X, ALU.max).then_inc(done, 1)
            dve.wait_ge(done, 1)
            dve.tensor_tensor(logits[:, :, :], logits[:, :, :], bc(top), ALU.subtract).then_inc(done, 1)
            dve.wait_ge(exp_done, 1)
            dve.tensor_reduce(total[:, :], ex[:, :, :], X, ALU.add).then_inc(done, 1)
            dve.wait_ge(done, 3)
            dve.reciprocal(inv[:, :], total[:, :]).then_inc(done, 1)
            dve.wait_ge(done, 4)
            dve.tensor_tensor(ex[:, :, :], ex[:, :, :], bc(inv), ALU.mult).then_inc(done, 1)
            dve.wait_ge(done, 5)
            dve.tensor_reduce(top[:, :], ex[:, :, :], X, ALU.max).then_inc(done, 1)
            dve.wait_ge(done, 6)
            dve.tensor_tensor(hot[:, :, :], ex[:, :, :], bc(top), ALU.is_equal).then_inc(done, 1)
            dve.wait_ge(done, 7)
            dve.tensor_scalar(hot[:, :, :], hot[:, :, :], -float(E), float(E), ALU.mult, ALU.add).then_inc(done, 1)
            dve.wait_ge(done, 8)
            dve.tensor_tensor(hot[:, :, :], hot[:, :, :], iota, ALU.add).then_inc(done, 1)
            dve.wait_ge(done, 9)
            dve.tensor_reduce(index[:, :], hot[:, :, :], X, ALU.min).then_inc(done, 1)
            dve.wait_ge(done, 10)
            dve.tensor_tensor(hot[:, :, :], bc(index), iota, ALU.is_equal).then_inc(hot_ready, 1)

            dve.wait_ge(ranked, 1)
            dve.tensor_copy(count[:, :, :], rank_bank[:, 1, :, :])
            dve.tensor_copy(upto_batch[0][:, :, :], rank_bank[:, 1, :, :]).then_inc(done, 1)
            n, shift, cur = 11, 1, 0
            while shift < B:
                a, z = upto_batch[cur], upto_batch[1 - cur]
                dve.wait_ge(done, n)
                dve.tensor_copy(z[:, 0:shift, :], a[:, 0:shift, :])
                dve.tensor_tensor(z[:, shift:, :], a[:, shift:, :], a[:, 0:B - shift, :], ALU.add).then_inc(done, 1)
                n, shift, cur = n + 1, 2 * shift, 1 - cur
            upto, spare = upto_batch[cur], upto_batch[1 - cur]
            dve.wait_ge(done, n)
            dve.tensor_tensor(is_full[:, :, :], upto[:, B - 1, :].unsqueeze(2).to_broadcast([P, E, B]),
                              cst("full").unsqueeze(1).to_broadcast([P, E, B]), ALU.is_gt).then_inc(done, 1)
            dve.tensor_tensor(spare[:, :, :], upto[:, :, :], count[:, :, :], ALU.subtract).then_inc(done, 1)
            dve.wait_ge(done, n + 1)
            dve.tensor_reduce(tiles[:, :], is_full[:, :, :], X, ALU.add).then_inc(done, 1)
            dve.wait_ge(done, n + 2)
            dve.tensor_tensor(row_of[:, :, :], spare[:, :, :], rank_bank[:, 0, :, :], ALU.add).then_inc(done, 1)
            dve.wait_ge(done, n + 3)
            dve.tensor_tensor(by_expert[:, :, :], tiles[:, :].unsqueeze(1).to_broadcast([P, E, E]),
                              cst("upto").rearrange("p (e f) -> p e f", f=E), ALU.mult).then_inc(done, 1)
            dve.wait_ge(done, n + 5)
            dve.tensor_reduce(tile_end[:, :], by_expert[:, :, :], X, ALU.add).then_inc(done, 1)
            dve.wait_ge(done, n + 6)
            dve.tensor_tensor(tile_start[:, :], tile_end[:, :], tiles[:, :], ALU.subtract).then_inc(done, 1)
            dve.tensor_tensor(after[:, :, :], cst("tile_at").unsqueeze(2).to_broadcast([P, NT, E - 1]),
                              tile_end[:, 0:E - 1].unsqueeze(1).to_broadcast([P, NT, E - 1]), ALU.is_ge).then_inc(done, 1)
            dve.wait_ge(done, n + 7)
            dve.scalar_tensor_tensor(row_of[:, :, :], tile_start[:, :].unsqueeze(1).to_broadcast([P, B, E]), float(P),
                                     row_of[:, :, :], ALU.mult, ALU.add).then_inc(done, 1)
            dve.wait_ge(done, n + 8)
            dve.tensor_reduce(expert_f[:, :], after[:, :, :], X, ALU.add).then_inc(done, 1)
            dve.wait_ge(done, n + 9)
            dve.tensor_tensor(row_of[:, :, :], row_of[:, :, :], hot[:, :, :], ALU.mult).then_inc(done, 1)
            dve.wait_ge(done, n + 11)
            dve.tensor_reduce(place_f[:, :], row_of[:, :, :], X, ALU.add).then_inc(done, 1)
            dve.tensor_copy(tile_expert[:, :], expert_f[:, :])
            dve.wait_ge(done, n + 12)
            dve.tensor_copy(place[:, :], place_f[:, :]).then_inc(placed, 1)


def expert_phase(nc, const, w1, w2, biases, tile_expert, sorted_x, y_rows):
    with ExitStack() as ctx:
        def sb(name, shape):
            return ctx.enter_context(nc.sbuf_tensor(name, shape, F32))

        def sem(name):
            return ctx.enter_context(nc.semaphore(name))

        def two(name, shape):
            return [sb(f"{name}{i}", shape) for i in range(2)]

        def banks(name):
            return [ctx.enter_context(nc.psum_tensor(f"{name}{i}", [P, BANK], F32)) for i in range(2)]

        ident = const[:, CONST_AT["ident"][0]:CONST_AT["ident"][1]]
        xs = sb("xs", [P, NT + 1, D + 1])
        x_cur, xT, w1_cur, b_cur = two("e_x", [P, D]), two("e_xT", [P, P]), two("w1_cur", [P, HID]), two("b_cur", [P, FT + D])
        hT, y = two("hT", [P, FT, P]), two("y", [P, D])
        carrier = sb("carrier", [P, 1])
        row = [ctx.enter_context(nc.sbuf_tensor(f"row{i}", [P, 1], U32)) for i in range(2)]
        turn_bank, y_bank = banks("e_turn"), banks("y_bank")
        h_bank = [banks("h_bank_a"), banks("h_bank_b")]
        cuts = (0, 3, NT)
        x_loaded = [sem(f"xs_loaded{i}") for i in range(len(cuts) - 1)]
        pad_done, x_staged, turned, xT_evac = sem("pad_done"), sem("e_x_staged"), sem("e_turned"), sem("e_xT_evac")
        b_staged = sem("b_staged")
        w1_staged, hid, hid_done = sem("w1_staged"), sem("hid"), sem("hid_done")
        y_done, y_added, row_ready = sem("y_done"), sem("y_added"), sem("row_ready")
        stored = [sem(f"y_stored{i}") for i in range(2)]
        block = ctx.enter_context(nc.Block())

        def expert_of(eng, t):
            return eng.value_load(tile_expert[0:1, bass.ds(t, 1)], min_val=0, max_val=E - 1)

        @block.sync
        def _(sp):
            rows = sorted_x.rearrange("(t p) d -> p t d", p=P)
            for i, ready in enumerate(x_loaded):
                a, z = cuts[i], cuts[i + 1]
                sp.dma_start(xs[:, a:z, :], rows[:, a:z, :]).then_inc(ready, 16)

        @block.gpsimd
        def _(pool):
            pool.memset(xs[:, NT:NT + 1, :], 0.0).then_inc(pad_done, 1)

            pool.wait_ge(pad_done, 1)
            pool.wait_ge(x_loaded[0], 16)

            def step(half, p, one, two):
                t = 2 * half + p
                if two:
                    u, q = t - 1, 1 - p
                    if is_step(t, 3):
                        for ready in x_loaded[1:]:
                            pool.wait_ge(ready, 16)
                    if not is_step(t, 1, 2):
                        pool.wait_ge(stored[q], 16 * (half if p == 1 else half - 1))
                    pool.tensor_copy(row[q][:, :], xs[:, bass.ds(u, 1), D:].rearrange("p o d -> p (o d)")).then_inc(row_ready, 1)
                    pool.wait_ge(row_ready, u + 1)
                    pool.wait_ge(y_added, u + 1)
                    pool.tensor_tensor(carrier[:, :], xs[:, NT, 0:1], xs[:, NT, 1:2], ALU.add)
                    pool.indirect_dma_start(y_rows, bass.IndirectOffsetOnAxis(ap=row[q][:, :], axis=0),
                                            y[q][:, :], None).then_inc(stored[q], 16)

            run_steps(pool, step, NT, peeled=2)
            pool.wait_ge(stored[0], 16 * ((NT + 1) // 2))
            pool.wait_ge(stored[1], 16 * (NT // 2))

        @block.tensor
        def _(pe):
            def turn(t, p):
                pe.wait_ge(x_staged, t + 1)
                if not is_step(t, 0, 1):
                    pe.wait_ge(xT_evac, t - 1)
                pe.transpose(turn_bank[p][:, 0:P], x_cur[p][:, :], ident).then_inc(turned, 1)

            turn(0, 0)

            def step(half, p, one, two):
                t = 2 * half + p
                u, q = t - 1, 1 - p
                if two:
                    e = expert_of(pe, u)
                if one:
                    pe.wait_ge(w1_staged, t + 1)
                    pe.wait_ge(xT_evac, t + 1)
                    if not is_step(t, 0, 1):
                        pe.wait_ge(hid_done, FT * (t - 1))
                    for part in range(2):
                        for f in range(FT // 2 * part, FT // 2 * (part + 1)):
                            last = pe.matmul(h_bank[p][part][:, f * P:(f + 1) * P], w1_cur[p][:, f * P:(f + 1) * P], xT[p][:, :],
                                             start=True, stop=True)
                        last.then_inc(hid, 1)
                    turn(t + 1, 1 - p)
                if two:
                    pe.wait_ge(hid_done, FT * (u + 1))
                    if not one:
                        pe.wait_ge(y_added, u - 1)
                    for f in range(FT):
                        last = pe.matmul(y_bank[q][:, 0:D], hT[q][:, f, :],
                                         w2[:, bass.ds(e, 1), f, :].rearrange("p o d -> p (o d)"),
                                         start=(f == 0), stop=(f == FT - 1))
                    last.then_inc(y_done, 1)

            run_steps(pe, step, NT)

        @block.scalar
        def _(act):
            def stage_x(t, p):
                if not is_step(t, 0, 1):
                    act.wait_ge(turned, t - 1)
                    act.wait_ge(x_loaded[0], 16)
                act.activation(x_cur[p][:, :], xs[:, bass.ds(t, 1), 0:D].rearrange("p o d -> p (o d)"), ACT.Copy).then_inc(x_staged, 1)

            def stage_b(t, p):
                e = expert_of(act, t)
                if not is_step(t, 0, 1):
                    act.wait_ge(y_added, t - 1)
                    act.wait_ge(x_loaded[0], 16)
                act.activation(b_cur[p][:, :], biases[:, bass.ds(e, 1), :].rearrange("p o d -> p (o d)"), ACT.Copy).then_inc(b_staged, 1)

            stage_b(0, 0)
            act.wait_ge(x_loaded[0], 16)
            stage_x(0, 0)
            stage_x(1, 1)

            def step(half, p, one, two):
                t = 2 * half + p
                if one:
                    for f in range(FT):
                        part = f // (FT // 2)
                        if f % (FT // 2) == 0:
                            act.wait_ge(hid, 2 * t + part + 1)
                        if f == 0:
                            act.wait_ge(b_staged, t + 1)
                            if not is_step(t, 0, 1):
                                act.wait_ge(y_done, t - 1)
                        act.activation(hT[p][:, f, :], h_bank[p][part][:, f * P:(f + 1) * P], ACT.Silu,
                                       bias=b_cur[p][:, f:f + 1]).then_inc(hid_done, 1)
                    if is_step(t, 1):
                        act.wait_ge(pad_done, 1)
                        for ready in x_loaded[1:]:
                            act.wait_ge(ready, 16)
                    if not is_step(t, NT - 1):
                        stage_x(t + 2, p)
                        stage_b(t + 1, 1 - p)

            run_steps(act, step, NT)

        @block.vector
        def _(dve):
            def stage_w1(t, p):
                e = expert_of(dve, t)
                if not is_step(t, 0, 1):
                    dve.wait_ge(hid, 2 * (t - 1))
                dve.tensor_copy(w1_cur[p][:, :], w1[:, bass.ds(e, 1), :].rearrange("p o d -> p (o d)")).then_inc(w1_staged, 1)

            def evac(t, p):
                dve.wait_ge(turned, t + 1)
                dve.tensor_copy(xT[p][:, :], turn_bank[p][:, 0:P]).then_inc(xT_evac, 1)

            stage_w1(0, 0)
            evac(0, 0)

            def step(half, p, one, two):
                t = 2 * half + p
                u, q = t - 1, 1 - p
                if one:
                    if is_step(t, NT - 1):
                        dve.wait_ge(hid, 2 * t)
                    else:
                        stage_w1(t + 1, 1 - p)
                    evac(t + 1, 1 - p)
                if two:
                    dve.wait_ge(y_done, u + 1)
                    if not is_step(t, 1, 2):
                        dve.wait_ge(stored[q], 16 * (half if p == 1 else half - 1))
                    dve.tensor_tensor(y[q][:, :], y_bank[q][:, 0:D], b_cur[q][:, FT:],
                                      ALU.add).then_inc(y_added, 1)

            run_steps(dve, step, NT, peeled=2)


def finish_phase(nc, r_all, x2_row, stats, top, y_rows, out):
    with ExitStack() as ctx:
        def sb(name, shape):
            return ctx.enter_context(nc.sbuf_tensor(name, shape, F32))

        def sem(name):
            return ctx.enter_context(nc.semaphore(name))

        y_tok = sb("y_tok", [P, B, D])
        norm = {n: sb("o_" + n, [P, B]) for n in ("mean", "var", "dev", "rstd", "tmp")}
        o = sb("o", [P, B, D])
        y_loaded = [sem(f"y_loaded{g}") for g in range(NG)]
        added, added_pool, stats_done, scaled = sem("f_added"), sem("f_added_pool"), sem("f_stats"), sem("f_scaled")
        dev_in, dev_out, stored = sem("f_dev_in"), sem("f_dev_out"), sem("o_stored")
        o_ready, o_ready_pool = sem("o_ready"), sem("o_ready_pool")
        pool_adds = tuple(range(2, NG, 3))
        pool_norms = (NG // 2,)
        block = ctx.enter_context(nc.Block())

        def normalise(eng, g, done):
            for b in range(G * g, G * g + G):
                last = eng.tensor_scalar(o[:, b, :], r_all[:, b, :], norm["mean"][:, b:b + 1], norm["rstd"][:, b:b + 1],
                                         ALU.subtract, ALU.mult)
            last.then_inc(done, 1)

        @block.sync
        def _(sp):
            for g in range(NG):
                b = G * g
                sp.dma_start(y_tok[:, b:b + G, :], y_rows[b * P:(b + G) * P, :].rearrange("(b p) d -> p b d", p=P)).then_inc(y_loaded[g], 16)
            ready = {o_ready: 0, o_ready_pool: 0}
            for g in range(NG):
                by = o_ready_pool if g in pool_norms else o_ready
                ready[by] += 1
                sp.wait_ge(by, ready[by])
                sp.dma_start(out[G * g:G * g + G].rearrange("b p d -> p b d"), o[:, G * g:G * g + G, :]).then_inc(stored, 16)
            sp.wait_ge(stored, 16 * NG)

        @block.scalar
        def _(act):
            norm_act(act, norm, dev_in, dev_out)

        @block.gpsimd
        def _(pool):
            for n, g in enumerate(pool_adds):
                s = slice(G * g, G * g + G)
                pool.wait_ge(y_loaded[g], 16)
                pool.tensor_tensor(y_tok[:, s, :], y_tok[:, s, :], top[:, s].unsqueeze(2).to_broadcast([P, G, D]), ALU.mult).then_inc(scaled, 1)
                pool.wait_ge(scaled, n + 1)
                pool.tensor_tensor(r_all[:, s, :], y_tok[:, s, :], x2_row[:, s, 0:D], ALU.add).then_inc(added_pool, 1)
            pool.wait_ge(dev_in, 8)
            for g in pool_norms:
                normalise(pool, g, o_ready_pool)

        @block.vector
        def _(dve):
            own = others = 0
            for g in range(NG):
                if g in pool_adds:
                    others += 1
                    dve.wait_ge(added_pool, others)
                else:
                    dve.wait_ge(y_loaded[g], 16)
                    for b in range(G * g, G * g + G):
                        last = dve.scalar_tensor_tensor(r_all[:, b, :], y_tok[:, b, :], top[:, b:b + 1], x2_row[:, b, 0:D],
                                                        ALU.mult, ALU.add)
                    last.then_inc(added, 1)
                    own += 1
                    dve.wait_ge(added, own)
                for b in range(G * g, G * g + G):
                    last = dve.bn_stats(stats[:, b, :], r_all[:, b, :])
                last.then_inc(stats_done, 1)
            dve.wait_ge(stats_done, NG)
            norm_dve(dve, stats, norm, dev_in, dev_out)
            for g in range(NG):
                if g not in pool_norms:
                    normalise(dve, g, o_ready)


def build(nc, x, context, Wq, Wk, Wv, Wo, betas, xWq, xWk, xWv, Wg, bg, W1, b1, W2, b2, consts, out):
    with ExitStack() as ctx:
        const = ctx.enter_context(nc.sbuf_tensor("const", [P, NCONST], F32))
        r_all = ctx.enter_context(nc.sbuf_tensor("r_all", [P, B, D], F32))
        stats = ctx.enter_context(nc.sbuf_tensor("stats", [P, B, 6], F32))
        scratch_qv = nc.dram_tensor("scratch_qv", (B, P, C, 2 * DK), F32, kind="Internal").ap()
        scratch_z = nc.dram_tensor("scratch_z", (B, H, 2, DK), F32, kind="Internal").ap()
        sorted_x = nc.dram_tensor("sorted_x", (NT * P, D + 1), F32, kind="Internal").ap()
        y_rows = nc.dram_tensor("y_rows", ((B + NT) * P, D), F32, kind="Internal").ap()
        attention_phase(nc, consts, const, r_all, stats, x, Wq, Wk, Wv, Wo, betas, scratch_qv, scratch_z)
        w1 = ctx.enter_context(nc.sbuf_tensor("w1", [P, E, HID], F32))
        w2 = ctx.enter_context(nc.sbuf_tensor("w2", [P, E, FT, D], F32))
        biases = ctx.enter_context(nc.sbuf_tensor("biases", [P, E, FT + D], F32))
        top = ctx.enter_context(nc.sbuf_tensor("top", [P, B], F32))
        tile_expert = ctx.enter_context(nc.sbuf_tensor("tile_expert", [P, NT], U32))
        preload = ((w1[:, :, :], W1.rearrange("e d h -> d e h")),
                   (w2[:, :, :, :], W2.rearrange("e (f p) d -> p e f d", p=P)),
                   (biases[:, :, FT:], b2.rearrange("(o e) d -> o e d", o=1).to_broadcast([P, E, D])))
        retention_phase(nc, const, r_all, stats, context, xWq, xWk, xWv, preload, sorted_x)
        x2_row = ctx.enter_context(nc.sbuf_tensor("x2_row", [P, B, D + 1], F32))
        gate_phase(nc, const, r_all, x2_row, stats, top, tile_expert, biases, Wg, bg, b1, sorted_x)
        expert_phase(nc, const, w1, w2, biases, tile_expert, sorted_x, y_rows)
        finish_phase(nc, r_all, x2_row, stats, top, y_rows, out)


_NAMES = ["x", "ctx_1024", "L0_attn_Wq", "L0_attn_Wk", "L0_attn_Wv", "L0_attn_Wo", "L0_attn_betas",
          "L0_xattn_Wq", "L0_xattn_Wk", "L0_xattn_Wv", "L0_ffn_Wg", "L0_ffn_bg", "L0_ffn_W1", "L0_ffn_b1",
          "L0_ffn_W2", "L0_ffn_b2"]


def kernel(**inputs):
    import numpy as _np
    import concourse.bacc as _bacc
    from concourse import mybir as _mybir
    from concourse.bass_utils import run_bass_kernel_spmd as _run

    nc = _bacc.Bacc("TRN2", target_bir_lowering=False, num_devices=1)
    arrays, args = {}, []
    for name in _NAMES:
        a = _np.ascontiguousarray(inputs[name])
        arrays[f"in_{name}_dram"] = a
        args.append(nc.dram_tensor(f"in_{name}_dram", a.shape, _mybir.dt.from_np(a.dtype), kind="ExternalInput").ap())
    a = shape_constants()
    arrays["in_consts_dram"] = a
    args.append(nc.dram_tensor("in_consts_dram", a.shape, _mybir.dt.from_np(a.dtype), kind="ExternalInput").ap())
    args.append(nc.dram_tensor("out_0_dram", (B, P, D), F32, kind="ExternalOutput").ap())
    build(nc, *args)
    r = _run(nc, [arrays], core_ids=[0])
    return r.results[0]["out_0_dram"]
```
